# Optimizing a Trainium2 kernel written in Bass

```python
import numpy as np
import jax
import jax.numpy as jnp

def _softmax(x, axis=-1):
    return jax.nn.softmax(x, axis=axis)

def _gelu(x):
    return jax.nn.gelu(x, approximate=True)

def _silu(x):
    return jax.nn.silu(x)

def _sigmoid(x):
    return jax.nn.sigmoid(x)

def _layernorm(x, axis=-1, eps=1e-05):
    m = jnp.mean(x, axis=axis, keepdims=True)
    v = jnp.var(x, axis=axis, keepdims=True)
    return (x - m) / jnp.sqrt(v + eps)

def _scatter_add(tgt, idx, src, axis=0):
    return tgt.at[idx].add(src)

def _segment_sum(src, seg, n):
    return jax.ops.segment_sum(src, seg, n)
kernel_name = 'mk_xattn_ffn_d1_seqx_r8_2d0b1d'

def setup_inputs(seed: int=0):
    np.random.seed(seed)
    _w = jnp.asarray

    def _rec_inputs():
        import jax
        import jax.numpy as jnp
        _rk = jax.random.key(seed)
        x = -0.0001661 + 0.9999 * jax.random.normal(jax.random.fold_in(_rk, 1), (64, 64, 256), jnp.float32)
        _lenS = 64 - jax.random.randint(jax.random.fold_in(_rk, 7), (64,), 0, max(1, 64 // 4) + 1, jnp.int32)
        _lenS2 = 64 - jax.random.randint(jax.random.fold_in(_rk, 8), (64,), 0, max(1, 64 // 4) + 1, jnp.int32)
        _ctx_2048P = jax.random.normal(jax.random.fold_in(_rk, 11), (64, 16, 256), jnp.float32)
        _ctx_2048c = jax.random.dirichlet(jax.random.fold_in(_rk, 511), 0.3 * jnp.ones((16,), jnp.float32), (64, 64))
        _ctx_2048t = jnp.einsum('bsk,bkd->bsd', _ctx_2048c, _ctx_2048P)
        _ctx_2048t = _ctx_2048t * jax.lax.rsqrt(jnp.mean(jnp.square(_ctx_2048t)) + 1e-12) * 0.953939
        ctx_2048 = -0.00016346 + 1.00032 * (_ctx_2048t + 0.3 * jax.random.normal(jax.random.fold_in(_rk, 611), (64, 64, 256), jnp.float32))
        return (x, ctx_2048, _lenS2)
    x, ctx_2048, _lenS2 = _rec_inputs()

    def _L0_xattn_setup():
        import jax, jax.numpy as jnp
        import numpy as np
        DIM = 256
        HEADS = 16
        HEAD_DIM = DIM // HEADS
        EPS = 1e-06
        IMG_TOKENS = 257
        B, L1, L2 = (2, 512, 769)
        SCALE = 1.0 / np.sqrt(HEAD_DIM).astype(np.float32)

        def rms_norm(x, g):
            return x * jax.lax.rsqrt(jnp.mean(x * x, axis=-1, keepdims=True) + EPS) * g

        def attention(q, k, v, kv_mask=None):
            s = jnp.einsum('bqhd,bkhd->bhqk', q, k) * SCALE
            if kv_mask is not None:
                s = jnp.where(kv_mask[:, None, None, :], s, jnp.float32(-1000000000.0))
            p = jax.nn.softmax(s, axis=-1)
            return jnp.einsum('bhqk,bkhd->bqhd', p, v)
        key = jax.random.key(seed)
        ks = jax.random.split(key, 20)
        std = 0.02

        def lin(i):
            return (jax.random.normal(ks[i], (DIM, DIM), jnp.float32) * std, jnp.zeros((DIM,), jnp.float32))
        w_q, b_q = lin(0)
        w_k, b_k = lin(1)
        w_v, b_v = lin(2)
        w_k_img, b_k_img = lin(3)
        w_v_img, b_v_img = lin(4)
        w_o, b_o = lin(5)
        return {'x': jax.random.normal(ks[6], (B, L1, DIM), jnp.float32), 'context': jax.random.normal(ks[7], (B, L2, DIM), jnp.float32), 'context_lens': jax.random.randint(ks[8], (B,), 32, 513, jnp.int64 if jax.config.jax_enable_x64 else jnp.int32), 'w_q': w_q, 'b_q': b_q, 'w_k': w_k, 'b_k': b_k, 'w_v': w_v, 'b_v': b_v, 'w_k_img': w_k_img, 'b_k_img': b_k_img, 'w_v_img': w_v_img, 'b_v_img': b_v_img, 'w_o': w_o, 'b_o': b_o, 'g_q': jnp.ones((DIM,), jnp.float32), 'g_k': jnp.ones((DIM,), jnp.float32), 'g_k_img': jnp.ones((DIM,), jnp.float32)}
    _L0_xattn_all = _L0_xattn_setup()
    _L0_xattn_in = {k: v for k, v in _L0_xattn_all.items() if k in ('w_q', 'b_q', 'w_k', 'b_k', 'w_v', 'b_v', 'w_k_img', 'b_k_img', 'w_v_img', 'b_v_img', 'w_o', 'b_o', 'g_q', 'g_k', 'g_k_img')}
    del _L0_xattn_all

    def _L0_ffn_setup():
        import jax, jax.numpy as jnp
        import numpy as np
        H = 256
        I = 176
        E = 32
        K = 4
        NS = 2
        RG = RU = RD = 128
        SI = I * NS
        B, S = (2, 256)

        def _init(key, shape, fan_in):
            return jax.random.normal(key, shape, jnp.float32) / np.sqrt(fan_in)

        def _moe_forward(x, gate_w, Rg, Ru, Rd, Ug, Cg, Uu, Cu, Ud, Cd, s_Rg, s_Ug, s_Cg, s_Ru, s_Uu, s_Cu, s_Rd, s_Ud, s_Cd):
            Bv, Sv, Hv = x.shape
            xf = x.reshape(-1, Hv)
            T = xf.shape[0]
            logits = xf @ gate_w.T
            scores = jax.nn.softmax(logits, axis=-1)
            tw, ti = jax.lax.top_k(scores, K)
            tw = tw / (tw.sum(-1, keepdims=True) + 1e-20)
            we = jnp.zeros((T, E), xf.dtype).at[jnp.arange(T)[:, None], ti].add(tw)
            rg = xf @ Rg.T
            ru = xf @ Ru.T

            def expert_fn(Ug_e, Cg_e, Uu_e, Cu_e, Ud_e, Cd_e, w_e, rg, ru):
                g = jax.nn.silu(rg @ Ug_e.T @ Cg_e.T)
                u = ru @ Uu_e.T @ Cu_e.T
                rd = g * u @ Rd.T
                return w_e[:, None] * (rd @ Ud_e.T @ Cd_e.T)
            expert_fn = jax.checkpoint(expert_fn)

            def body(acc, ws):
                Ug_e, Cg_e, Uu_e, Cu_e, Ud_e, Cd_e, w_e = ws
                return (acc + expert_fn(Ug_e, Cg_e, Uu_e, Cu_e, Ud_e, Cd_e, w_e, rg, ru), None)
            y, _ = jax.lax.scan(body, jnp.zeros_like(xf), (Ug, Cg, Uu, Cu, Ud, Cd, we.T))
            g = jax.nn.silu(xf @ s_Rg.T @ s_Ug.T @ s_Cg.T)
            u = xf @ s_Ru.T @ s_Uu.T @ s_Cu.T
            sh = g * u @ s_Rd.T @ s_Ud.T @ s_Cd.T
            return (y + sh).reshape(Bv, Sv, Hv)
        ks = jax.random.split(jax.random.key(seed), 20)
        return {'x': jax.random.normal(ks[0], (B, S, H), jnp.float32), 'gate_w': _init(ks[1], (E, H), H), 'Rg': _init(ks[2], (RG, H), H), 'Ru': _init(ks[3], (RU, H), H), 'Rd': _init(ks[4], (RD, I), I), 'Ug': _init(ks[5], (E, RG, RG), RG), 'Cg': _init(ks[6], (E, I, RG), RG), 'Uu': _init(ks[7], (E, RU, RU), RU), 'Cu': _init(ks[8], (E, I, RU), RU), 'Ud': _init(ks[9], (E, RD, RD), RD), 'Cd': _init(ks[10], (E, H, RD), RD), 's_Rg': _init(ks[11], (RG, H), H), 's_Ug': _init(ks[12], (RG, RG), RG), 's_Cg': _init(ks[13], (SI, RG), RG), 's_Ru': _init(ks[14], (RU, H), H), 's_Uu': _init(ks[15], (RU, RU), RU), 's_Cu': _init(ks[16], (SI, RU), RU), 's_Rd': _init(ks[17], (RD, SI), SI), 's_Ud': _init(ks[18], (RD, RD), RD), 's_Cd': _init(ks[19], (H, RD), RD)}
    _L0_ffn_all = _L0_ffn_setup()
    _L0_ffn_in = {k: v for k, v in _L0_ffn_all.items() if k in ('gate_w', 'Rg', 'Ru', 'Rd', 'Ug', 'Cg', 'Uu', 'Cu', 'Ud', 'Cd', 's_Rg', 's_Ug', 's_Cg', 's_Ru', 's_Uu', 's_Cu', 's_Rd', 's_Ud', 's_Cd')}
    del _L0_ffn_all
    return {'x': x, 'ctx_2048': ctx_2048, '_lenS2': _lenS2, 'L0_xattn_w_q': _L0_xattn_in['w_q'], 'L0_xattn_b_q': _L0_xattn_in['b_q'], 'L0_xattn_w_k': _L0_xattn_in['w_k'], 'L0_xattn_b_k': _L0_xattn_in['b_k'], 'L0_xattn_w_v': _L0_xattn_in['w_v'], 'L0_xattn_b_v': _L0_xattn_in['b_v'], 'L0_xattn_w_k_img': _L0_xattn_in['w_k_img'], 'L0_xattn_b_k_img': _L0_xattn_in['b_k_img'], 'L0_xattn_w_v_img': _L0_xattn_in['w_v_img'], 'L0_xattn_b_v_img': _L0_xattn_in['b_v_img'], 'L0_xattn_w_o': _L0_xattn_in['w_o'], 'L0_xattn_b_o': _L0_xattn_in['b_o'], 'L0_xattn_g_q': _L0_xattn_in['g_q'], 'L0_xattn_g_k': _L0_xattn_in['g_k'], 'L0_xattn_g_k_img': _L0_xattn_in['g_k_img'], 'L0_ffn_gate_w': _L0_ffn_in['gate_w'], 'L0_ffn_Rg': _L0_ffn_in['Rg'], 'L0_ffn_Ru': _L0_ffn_in['Ru'], 'L0_ffn_Rd': _L0_ffn_in['Rd'], 'L0_ffn_Ug': _L0_ffn_in['Ug'], 'L0_ffn_Cg': _L0_ffn_in['Cg'], 'L0_ffn_Uu': _L0_ffn_in['Uu'], 'L0_ffn_Cu': _L0_ffn_in['Cu'], 'L0_ffn_Ud': _L0_ffn_in['Ud'], 'L0_ffn_Cd': _L0_ffn_in['Cd'], 'L0_ffn_s_Rg': _L0_ffn_in['s_Rg'], 'L0_ffn_s_Ug': _L0_ffn_in['s_Ug'], 'L0_ffn_s_Cg': _L0_ffn_in['s_Cg'], 'L0_ffn_s_Ru': _L0_ffn_in['s_Ru'], 'L0_ffn_s_Uu': _L0_ffn_in['s_Uu'], 'L0_ffn_s_Cu': _L0_ffn_in['s_Cu'], 'L0_ffn_s_Rd': _L0_ffn_in['s_Rd'], 'L0_ffn_s_Ud': _L0_ffn_in['s_Ud'], 'L0_ffn_s_Cd': _L0_ffn_in['s_Cd']}

def reference(x, ctx_2048, _lenS2, L0_xattn_w_q, L0_xattn_b_q, L0_xattn_w_k, L0_xattn_b_k, L0_xattn_w_v, L0_xattn_b_v, L0_xattn_w_k_img, L0_xattn_b_k_img, L0_xattn_w_v_img, L0_xattn_b_v_img, L0_xattn_w_o, L0_xattn_b_o, L0_xattn_g_q, L0_xattn_g_k, L0_xattn_g_k_img, L0_ffn_gate_w, L0_ffn_Rg, L0_ffn_Ru, L0_ffn_Rd, L0_ffn_Ug, L0_ffn_Cg, L0_ffn_Uu, L0_ffn_Cu, L0_ffn_Ud, L0_ffn_Cd, L0_ffn_s_Rg, L0_ffn_s_Ug, L0_ffn_s_Cg, L0_ffn_s_Ru, L0_ffn_s_Uu, L0_ffn_s_Cu, L0_ffn_s_Rd, L0_ffn_s_Ud, L0_ffn_s_Cd):
    import jax
    import jax.numpy as jnp

    def _L0_xattn_ref(x, context, context_lens, w_q, b_q, w_k, b_k, w_v, b_v, w_k_img, b_k_img, w_v_img, b_v_img, w_o, b_o, g_q, g_k, g_k_img):
        import jax, jax.numpy as jnp
        import numpy as np
        DIM = 256
        HEADS = 16
        HEAD_DIM = DIM // HEADS
        EPS = 1e-06
        IMG_TOKENS = 257
        B, L1, L2 = (2, 512, 769)
        SCALE = 1.0 / np.sqrt(HEAD_DIM).astype(np.float32)

        def rms_norm(x, g):
            return x * jax.lax.rsqrt(jnp.mean(x * x, axis=-1, keepdims=True) + EPS) * g

        def attention(q, k, v, kv_mask=None):
            s = jnp.einsum('bqhd,bkhd->bhqk', q, k) * SCALE
            if kv_mask is not None:
                s = jnp.where(kv_mask[:, None, None, :], s, jnp.float32(-1000000000.0))
            p = jax.nn.softmax(s, axis=-1)
            return jnp.einsum('bhqk,bkhd->bqhd', p, v)
        b = x.shape[0]
        ctx_img = context[:, :IMG_TOKENS]
        ctx_txt = context[:, IMG_TOKENS:]
        q = rms_norm(x @ w_q.T + b_q, g_q).reshape(b, -1, HEADS, HEAD_DIM)
        k = rms_norm(ctx_txt @ w_k.T + b_k, g_k).reshape(b, -1, HEADS, HEAD_DIM)
        v = (ctx_txt @ w_v.T + b_v).reshape(b, -1, HEADS, HEAD_DIM)
        k_img = rms_norm(ctx_img @ w_k_img.T + b_k_img, g_k_img).reshape(b, -1, HEADS, HEAD_DIM)
        v_img = (ctx_img @ w_v_img.T + b_v_img).reshape(b, -1, HEADS, HEAD_DIM)
        txt_len = ctx_txt.shape[1]
        kv_mask = jnp.arange(txt_len)[None, :] < context_lens[:, None]
        img_x = attention(q, k_img, v_img)
        txt_x = attention(q, k, v, kv_mask)
        out = (txt_x + img_x).reshape(b, -1, DIM)
        return out @ w_o.T + b_o

    def _L0_ffn_ref(x, gate_w, Rg, Ru, Rd, Ug, Cg, Uu, Cu, Ud, Cd, s_Rg, s_Ug, s_Cg, s_Ru, s_Uu, s_Cu, s_Rd, s_Ud, s_Cd):
        import jax, jax.numpy as jnp
        import numpy as np
        H = 256
        I = 176
        E = 32
        K = 4
        NS = 2
        RG = RU = RD = 128
        SI = I * NS
        B, S = (2, 256)

        def _init(key, shape, fan_in):
            return jax.random.normal(key, shape, jnp.float32) / np.sqrt(fan_in)

        def _moe_forward(x, gate_w, Rg, Ru, Rd, Ug, Cg, Uu, Cu, Ud, Cd, s_Rg, s_Ug, s_Cg, s_Ru, s_Uu, s_Cu, s_Rd, s_Ud, s_Cd):
            Bv, Sv, Hv = x.shape
            xf = x.reshape(-1, Hv)
            T = xf.shape[0]
            logits = xf @ gate_w.T
            scores = jax.nn.softmax(logits, axis=-1)
            tw, ti = jax.lax.top_k(scores, K)
            tw = tw / (tw.sum(-1, keepdims=True) + 1e-20)
            we = jnp.zeros((T, E), xf.dtype).at[jnp.arange(T)[:, None], ti].add(tw)
            rg = xf @ Rg.T
            ru = xf @ Ru.T

            def expert_fn(Ug_e, Cg_e, Uu_e, Cu_e, Ud_e, Cd_e, w_e, rg, ru):
                g = jax.nn.silu(rg @ Ug_e.T @ Cg_e.T)
                u = ru @ Uu_e.T @ Cu_e.T
                rd = g * u @ Rd.T
                return w_e[:, None] * (rd @ Ud_e.T @ Cd_e.T)
            expert_fn = jax.checkpoint(expert_fn)

            def body(acc, ws):
                Ug_e, Cg_e, Uu_e, Cu_e, Ud_e, Cd_e, w_e = ws
                return (acc + expert_fn(Ug_e, Cg_e, Uu_e, Cu_e, Ud_e, Cd_e, w_e, rg, ru), None)
            y, _ = jax.lax.scan(body, jnp.zeros_like(xf), (Ug, Cg, Uu, Cu, Ud, Cd, we.T))
            g = jax.nn.silu(xf @ s_Rg.T @ s_Ug.T @ s_Cg.T)
            u = xf @ s_Ru.T @ s_Uu.T @ s_Cu.T
            sh = g * u @ s_Rd.T @ s_Ud.T @ s_Cd.T
            return (y + sh).reshape(Bv, Sv, Hv)
        return _moe_forward(x, gate_w, Rg, Ru, Rd, Ug, Cg, Uu, Cu, Ud, Cd, s_Rg, s_Ug, s_Cg, s_Ru, s_Uu, s_Cu, s_Rd, s_Ud, s_Cd)
    x = x + _L0_xattn_ref(_layernorm(x, axis=-1), ctx_2048, _lenS2, L0_xattn_w_q, L0_xattn_b_q, L0_xattn_w_k, L0_xattn_b_k, L0_xattn_w_v, L0_xattn_b_v, L0_xattn_w_k_img, L0_xattn_b_k_img, L0_xattn_w_v_img, L0_xattn_b_v_img, L0_xattn_w_o, L0_xattn_b_o, L0_xattn_g_q, L0_xattn_g_k, L0_xattn_g_k_img)
    x = x + _L0_ffn_ref(_layernorm(x, axis=-1), L0_ffn_gate_w, L0_ffn_Rg, L0_ffn_Ru, L0_ffn_Rd, L0_ffn_Ug, L0_ffn_Cg, L0_ffn_Uu, L0_ffn_Cu, L0_ffn_Ud, L0_ffn_Cd, L0_ffn_s_Rg, L0_ffn_s_Ug, L0_ffn_s_Cg, L0_ffn_s_Ru, L0_ffn_s_Uu, L0_ffn_s_Cu, L0_ffn_s_Rd, L0_ffn_s_Ud, L0_ffn_s_Cd)
    return x

_drawn_inputs = setup_inputs


def setup_inputs(seed=0):
    import zlib

    import numpy as np

    out = dict(_drawn_inputs(seed))
    spreads = {'L0_xattn_b_q': (0.0, 0.38),
     'L0_xattn_b_k': (0.0, 0.1),
     'L0_xattn_b_v': (0.0, 0.1),
     'L0_xattn_b_k_img': (0.0, 0.724),
     'L0_xattn_b_v_img': (0.0, 0.1),
     'L0_xattn_b_o': (0.0, 0.1),
     'L0_xattn_g_q': (1.0, 0.6),
     'L0_xattn_g_k': (1.0, 0.2),
     'L0_xattn_g_k_img': (1.0, 0.6)}
    factors = {}
    for name, (base, spread) in spreads.items():
        noise = np.random.default_rng([zlib.crc32(name.encode()), seed]).standard_normal(out[name].shape)
        drawn = base * np.exp(spread * noise) if base else spread * noise
        out[name] = jnp.asarray(drawn.astype(out[name].dtype))
    for name, factor in factors.items():
        out[name] = (out[name] * factor).astype(out[name].dtype)
    return out
```

```python
from contextlib import ExitStack

import numpy as np

import concourse.bass as bass
from concourse import mybir

F32 = mybir.dt.float32
I32 = mybir.dt.int32
U32 = mybir.dt.uint32
ALU = mybir.AluOpType
ACT = mybir.ActivationFunctionType
AX = mybir.AxisListType

P = 128
BATCH, SEQ, DIM = 64, 64, 256
TOKENS = BATCH * SEQ
TILES = TOKENS // P
CH = DIM // P
HEADS, HD = 16, 16
PAIRS = HEADS // 2
GROUPS, GH = 2, 4
EXPERTS, TOPK = 32, 4
RANK = 128
INNER = 176
HALF = INNER // 2
SHARED = 2 * INNER
SCH = 3
SLAST = SHARED - 2 * P
SPAD = SCH * P
CAP = TOKENS + P
ETILES = (TOKENS * TOPK + EXPERTS * (P - 1)) // P + 1
DUMP = EXPERTS * CAP
LN_EPS, RMS_EPS = 1e-5, 1e-6
RAW = 2 * (RANK + INNER) + RANK + DIM


def live(i, n):
    return not isinstance(i, int) or 0 <= i < n


def past(i, k):
    return not isinstance(i, int) or i >= k


def landed(i, ring, slot, per=16):
    return (i - slot) * (per // ring) + per


def pipeline(eng, lead, stop, total, unroll, body):
    for s in range(lead):
        body(s, s)
    with eng.Fori(0, (stop - lead) // unroll) as g:
        for u in range(unroll):
            body(g * unroll + (lead + u), lead + u)
    for s in range(stop, total):
        body(s, s)


def at(ap, i):
    return ap[i] if isinstance(i, int) else ap[bass.ds(i, 1), :, :].rearrange("t p m -> (t p) m")


def col(tile, i):
    return tile[:, i, :] if isinstance(i, int) else tile[:, bass.ds(i, 1), :].rearrange("p t m -> p (t m)")


def build(nc, a):
    ctx = ExitStack()
    with ctx:
        def sb(name, shape, dt=F32):
            return ctx.enter_context(nc.sbuf_tensor(name, shape, dt))

        def ps(name, shape):
            return ctx.enter_context(nc.psum_tensor(name, shape, F32))

        def sem(name):
            return ctx.enter_context(nc.semaphore(name))

        def sems(name, n=2):
            return [sem(f"{name}{k}") for k in range(n)]

        x1_d = nc.dram_tensor("x1_d", [TILES, P, DIM], F32, kind="Internal").ap()
        xn2t_d = nc.dram_tensor("xn2t_d", [TILES, P, DIM], F32, kind="Internal").ap()
        xs_d = nc.dram_tensor("xs_d", [DUMP + P, DIM], F32, kind="Internal").ap()
        ys_d = nc.dram_tensor("ys_d", [ETILES * P, DIM], F32, kind="Internal").ap()

        ident = sb("ident", [P, P])
        tri = sb("tri", [P, P])
        ones = sb("ones", [P, P])
        headmask = sb("headmask", [P, GH])
        eiota = sb("eiota", [P, EXPERTS])
        ebase = sb("ebase", [P, EXPERTS])
        mhalf = sb("mhalf", [P, 2])
        wq = sb("wq", [P, CH, DIM])
        wkv = sb("wkv", [P, CH, 2 * DIM])
        wo = sb("wo", [P, CH, DIM])
        bq = sb("bq", [P, DIM])
        bk = sb("bk", [P, DIM])
        bo = sb("bo", [P, DIM])
        bv = sb("bv", [P, CH])
        gq = sb("gq", [P, CH])
        gk = sb("gk", [P, CH])
        gqk = sb("gqk", [P, CH])
        gate = sb("gate", [P, CH, EXPERTS])
        rgu_w = sb("rgu_w", [P, CH, 2 * RANK])
        rd_w = sb("rd_w", [HALF, 2, RANK])
        srgu_w = sb("srgu_w", [P, CH, 2, RANK])
        srd_w = sb("srd_w", [P, SCH, RANK])
        up_w = sb("up_w", [P, EXPERTS, 2 * INNER])
        down_w = sb("down_w", [P, EXPERTS, DIM])
        sup_w = sb("sup_w", [P, 2, SPAD])
        sdown_w = sb("sdown_w", [P, DIM])
        slots = sb("slots", [P, TILES, TOPK])
        experts = sb("experts", [P, TILES, TOPK])
        weights = sb("weights", [P, TILES, TOPK])

        bank03 = ps("bank03", [P, 4, 512])
        bank4, bank5, bank6, bank7 = (ps(f"bank{k}", [P, 512]) for k in range(4, 8))

        ld_const = sem("ld_const")
        consts = [(ident, "ident"), (tri, "tri"), (ones, "ones"), (headmask, "headmask"), (eiota, "eiota"),
                  (ebase, "ebase"), (wq, "wq"), (wkv, "wkv"), (wo, "wo"), (bv, "bv"), (gq, "gq"), (gk, "gk"),
                  (gate, "gate"), (rgu_w, "rgu"), (rd_w, "rd"), (srgu_w, "srgu")]
        bcasts = [(bq, "bq"), (bk, "bk"), (bo, "bo")]
        N_CONST = 16 * (len(consts) + len(bcasts) + 2)

        with ExitStack() as cx:
            def csb(name, shape, dt=F32):
                return cx.enter_context(nc.sbuf_tensor(name, shape, dt))
            raw = csb("raw", [P, 2, RAW])
            sraw = csb("sraw", [P, 3 * RANK + 2 * SHARED + DIM])
            bv_cols = csb("bv_cols", [P, CH, P])
            o_ug, o_cg, o_uu, o_cu = 0, RANK, RANK + INNER, 2 * RANK + INNER
            o_ud, o_cd = 2 * (RANK + INNER), 2 * (RANK + INNER) + RANK
            s_ug, s_cg, s_uu, s_cu = 0, RANK, RANK + SHARED, 2 * RANK + SHARED
            s_ud, s_cd = 2 * (RANK + SHARED), 2 * (RANK + SHARED) + RANK
            ld_sraw = cx.enter_context(nc.semaphore("ld_sraw"))
            ld_raw = [cx.enter_context(nc.semaphore(f"ld_raw{k}")) for k in range(2)]
            set_up = cx.enter_context(nc.semaphore("set_up"))
            sh_psum = cx.enter_context(nc.semaphore("sh_psum"))
            sh_done = cx.enter_context(nc.semaphore("sh_done"))
            up_psum = cx.enter_context(nc.semaphore("up_psum"))
            up_kept = cx.enter_context(nc.semaphore("up_kept"))
            up_ps = [bank03[:, k, 0:2 * INNER] for k in range(2)]
            down_ps = [bank03[:, 2 + k, 0:DIM] for k in range(2)]

            with nc.Block() as block:
                @block.sync
                def _(sp):
                    for tile, name in consts:
                        sp.dma_start(tile[:], a[name]).then_inc(ld_const, 16)
                    for tile, name in bcasts:
                        sp.dma_start(tile[:], a[name].broadcast_to([P, DIM])).then_inc(ld_const, 16)
                    sp.dma_start(srd_w[:, 0:2, :], a["srd"][0:2 * P].rearrange("(c p) r -> p c r", p=P))\
                        .then_inc(ld_const, 16)
                    sp.dma_start(srd_w[0:SLAST, 2, :], a["srd"][2 * P:SHARED]).then_inc(ld_const, 16)
                    sp.dma_start(sraw[:, :], a["sraw"]).then_inc(ld_sraw, 16)

                    def load(e, ph):
                        if past(e, 2):
                            sp.wait_ge(up_psum, e - 1)
                        sp.dma_start(raw[:, ph % 2, :], at(a["raw"], e)).then_inc(ld_raw[ph % 2], 16)
                    pipeline(sp, 2, EXPERTS, EXPERTS, 2, load)

                @block.tensor
                def _(pe):
                    pe.wait_ge(ld_sraw, 16)
                    nc.tensor.matmul(bank4[:, 0:SHARED], sraw[:, s_ug:s_ug + RANK], sraw[:, s_cg:s_cg + SHARED],
                                     start=True, stop=True)
                    nc.tensor.matmul(bank5[:, 0:SHARED], sraw[:, s_uu:s_uu + RANK], sraw[:, s_cu:s_cu + SHARED],
                                     start=True, stop=True)
                    nc.tensor.matmul(bank6[:, 0:DIM], sraw[:, s_ud:s_ud + RANK], sraw[:, s_cd:s_cd + DIM],
                                     start=True, stop=True)
                    pe.wait_ge(ld_const, N_CONST)
                    pe.wait_ge(set_up, 4)
                    for c in range(CH):
                        m = nc.tensor.matmul(bank7[:, 0:DIM], bv_cols[:, c, :], wo[:, c, :],
                                             start=(c == 0), stop=(c == CH - 1))
                    m.then_inc(sh_psum, 1)

                    def products(e, ph):
                        b = ph % 2
                        pe.wait_ge(ld_raw[b], landed(e, 2, b))
                        if past(e, 2):
                            pe.wait_ge(up_kept, 2 * e - 2)
                        r = raw[:, b, :]
                        nc.tensor.matmul(up_ps[b][:, 0:INNER], r[:, o_ug:o_ug + RANK], r[:, o_cg:o_cg + INNER],
                                         start=True, stop=True)
                        nc.tensor.matmul(up_ps[b][:, INNER:2 * INNER], r[:, o_uu:o_uu + RANK],
                                         r[:, o_cu:o_cu + INNER], start=True, stop=True)
                        nc.tensor.matmul(down_ps[b], r[:, o_ud:o_ud + RANK], r[:, o_cd:o_cd + DIM],
                                         start=True, stop=True).then_inc(up_psum, 1)
                    pipeline(pe, 4, EXPERTS, EXPERTS, 2, products)

                @block.vector
                def _(dve):
                    nc.vector.memset(mhalf[:, :], -0.5)
                    nc.vector.memset(sup_w[:, :, SHARED:SPAD], 0.0)
                    dve.wait_ge(ld_const, N_CONST)
                    nc.vector.tensor_tensor(gqk[:, :], gq[:, :], gk[:, :], ALU.mult).then_inc(set_up, 1)
                    dve.wait_ge(set_up, 1)
                    nc.vector.tensor_scalar(gqk[:, :], gqk[:, :], float(HD) ** -0.5, None, ALU.mult)\
                        .then_inc(set_up, 1)
                    for c in range(CH):
                        nc.vector.tensor_scalar(bv_cols[:, c, :], ones[:, :], bv[:, c:c + 1], None, ALU.mult)\
                            .then_inc(set_up, 1)
                    dve.wait_ge(sh_psum, 1)
                    nc.vector.tensor_copy(sup_w[:, 0, 0:SHARED], bank4[:, 0:SHARED])
                    nc.vector.tensor_copy(sup_w[:, 1, 0:SHARED], bank5[:, 0:SHARED])
                    nc.vector.tensor_copy(sdown_w[:, :], bank6[:, 0:DIM])
                    nc.vector.tensor_tensor(bo[:, :], bank7[:, 0:DIM], bo[:, :], ALU.add).then_inc(sh_done, 1)

                    def keep(e, ph):
                        b = ph % 2
                        dve.wait_ge(up_psum, e + 1)
                        nc.vector.tensor_scalar(col(up_w, e), up_ps[b], 1.0, None,
                                                ALU.mult).then_inc(up_kept, 1)
                        nc.vector.tensor_scalar(col(down_w, e), down_ps[b], 1.0, None,
                                                ALU.mult).then_inc(up_kept, 1)
                    pipeline(dve, 2, EXPERTS, EXPERTS, 2, keep)
                    dve.wait_ge(sh_done, 1)
                    dve.wait_ge(up_kept, 2 * EXPERTS)

        with ExitStack() as cx:
            def asb(name, shape, dt=F32):
                return cx.enter_context(nc.sbuf_tensor(name, shape, dt))

            def asem(name):
                return cx.enter_context(nc.semaphore(name))
            xin = asb("xin", [P, 2, DIM])
            ctxt = asb("ctxt", [P, 2, CH, P])
            xres = asb("xres", [P, 2, DIM])
            stats = asb("stats", [P, 2, 6])
            mean1 = asb("mean1", [P, 2, 2])
            rstd1 = asb("rstd1", [P, 2, 1])
            xn1 = asb("xn1", [P, 2, DIM])
            xn1t = asb("xn1t", [P, 2, CH, P])
            qb = asb("qb", [P, 2, DIM])
            kb = asb("kb", [P, 2, DIM])
            squares = asb("squares", [P, DIM])
            ssq = asb("ssq", [P, 2, 2])
            rqk = asb("rqk", [P, 2, 2])
            v17 = asb("v17", [P, 2, 2, PAIRS, HD + 1])
            v2 = asb("v2", [P, 2, 2, 2, PAIRS, HD + 1])
            qt = asb("qt", [P, 2, CH, P])
            ktm = asb("ktm", [P, 2, 2 * CH, GH, SEQ])
            smax = asb("smax", [P, 2, GROUPS, CH * GH])
            prob = asb("prob", [P, 2, PAIRS, P])
            probt = asb("probt", [P, 2, PAIRS, P])
            rsum = asb("rsum", [P, 2, PAIRS, 2])
            on = asb("on", [P, 2, DIM])
            ot = asb("ot", [P, 2, CH, P])
            xrb = asb("xrb", [P, 2, DIM])
            x1 = asb("x1", [P, 2, DIM])
            stats2 = asb("stats2", [P, 2, 6])
            mean2 = asb("mean2", [P, 2, 2])
            rstd2 = asb("rstd2", [P, 2, 1])
            xn2 = asb("xn2", [P, 2, DIM])
            xn2t = asb("xn2t", [P, 2, CH, P])
            rgu = asb("rgu", [P, 2, DIM])
            top8 = asb("top8", [P, 2, 8])
            ntop = asb("ntop", [P, 2, 1])
            top8i = asb("top8i", [P, 2, 8], U32)
            topif = asb("topif", [P, 2, TOPK])
            egate = asb("egate", [P, 2, EXPERTS])
            etop = asb("etop", [P, 2, TOPK])
            zsum = asb("zsum", [P, 2, 2])
            wden = asb("wden", [P, 2, 2])
            chosen = asb("chosen", [P, 2, TOPK, EXPERTS])
            member = asb("member", [P, 2, EXPERTS])
            members = asb("members", [P, EXPERTS])
            rowof = asb("rowof", [P, 2, EXPERTS])
            picked = asb("picked", [P, 2, TOPK, EXPERTS])
            slotf = asb("slotf", [P, 2, TOPK])
            sloti = asb("sloti", [P, 2, TOPK], I32)

            s_ps = bank03[:, 0:GROUPS, :]
            kv_ps = bank03[:, 2, :]
            qkt_ps = bank03[:, 3, :].rearrange("p (c t) -> p c t", c=2 * CH)
            y_ps = bank03[:, 3, 0:DIM]
            pt_ps = bank4[:, :].rearrange("p (c t) -> p c t", c=4)
            r_ps = bank5[:, 480:480 + EXPERTS]
            o_ps = bank5[:, 0:PAIRS * 2 * (HD + 1)].rearrange("p (g r d) -> p g r d", g=PAIRS, r=2)
            x2t_ps = bank6[:, 0:DIM]
            l_ps = bank6[:, DIM:DIM + EXPERTS]
            xnt_ps = bank7[:, 0:DIM].rearrange("p (c t) -> p c t", c=CH)
            q_ps = bank7[:, 0:DIM]

            ld_x, ld_ctx, ld_xres, v2_in, st_x1, st_x2t, sc_out = (
                [asem(f"{n}{k}") for k in range(2)]
                for n in ("ld_x", "ld_ctx", "ld_xres", "v2_in", "st_x1", "st_x2t", "sc_out"))
            preset = asem("preset")
            ln1_st, ln1_mv, ln1_ve, ln1_rstd, xn1_done = (asem(n) for n in ("ln1_st", "ln1_mv", "ln1_ve", "ln1_rstd", "xn1_done"))
            xnt_psum, xnt_done, q_psum, kv_psum = (asem(n) for n in ("xnt_psum", "xnt_done", "q_psum", "kv_psum"))
            qb_done, kb_done, v_done, ssq_done, msq_done, rqk_done, kn_done = (
                asem(n) for n in ("qb_done", "kb_done", "v_done", "ssq_done", "msq_done", "rqk_done", "kn_done"))
            qkt_psum, qt_done, ktm_done, s_psum, smax_done, ssub_done, prob_done = (
                asem(n) for n in ("qkt_psum", "qt_done", "ktm_done", "s_psum", "smax_done", "ssub_done", "prob_done"))
            pt_psum, pt_done, o_psum, rsum_done, on_done, ot_psum, ot_done, y_psum, xrb_done, x1_done = (
                asem(n) for n in ("pt_psum", "pt_done", "o_psum", "rsum_done", "on_done", "ot_psum", "ot_done",
                                  "y_psum", "xrb_done", "x1_done"))
            ln2_st, ln2_mv, ln2_ve, ln2_rstd, xn2_done, x2t_psum, x2t_done = (
                asem(n) for n in ("ln2_st", "ln2_mv", "ln2_ve", "ln2_rstd", "xn2_done", "x2t_psum", "x2t_done"))
            l_psum, rgu_psum, rgu_done, top_done, ntop_done, topi_done, topif_done, gexp_done, wden_done, wt_done = (
                asem(n) for n in ("l_psum", "rgu_psum", "rgu_done", "top_done", "ntop_done", "topi_done",
                                  "topif_done", "gexp_done", "wden_done", "wt_done"))
            chosen_done, member_done, r_psum, rowof_done, picked_done, slotf_done, sloti_done, members_done = (
                asem(n) for n in ("chosen_done", "member_done", "r_psum", "rowof_done", "picked_done",
                                  "slotf_done", "sloti_done", "members_done"))
            STEPS = TILES + 5
            LEAD = 8

            x_t = a["x"].rearrange("(t p) d -> t p d", p=P)
            ctx_t = a["ctxt"].rearrange("p c (t k) -> t p c k", k=P)

            def run(eng, body):
                pipeline(eng, LEAD, TILES, STEPS, 2, body)

            with nc.Block() as block:
                @block.sync
                def _(sp):
                    def body(s, ph):
                        i, b = s, ph % 2
                        if live(i, TILES):
                            if past(i, 2):
                                sp.wait_ge(xn1_done, i - 1)
                            sp.dma_start(xin[:, b, :], at(x_t, i)).then_inc(ld_x[b], 16)
                            if past(i, 2):
                                sp.wait_ge(kv_psum, i - 1)
                            src = ctx_t[i] if isinstance(i, int) else \
                                ctx_t[bass.ds(i, 1), :, :, :].rearrange("t p c k -> (t p) c k")
                            sp.dma_start(ctxt[:, b, :, :], src).then_inc(ld_ctx[b], 16)
                        i, b = s - 2, ph % 2
                        if live(i, TILES):
                            if past(i, 2):
                                sp.wait_ge(xrb_done, i - 1)
                            sp.dma_start(xres[:, b, :], at(x_t, i)).then_inc(ld_xres[b], 16)
                        i, b = s - 4, ph % 2
                        if live(i, TILES):
                            sp.wait_ge(x2t_done, i + 1)
                            sp.dma_start(at(xn2t_d, i), xn2t[:, b, :, :].rearrange("p c t -> p (c t)"))\
                                .then_inc(st_x2t[b], 16)
                        i, b = s - 1, (ph - 1) % 2
                        if live(i, TILES):
                            sp.wait_ge(v_done, i + 1)
                            if past(i, 2):
                                sp.wait_ge(o_psum, i - 1)
                            for n in range(2):
                                for r in range(2):
                                    sp.dma_start(v2[SEQ * r:SEQ * (r + 1), b, n, r, :, :],
                                                 v17[SEQ * n:SEQ * (n + 1), b, r, :, :]).then_inc(v2_in[b], 16)
                        i, b = s - 3, (ph - 3) % 2
                        if live(i, TILES):
                            sp.wait_ge(x1_done, i + 1)
                            sp.dma_start(at(x1_d, i), x1[:, b, :]).then_inc(st_x1[b], 16)
                    run(sp, body)
                    for k in range(2):
                        sp.wait_ge(st_x1[k], 16 * TILES // 2)
                        sp.wait_ge(st_x2t[k], 16 * TILES // 2)

                @block.tensor
                def _(pe):
                    def rank(s, ph):
                        i, b = s - 5, (ph - 5) % 2
                        if not live(i, TILES):
                            return
                        pe.wait_ge(member_done, i + 1)
                        pe.wait_ge(members_done, i + 1)
                        nc.tensor.matmul(r_ps, tri[:, :], member[:, b, :], start=True, stop=False)
                        nc.tensor.matmul(r_ps, ones[:, :], members[:, :], start=False, stop=True).then_inc(r_psum, 1)

                    def p_turn(s, ph, r):
                        i, b = s - 3, (ph - 3) % 2
                        if not live(i, TILES):
                            return
                        if r == 0:
                            pe.wait_ge(prob_done, i + 1)
                            if past(i, 1):
                                pe.wait_ge(ot_done, i)
                        else:
                            pe.wait_ge(pt_done, 2 * i + 1)
                        for k in range(4):
                            blk = 4 * r + k
                            m = nc.tensor.transpose(pt_ps[:, k, :], prob[:, b, blk, :], ident[:, :])
                        m.then_inc(pt_psum, 1)

                    def p_times_v(s, ph, r):
                        i, b = s - 3, (ph - 3) % 2
                        if not live(i, TILES):
                            return
                        pe.wait_ge(pt_done, 2 * i + r + 1)
                        if r == 0:
                            pe.wait_ge(v2_in[b], landed(i, 2, b, 64))
                            if past(i, 1):
                                pe.wait_ge(on_done, i)
                            if live(s - 5, TILES):
                                pe.wait_ge(rowof_done, s - 4)
                        for k in range(4):
                            blk = 4 * r + k
                            group, c, hp = blk // 4, blk // 2 % 2, blk % 2
                            pair = PAIRS // CH * c + GH // 2 * group + hp
                            for n in range(2):
                                m = nc.tensor.matmul(o_ps[SEQ * n:SEQ * (n + 1), pair, :, :],
                                                     probt[:, b, blk, SEQ * n:SEQ * (n + 1)],
                                                     v2[:, b, n, :, pair, :], start=True, stop=True)
                        if r == 1:
                            m.then_inc(o_psum, 1)

                    def x_turn(s, ph):
                        i, b = s - 1, (ph - 1) % 2
                        if not live(i, TILES):
                            return
                        pe.wait_ge(xn1_done, i + 1)
                        if past(i, 1):
                            pe.wait_ge(qb_done, i)
                        for c in range(CH):
                            m = nc.tensor.transpose(xnt_ps[:, c, :], xn1[:, b, c * P:(c + 1) * P], ident[:, :])
                        m.then_inc(xnt_psum, 1)

                    def qkv(s, ph):
                        i, b = s - 1, (ph - 1) % 2
                        if not live(i, TILES):
                            return
                        pe.wait_ge(xnt_done, i + 1)
                        for c in range(CH):
                            m = nc.tensor.matmul(q_ps, xn1t[:, b, c, :], wq[:, c, :], start=(c == 0), stop=(c == CH - 1))
                        m.then_inc(q_psum, 1)
                        pe.wait_ge(ld_ctx[b], landed(i, 2, b))
                        if past(i, 1):
                            pe.wait_ge(kb_done, i)
                            pe.wait_ge(v_done, i)
                        for c in range(CH):
                            m = nc.tensor.matmul(kv_ps, ctxt[:, b, c, :], wkv[:, c, :], start=(c == 0), stop=(c == CH - 1))
                        m.then_inc(kv_psum, 1)

                    def qk_turn(s, ph):
                        i, b = s - 2, ph % 2
                        if not live(i, TILES):
                            return
                        pe.wait_ge(qb_done, i + 1)
                        pe.wait_ge(kn_done, i + 1)
                        if live(s - 4, TILES):
                            pe.wait_ge(x1_done, s - 3)
                        for c in range(CH):
                            nc.tensor.transpose(qkt_ps[:, c, :], qb[:, b, c * P:(c + 1) * P], ident[:, :])
                        for c in range(CH):
                            m = nc.tensor.transpose(qkt_ps[:, CH + c, :], kb[:, b, c * P:(c + 1) * P], ident[:, :])
                        m.then_inc(qkt_psum, 1)

                    def scores_ready(s, ph):
                        i = s - 2
                        if not live(i, TILES):
                            return
                        pe.wait_ge(ktm_done, i + 1)
                        if past(i, 1):
                            pe.wait_ge(ssub_done, i)

                    def scores(s, ph):
                        i, b = s - 2, ph % 2
                        if not live(i, TILES):
                            return
                        for c in range(CH):
                            for n in range(2):
                                for g in range(GROUPS):
                                    feats = slice(64 * g, 64 * (g + 1))
                                    m = nc.tensor.matmul(s_ps[SEQ * n:SEQ * (n + 1), g, c * 256:(c + 1) * 256],
                                                         qt[feats, b, c, SEQ * n:SEQ * (n + 1)],
                                                         ktm[feats, b, 2 * c + n, :, :], start=True, stop=True)
                        m.then_inc(s_psum, 1)

                    def x2_turn(s, ph):
                        i, b = s - 4, ph % 2
                        if not live(i, TILES):
                            return
                        pe.wait_ge(xn2_done, i + 1)
                        if past(i, 1):
                            pe.wait_ge(gexp_done, 2 * i)
                        for c in range(CH):
                            m = nc.tensor.transpose(x2t_ps[:, c * P:(c + 1) * P], xn2[:, b, c * P:(c + 1) * P], ident[:, :])
                        m.then_inc(x2t_psum, 1)

                    def gate_in(s, ph):
                        i, b = s - 4, ph % 2
                        if not live(i, TILES):
                            return
                        pe.wait_ge(x2t_done, i + 1)
                        for c in range(CH):
                            m = nc.tensor.matmul(l_ps, xn2t[:, b, c, :], gate[:, c, :], start=(c == 0), stop=(c == CH - 1))
                        m.then_inc(l_psum, 1)
                        for c in range(CH):
                            m = nc.tensor.matmul(x2t_ps, xn2t[:, b, c, :], rgu_w[:, c, :], start=(c == 0), stop=(c == CH - 1))
                        m.then_inc(rgu_psum, 1)

                    def o_turn(s, ph):
                        i, b = s - 3, (ph - 3) % 2
                        if not live(i, TILES):
                            return
                        pe.wait_ge(on_done, i + 1)
                        for c in range(CH):
                            m = nc.tensor.transpose(pt_ps[:, c, :], on[:, b, c * P:(c + 1) * P], ident[:, :])
                        m.then_inc(ot_psum, 1)

                    def project(s, ph):
                        i, b = s - 3, (ph - 3) % 2
                        if not live(i, TILES):
                            return
                        pe.wait_ge(ot_done, i + 1)
                        if live(s - 2, TILES):
                            pe.wait_ge(ktm_done, s - 1)
                        for c in range(CH):
                            m = nc.tensor.matmul(y_ps, ot[:, b, c, :], wo[:, c, :], start=(c == 0), stop=(c == CH - 1))
                        m.then_inc(y_psum, 1)

                    def body(s, ph):
                        rank(s, ph)
                        p_turn(s, ph, 0)
                        x_turn(s, ph)
                        qk_turn(s, ph)
                        p_times_v(s, ph, 0)
                        scores_ready(s, ph)
                        p_turn(s, ph, 1)
                        scores(s, ph)
                        x2_turn(s, ph)
                        qkv(s, ph)
                        p_times_v(s, ph, 1)
                        gate_in(s, ph)
                        o_turn(s, ph)
                        project(s, ph)
                    run(pe, body)

                @block.scalar
                def _(act):
                    act.wait_ge(preset, 2)

                    def p_keep(s, ph, r):
                        i, b = s - 3, (ph - 3) % 2
                        if not live(i, TILES):
                            return
                        act.wait_ge(pt_psum, 2 * i + r + 1)
                        nc.scalar.activation(probt[:, b, 4 * r:4 * r + 4, :], pt_ps, ACT.Copy).then_inc(pt_done, 1)

                    def body(s, ph):
                        p_keep(s, ph, 0)
                        i, b = s - 1, (ph - 1) % 2
                        if live(i, TILES):
                            act.wait_ge(xnt_psum, i + 1)
                            nc.scalar.activation(xn1t[:, b, :, :], xnt_ps, ACT.Copy).then_inc(xnt_done, 1)
                        i, b = s - 2, ph % 2
                        if live(i, TILES):
                            act.wait_ge(qkt_psum, i + 1)
                            for c in range(CH):
                                nc.scalar.activation(qt[:, b, c, :], qkt_ps[:, c, :], ACT.Copy,
                                                     scale=gqk[:, c:c + 1]).then_inc(qt_done, 1)
                        p_keep(s, ph, 1)
                        i, b = s - 4, ph % 2
                        if live(i, TILES):
                            act.wait_ge(x2t_psum, i + 1)
                            if past(i, 2):
                                act.wait_ge(st_x2t[b], landed(i, 2, b) - 16)
                            nc.scalar.activation(xn2t[:, b, :, :].rearrange("p c t -> p (c t)"), x2t_ps,
                                                 ACT.Copy).then_inc(x2t_done, 1)
                        i, b = s - 2, ph % 2
                        if live(i, TILES):
                            act.wait_ge(ssub_done, i + 1)
                            pb = prob[:, b, :, :].rearrange("p q k -> p (q k)")
                            nc.scalar.activation(pb, pb, ACT.Exp, scale=rqk[:, b, 0:1]).then_inc(prob_done, 1)
                        i, b = s - 1, (ph - 1) % 2
                        if live(i, TILES):
                            act.wait_ge(kb_done, i + 1)
                            if past(i, 2):
                                act.wait_ge(v2_in[b], landed(i, 2, b, 64) - 64)
                            nc.scalar.activation(
                                v17[:, b, :, :, 0:HD],
                                kv_ps[:, DIM:2 * DIM].rearrange("p (r g d) -> p r g d", r=2, g=PAIRS),
                                ACT.Copy).then_inc(v_done, 1)
                            act.wait_ge(qb_done, i + 1)
                            if past(i, 1):
                                act.wait_ge(ssq_done, 2 * i)
                            nc.scalar.activation(squares[:, :], qb[:, b, :], ACT.Square,
                                                 accum_out=ssq[:, b, 0:1]).then_inc(ssq_done, 1)
                            act.wait_ge(kb_done, i + 1)
                            act.wait_ge(ssq_done, 2 * i + 1)
                            nc.scalar.activation(squares[:, :], kb[:, b, :], ACT.Square,
                                                 accum_out=ssq[:, b, 1:2]).then_inc(ssq_done, 1)
                        i, b = s - 3, (ph - 3) % 2
                        if live(i, TILES):
                            act.wait_ge(ot_psum, i + 1)
                            nc.scalar.activation(ot[:, b, :, :], pt_ps[:, 0:CH, :], ACT.Copy).then_inc(ot_done, 1)
                        i, b = s - 4, ph % 2
                        if live(i, TILES):
                            act.wait_ge(topi_done, i + 1)
                            nc.scalar.activation(egate[:, b, :], l_ps, ACT.Exp, bias=ntop[:, b, :],
                                                 accum_out=zsum[:, b, 0:1]).then_inc(gexp_done, 1)
                            nc.scalar.activation(etop[:, b, :], top8[:, b, 0:TOPK], ACT.Exp, bias=ntop[:, b, :],
                                                 accum_out=zsum[:, b, 1:2]).then_inc(gexp_done, 1)
                    run(act, body)

                @block.gpsimd
                def _(pool):
                    def body(s, ph):
                        i, b = s - 5, (ph - 5) % 2
                        if live(i, TILES):
                            pool.wait_ge(sloti_done, i + 1)
                            pool.wait_ge(rgu_done, i + 1)
                        i, b = s, ph % 2
                        if live(i, TILES):
                            pool.wait_ge(ln1_ve, i + 1)
                        pool.wait_ge(preset, 2)
                        if live(i, TILES):
                            nc.gpsimd.tensor_tensor(rstd1[:, b, :], mean1[:, b, 1:2], mhalf[:, 0:1], ALU.pow)\
                                .then_inc(ln1_rstd, 1)
                        i, b = s - 5, (ph - 5) % 2
                        if live(i, TILES):
                            for k in range(TOPK):
                                nc.gpsimd.indirect_dma_start(
                                    xs_d, bass.IndirectOffsetOnAxis(sloti[:, b, k:k + 1], 0), rgu[:, b, :], None)\
                                    .then_inc(sc_out[b], 16)
                        i, b = s - 3, (ph - 3) % 2
                        if live(i, TILES):
                            pool.wait_ge(ld_xres[b], landed(i, 2, b))
                            if past(i, 2):
                                pool.wait_ge(x1_done, i - 1)
                            nc.gpsimd.tensor_tensor(xrb[:, b, :], xres[:, b, :], bo[:, :], ALU.add).then_inc(xrb_done, 1)
                        i, b = s - 1, (ph - 1) % 2
                        if live(i, TILES):
                            pool.wait_ge(msq_done, i + 1)
                            nc.gpsimd.tensor_tensor(rqk[:, b, :], ssq[:, b, :], mhalf[:, :], ALU.pow).then_inc(rqk_done, 1)
                        i, b = s - 3, (ph - 3) % 2
                        if live(i, TILES):
                            pool.wait_ge(ln2_ve, i + 1)
                            nc.gpsimd.tensor_tensor(rstd2[:, b, :], mean2[:, b, 1:2], mhalf[:, 0:1], ALU.pow)\
                                .then_inc(ln2_rstd, 1)
                    run(pool, body)
                    for k in range(2):
                        pool.wait_ge(sc_out[k], 16 * TOPK * TILES // 2)

                @block.vector
                def _(dve):
                    nc.vector.memset(v17[:, :, :, :, :], 1.0).then_inc(preset, 1)
                    nc.vector.memset(v2[:, :, :, :, :, :], 0.0).then_inc(preset, 1)
                    nc.vector.memset(members[:, :], 0.0).then_inc(members_done, 1)

                    def slot_rows(s, ph):
                        i, b = s - 5, (ph - 5) % 2
                        if not live(i, TILES):
                            return
                        dve.wait_ge(r_psum, i + 1)
                        nc.vector.tensor_tensor(rowof[:, b, :], r_ps, ebase[:, :], ALU.add).then_inc(rowof_done, 1)
                        nc.vector.tensor_tensor(members[:, :], members[:, :], member[:, b, :], ALU.add)\
                            .then_inc(members_done, 1)
                        dve.wait_ge(rowof_done, i + 1)
                        nc.vector.tensor_tensor(picked[:, b, :, :], chosen[:, b, :, :],
                                                rowof[:, b, :].unsqueeze(1).broadcast_to([P, TOPK, EXPERTS]),
                                                ALU.mult).then_inc(picked_done, 1)
                        dve.wait_ge(picked_done, i + 1)
                        nc.vector.tensor_reduce(slotf[:, b, :], picked[:, b, :, :], AX.X, ALU.add).then_inc(slotf_done, 1)
                        dve.wait_ge(slotf_done, i + 1)
                        nc.vector.tensor_scalar(col(slots, i), slotf[:, b, :], 1.0, None, ALU.mult)
                        if past(i, 2):
                            dve.wait_ge(sc_out[b], landed(i, 2, b, 64) - 64)
                        nc.vector.tensor_copy(sloti[:, b, :], slotf[:, b, :]).then_inc(sloti_done, 1)

                    def k_spread(s, ph):
                        i, b = s - 2, ph % 2
                        if not live(i, TILES):
                            return
                        dve.wait_ge(qt_done, 2 * i + 2)
                        kt = qkt_ps[:, CH:2 * CH, :].rearrange("p c (n k) -> p (c n) k", n=2)
                        nc.vector.tensor_tensor(
                            ktm[:, b, :, :, :], kt.unsqueeze(2).broadcast_to([P, 2 * CH, GH, SEQ]),
                            headmask[:, :].unsqueeze(1).unsqueeze(3).broadcast_to([P, 2 * CH, GH, SEQ]),
                            ALU.mult).then_inc(ktm_done, 1)

                    def norm1_stats(s, ph):
                        i, b = s, ph % 2
                        if not live(i, TILES):
                            return
                        dve.wait_ge(ld_x[b], landed(i, 2, b))
                        nc.vector.bn_stats(stats[:, b, :], xin[:, b, :]).then_inc(ln1_st, 1)
                        dve.wait_ge(ln1_st, i + 1)
                        k_spread(s, ph)
                        nc.vector.bn_aggr(mean1[:, b, :], stats[:, b, :]).then_inc(ln1_mv, 1)
                        dve.wait_ge(ln1_mv, i + 1)
                        nc.vector.tensor_scalar(mean1[:, b, 1:2], mean1[:, b, 1:2], LN_EPS, None, ALU.add)\
                            .then_inc(ln1_ve, 1)

                    def norm1(s, ph):
                        i, b = s, ph % 2
                        if not live(i, TILES):
                            return
                        dve.wait_ge(ln1_rstd, i + 1)
                        nc.vector.tensor_scalar(xn1[:, b, :], xin[:, b, :], mean1[:, b, 0:1], rstd1[:, b, :],
                                                ALU.subtract, ALU.mult).then_inc(xn1_done, 1)

                    def soft(s, ph):
                        i, b = s - 2, ph % 2
                        if not live(i, TILES):
                            return
                        dve.wait_ge(s_psum, i + 1)
                        sv = s_ps.rearrange("p g (h k) -> p (g h) k", k=SEQ)
                        mv = smax[:, b, :, :].rearrange("p g h -> p (g h)")
                        nc.vector.tensor_reduce(mv, sv, AX.X, ALU.max).then_inc(smax_done, 1)
                        dve.wait_ge(smax_done, i + 1)
                        nc.vector.tensor_tensor(
                            prob[:, b, :, :].rearrange("p q (r k) -> p (q r) k", r=2), sv,
                            mv.unsqueeze(2).broadcast_to([P, HEADS, SEQ]), ALU.subtract).then_inc(ssub_done, 1)

                    def qk_bias(s, ph):
                        i, b = s - 1, (ph - 1) % 2
                        if not live(i, TILES):
                            return
                        dve.wait_ge(q_psum, i + 1)
                        nc.vector.tensor_tensor(qb[:, b, :], q_ps, bq[:, :], ALU.add).then_inc(qb_done, 1)
                        dve.wait_ge(kv_psum, i + 1)
                        nc.vector.tensor_tensor(kb[:, b, :], kv_ps[:, 0:DIM], bk[:, :], ALU.add).then_inc(kb_done, 1)

                    def o_norm(s, ph):
                        i, b = s - 3, (ph - 3) % 2
                        if not live(i, TILES):
                            return
                        dve.wait_ge(o_psum, i + 1)
                        nc.vector.reciprocal(rsum[:, b, :, :], o_ps[:, :, :, HD]).then_inc(rsum_done, 1)
                        dve.wait_ge(rsum_done, i + 1)
                        ov = on[:, b, :].rearrange("p (g r d) -> p (g r) d", g=PAIRS, r=2)
                        nc.vector.tensor_tensor(
                            ov, o_ps[:, :, :, 0:HD].rearrange("p g r d -> p (g r) d"),
                            rsum[:, b, :, :].rearrange("p g r -> p (g r)").unsqueeze(2).broadcast_to([P, HEADS, HD]),
                            ALU.mult).then_inc(on_done, 1)

                    def mean_square(s, ph):
                        i, b = s - 1, (ph - 1) % 2
                        if not live(i, TILES):
                            return
                        dve.wait_ge(ssq_done, 2 * i + 2)
                        nc.vector.tensor_scalar(ssq[:, b, :], ssq[:, b, :], 1.0 / DIM, RMS_EPS, ALU.mult, ALU.add)\
                            .then_inc(msq_done, 1)

                    def k_norm(s, ph):
                        i, b = s - 1, (ph - 1) % 2
                        if not live(i, TILES):
                            return
                        dve.wait_ge(rqk_done, i + 1)
                        nc.vector.tensor_scalar(kb[:, b, :], kb[:, b, :], rqk[:, b, 1:2], None, ALU.mult)\
                            .then_inc(kn_done, 1)

                    def gate_top(s, ph):
                        i, b = s - 4, ph % 2
                        if not live(i, TILES):
                            return
                        dve.wait_ge(l_psum, i + 1)
                        dve.wait_ge(rgu_psum, i + 1)
                        if past(i, 2):
                            dve.wait_ge(sc_out[b], landed(i, 2, b, 64) - 64)
                        nc.vector.tensor_copy(rgu[:, b, :], x2t_ps).then_inc(rgu_done, 1)
                        nc.vector.max(top8[:, b, :], l_ps).then_inc(top_done, 1)
                        dve.wait_ge(top_done, i + 1)
                        nc.vector.tensor_scalar(ntop[:, b, :], top8[:, b, 0:1], -1.0, None, ALU.mult).then_inc(ntop_done, 1)
                        nc.vector.max_index(top8i[:, b, :], top8[:, b, :], l_ps).then_inc(topi_done, 1)
                        dve.wait_ge(topi_done, i + 1)
                        nc.vector.tensor_copy(topif[:, b, :], top8i[:, b, 0:TOPK]).then_inc(topif_done, 1)
                        nc.vector.tensor_scalar(col(experts, i), top8i[:, b, 0:TOPK], 1, None, ALU.mult)
                        dve.wait_ge(topif_done, i + 1)
                        nc.vector.tensor_tensor(chosen[:, b, :, :],
                                                eiota[:, :].unsqueeze(1).broadcast_to([P, TOPK, EXPERTS]),
                                                topif[:, b, :].unsqueeze(2).broadcast_to([P, TOPK, EXPERTS]),
                                                ALU.is_equal).then_inc(chosen_done, 1)
                        dve.wait_ge(chosen_done, i + 1)
                        nc.vector.tensor_reduce(member[:, b, :], chosen[:, b, :, :].rearrange("p k e -> p e k"),
                                                AX.X, ALU.add).then_inc(member_done, 1)

                    def gate_weights(s, ph):
                        i, b = s - 4, ph % 2
                        if not live(i, TILES):
                            return
                        dve.wait_ge(gexp_done, 2 * i + 2)
                        nc.vector.scalar_tensor_tensor(out=wden[:, b, 0:1], in0=zsum[:, b, 0:1], scalar=1e-20,
                                                       in1=zsum[:, b, 1:2], op0=ALU.mult, op1=ALU.add)\
                            .then_inc(wden_done, 1)
                        dve.wait_ge(wden_done, 2 * i + 1)
                        nc.vector.reciprocal(wden[:, b, 1:2], wden[:, b, 0:1]).then_inc(wden_done, 1)
                        dve.wait_ge(wden_done, 2 * i + 2)
                        nc.vector.tensor_scalar(col(weights, i), etop[:, b, :], wden[:, b, 1:2], None, ALU.mult)\
                            .then_inc(wt_done, 1)

                    def residual(s, ph):
                        i, b = s - 3, (ph - 3) % 2
                        if not live(i, TILES):
                            return
                        dve.wait_ge(y_psum, i + 1)
                        dve.wait_ge(xrb_done, i + 1)
                        if past(i, 2):
                            dve.wait_ge(st_x1[b], landed(i, 2, b) - 16)
                        nc.vector.tensor_tensor(x1[:, b, :], y_ps, xrb[:, b, :], ALU.add).then_inc(x1_done, 1)
                        dve.wait_ge(x1_done, i + 1)
                        nc.vector.bn_stats(stats2[:, b, :], x1[:, b, :]).then_inc(ln2_st, 1)
                        dve.wait_ge(ln2_st, i + 1)
                        gate_weights(s, ph)
                        nc.vector.bn_aggr(mean2[:, b, :], stats2[:, b, :]).then_inc(ln2_mv, 1)
                        dve.wait_ge(ln2_mv, i + 1)
                        nc.vector.tensor_scalar(mean2[:, b, 1:2], mean2[:, b, 1:2], LN_EPS, None, ALU.add)\
                            .then_inc(ln2_ve, 1)

                    def norm2(s, ph):
                        i, b = s - 3, (ph - 3) % 2
                        if not live(i, TILES):
                            return
                        dve.wait_ge(ln2_rstd, i + 1)
                        nc.vector.tensor_scalar(xn2[:, b, :], x1[:, b, :], mean2[:, b, 0:1], rstd2[:, b, :],
                                                ALU.subtract, ALU.mult).then_inc(xn2_done, 1)

                    def body(s, ph):
                        slot_rows(s, ph)
                        norm1_stats(s, ph)
                        if not live(s, TILES):
                            k_spread(s, ph)
                        soft(s, ph)
                        norm1(s, ph)
                        qk_bias(s, ph)
                        o_norm(s, ph)
                        mean_square(s, ph)
                        gate_top(s, ph)
                        k_norm(s, ph)
                        residual(s, ph)
                        if not live(s - 3, TILES):
                            gate_weights(s, ph)
                        norm2(s, ph)
                    run(dve, body)
        table = sb("table", [1, ETILES, 2], I32)
        shift = sb("shift", [P, EXPERTS])
        zeros = sb("zeros", [P, DIM])
        counts = sb("counts", [1, EXPERTS], I32)
        with ExitStack() as cx:
            def tsb(name, shape, dt=F32):
                return cx.enter_context(nc.sbuf_tensor(name, shape, dt))
            total_f = tsb("total_f", [P, EXPERTS])
            total_i = tsb("total_i", [P, EXPERTS], I32)
            tiles_i = tsb("tiles_i", [P, EXPERTS], I32)
            tiles_f = tsb("tiles_f", [P, EXPERTS])
            tail_f = tsb("tail_f", [P, EXPERTS])
            ends = tsb("ends", [P, EXPERTS])
            tile_no = tsb("tile_no", [1, ETILES])
            over = tsb("over", [1, ETILES, EXPERTS])
            skipped = tsb("skipped", [1, ETILES, EXPERTS])
            owner = tsb("owner", [1, ETILES])
            start = tsb("start", [1, ETILES])
            row = tsb("row", [1, ETILES])
            tmp = tsb("tmp", [1, ETILES, 2])
            ld_no = cx.enter_context(nc.semaphore("ld_no"))
            tot_psum = cx.enter_context(nc.semaphore("tot_psum"))
            chain = cx.enter_context(nc.semaphore("chain"))
            tail_out = cx.enter_context(nc.semaphore("tail_out"))
            with nc.Block() as block:
                @block.tensor
                def _(pe):
                    nc.tensor.matmul(bank7[:, 0:EXPERTS], ones[:, :], members[:, :], start=True, stop=True)\
                        .then_inc(tot_psum, 1)

                @block.vector
                def _(dve):
                    done = [0]

                    def step(ins):
                        ins.then_inc(chain, 1)
                        done[0] += 1
                        dve.wait_ge(chain, done[0])
                    step(nc.vector.memset(zeros[:, :], 0.0))
                    dve.wait_ge(tot_psum, 1)
                    step(nc.vector.tensor_copy(total_f[:, :], bank7[:, 0:EXPERTS]))
                    step(nc.vector.tensor_tensor(tail_f[:, :], total_f[:, :], ebase[:, :], ALU.add))
                    step(nc.vector.tensor_copy(counts[:, :], tail_f[0:1, :]))
                    step(nc.vector.tensor_scalar(total_f[:, :], total_f[:, :], float(P - 1), None, ALU.add))
                    step(nc.vector.tensor_copy(total_i[:, :], total_f[:, :]))
                    step(nc.vector.tensor_scalar(tiles_i[:, :], total_i[:, :], 7, None, ALU.logical_shift_right))
                    step(nc.vector.tensor_copy(tiles_f[:, :], tiles_i[:, :]))
                    step(nc.vector.tensor_tensor_scan(ends[:, :], ones[:, 0:EXPERTS], tiles_f[:, :], 0.0,
                                                      ALU.mult, ALU.add))
                    step(nc.vector.tensor_tensor(shift[:, :], ends[:, :], tiles_f[:, :], ALU.subtract))
                    step(nc.vector.scalar_tensor_tensor(out=shift[:, :], in0=shift[:, :], scalar=float(P),
                                                        in1=ebase[:, :], op0=ALU.mult, op1=ALU.subtract))
                    dve.wait_ge(ld_no, 16)
                    shape = [1, ETILES, EXPERTS]
                    step(nc.vector.tensor_tensor(over[:, :, :], ends[0:1, :].unsqueeze(1).broadcast_to(shape),
                                                 tile_no[:, :].unsqueeze(2).broadcast_to(shape), ALU.is_le))
                    step(nc.vector.tensor_tensor(skipped[:, :, :], over[:, :, :],
                                                 tiles_f[0:1, :].unsqueeze(1).broadcast_to(shape), ALU.mult))
                    step(nc.vector.tensor_reduce(owner[:, :], over[:, :, :], AX.X, ALU.add))
                    step(nc.vector.tensor_reduce(start[:, :], skipped[:, :, :], AX.X, ALU.add))
                    step(nc.vector.tensor_tensor(start[:, :], tile_no[:, :], start[:, :], ALU.subtract))
                    step(nc.vector.tensor_scalar(start[:, :], start[:, :], float(P), None, ALU.mult))
                    step(nc.vector.scalar_tensor_tensor(out=row[:, :], in0=owner[:, :], scalar=float(CAP),
                                                        in1=start[:, :], op0=ALU.mult, op1=ALU.add))
                    step(nc.vector.tensor_scalar(tmp[:, :, 0], owner[:, :], float(EXPERTS - 1), None, ALU.min))
                    step(nc.vector.tensor_scalar(tmp[:, :, 1], row[:, :], float(DUMP), None, ALU.min))
                    step(nc.vector.tensor_copy(table[:, :, :], tmp[:, :, :]))

                @block.sync
                def _(sp):
                    sp.dma_start(tile_no[:, :], a["tileno"]).then_inc(ld_no, 16)
                    sp.wait_ge(chain, 4)
                    sp.dma_start(xs_d[DUMP:DUMP + P, :], zeros[:, :]).then_inc(tail_out, 16)

                    def tail(e, ph):
                        at_e = counts[0:1, e:e + 1] if isinstance(e, int) else counts[0:1, bass.ds(e, 1)]
                        free = sp.value_load(at_e, min_val=0, max_val=DUMP - P)
                        sp.dma_start(xs_d[bass.ds(free, P), :], zeros[:, :]).then_inc(tail_out, 16)
                    pipeline(sp, 1, EXPERTS, EXPERTS, 1, tail)
                    sp.wait_ge(tail_out, 16 * (EXPERTS + 1))

        with ExitStack() as cx:
            def esb(name, shape, dt=F32):
                return cx.enter_context(nc.sbuf_tensor(name, shape, dt))
            RING = 4
            xg = esb("xg", [P, RING, DIM])
            xgt = esb("xgt", [P, 2, 2, P])
            gated = esb("gated", [P, 2, INNER])
            h = esb("h", [P, 2, INNER])
            ht = esb("ht", [HALF, 2, 2, P])
            rdt = esb("rdt", [P, 2, P])
            yo = esb("yo", [P, RING, DIM])
            xgt_ps = bank03[:, 0, 0:2 * P]
            ht_ps = bank03[0:HALF, 1, 0:2 * P]
            gu_ps = [bank03[:, 2 + k, 0:2 * INNER] for k in range(2)]
            y_ps = [bank4[:, 0:DIM], bank5[:, 0:DIM]]
            rd_ps = bank6[:, 0:P]
            ld_xg = [cx.enter_context(nc.semaphore(f"ld_xg{k}")) for k in range(RING)]
            st_y = [cx.enter_context(nc.semaphore(f"st_y{k}")) for k in range(RING)]
            (xgt_psum, xgt_done, gu_psum, gated_done, h_done, ht_psum, ht_done, rd_psum, rdt_done, ye_psum,
             yo_done) = (cx.enter_context(nc.semaphore(n)) for n in (
                 "xgt_psum", "xgt_done", "gu_psum", "gated_done", "h_done", "ht_psum", "ht_done", "rd_psum",
                 "rdt_done", "ye_psum", "yo_done"))
            N = ETILES
            ys_t = ys_d.rearrange("(t p) d -> t p d", p=P)
            LAG = 8

            def run(eng, body):
                pipeline(eng, 12, N, N + LAG, RING, body)

            def entry(eng, i, k, top):
                src = table[0:1, i, k:k + 1] if isinstance(i, int) else \
                    table[0:1, bass.ds(i, 1), k:k + 1].rearrange("p t k -> p (t k)")
                return eng.value_load(src, min_val=0, max_val=top)

            with nc.Block() as block:
                @block.sync
                def _(sp):
                    def body(s, ph):
                        i, b = s, ph % RING
                        if live(i, N):
                            first = entry(sp, i, 1, DUMP)
                            if past(i, RING):
                                sp.wait_ge(xgt_psum, i - RING + 1)
                            sp.dma_start(xg[:, b, :], xs_d[bass.ds(first, P), :]).then_inc(ld_xg[b], 16)
                        i, b = s - 8, ph % RING
                        if live(i, N):
                            sp.wait_ge(yo_done, i + 1)
                            sp.dma_start(at(ys_t, i), yo[:, b, :]).then_inc(st_y[b], 16)
                    run(sp, body)
                    for k in range(RING):
                        sp.wait_ge(st_y[k], 16 * N // RING)

                @block.tensor
                def _(pe):
                    def body(s, ph):
                        i, b = s - 3, (ph - 3) % 2
                        if live(i, N):
                            pe.wait_ge(ld_xg[(ph - 3) % RING], landed(i, RING, (ph - 3) % RING))
                            if past(i, 1):
                                pe.wait_ge(xgt_done, i)
                            for c in range(2):
                                m = nc.tensor.transpose(xgt_ps[:, c * P:(c + 1) * P],
                                                        xg[:, (ph - 3) % RING, c * P:(c + 1) * P], ident[:, :])
                            m.then_inc(xgt_psum, 1)
                        i, b = s - 4, ph % 2
                        if live(i, N):
                            e = entry(pe, i, 0, EXPERTS - 1)
                            w = up_w[:, bass.ds(e, 1), :].rearrange("p e n -> p (e n)")
                            pe.wait_ge(xgt_done, i + 1)
                            if past(i, 2):
                                pe.wait_ge(h_done, i - 1)
                            nc.tensor.matmul(gu_ps[b][:, 0:INNER], xgt[:, b, 0, :], w[:, 0:INNER],
                                             start=True, stop=True)
                            nc.tensor.matmul(gu_ps[b][:, INNER:2 * INNER], xgt[:, b, 1, :], w[:, INNER:2 * INNER],
                                             start=True, stop=True).then_inc(gu_psum, 1)
                        i, b = s - 5, (ph - 5) % 2
                        if live(i, N):
                            pe.wait_ge(h_done, i + 1)
                            if past(i, 1):
                                pe.wait_ge(ht_done, i)
                            for c in range(2):
                                m = nc.tensor.transpose(ht_ps[:, c * P:(c + 1) * P],
                                                        h[:, b, c * HALF:(c + 1) * HALF], ident[:, :])
                            m.then_inc(ht_psum, 1)
                        i, b = s - 6, ph % 2
                        if live(i, N):
                            pe.wait_ge(ht_done, i + 1)
                            if past(i, 1):
                                pe.wait_ge(rdt_done, i)
                            for c in range(2):
                                m = nc.tensor.matmul(rd_ps, rd_w[:, c, :], ht[:, b, c, :],
                                                     start=(c == 0), stop=(c == 1))
                            m.then_inc(rd_psum, 1)
                        i, b = s - 7, (ph - 7) % 2
                        if live(i, N):
                            e = entry(pe, i, 0, EXPERTS - 1)
                            w = down_w[:, bass.ds(e, 1), :].rearrange("p e n -> p (e n)")
                            pe.wait_ge(rdt_done, i + 1)
                            if past(i, 2):
                                pe.wait_ge(yo_done, i - 1)
                            nc.tensor.matmul(y_ps[b], rdt[:, b, :], w, start=True, stop=True).then_inc(ye_psum, 1)
                    run(pe, body)

                @block.scalar
                def _(act):
                    def body(s, ph):
                        i, b = s - 3, (ph - 3) % 2
                        if live(i, N):
                            act.wait_ge(xgt_psum, i + 1)
                            nc.scalar.activation(xgt[:, b, :, :].rearrange("p c t -> p (c t)"), xgt_ps, ACT.Copy)\
                                .then_inc(xgt_done, 1)
                        i, b = s - 4, ph % 2
                        if live(i, N):
                            act.wait_ge(gu_psum, i + 1)
                            nc.scalar.activation(gated[:, b, :], gu_ps[b][:, 0:INNER], ACT.Silu).then_inc(gated_done, 1)
                        i, b = s - 6, ph % 2
                        if live(i, N):
                            act.wait_ge(rd_psum, i + 1)
                            nc.scalar.activation(rdt[:, b, :], rd_ps, ACT.Copy).then_inc(rdt_done, 1)
                    run(act, body)

                @block.vector
                def _(dve):
                    def body(s, ph):
                        i, b = s - 4, ph % 2
                        if live(i, N):
                            dve.wait_ge(gated_done, i + 1)
                            nc.vector.tensor_tensor(h[:, b, :], gu_ps[b][:, INNER:2 * INNER], gated[:, b, :], ALU.mult)\
                                .then_inc(h_done, 1)
                        i, b = s - 5, (ph - 5) % 2
                        if live(i, N):
                            dve.wait_ge(ht_psum, i + 1)
                            nc.vector.tensor_copy(ht[:, b, :, :].rearrange("p c t -> p (c t)"), ht_ps)\
                                .then_inc(ht_done, 1)
                        i, b = s - 7, (ph - 7) % 2
                        if live(i, N):
                            dve.wait_ge(ye_psum, i + 1)
                            if past(i, RING):
                                dve.wait_ge(st_y[(ph - 7) % RING], landed(i, RING, (ph - 7) % RING) - 16)
                            nc.vector.tensor_copy(yo[:, (ph - 7) % RING, :], y_ps[b]).then_inc(yo_done, 1)
                    run(dve, body)

        with ExitStack() as cx:
            def fsb(name, shape, dt=F32):
                return cx.enter_context(nc.sbuf_tensor(name, shape, dt))
            x2t = fsb("x2t", [P, 2, CH, P])
            xr1 = fsb("xr1", [P, 2, DIM])
            rt = fsb("rt", [P, 2, 2, P])
            sg = fsb("sg", [P, 2, SCH, P])
            sh = fsb("sh", [P, 2, SCH, P])
            srt = fsb("srt", [P, 2, P])
            rows = fsb("rows", [P, 2, TOPK], I32)
            onehot = fsb("onehot", [P, 2, TOPK, EXPERTS])
            shifts = fsb("shifts", [P, 2, TOPK, EXPERTS])
            moved = fsb("moved", [P, 2, TOPK])
            wts = fsb("wts", [P, 2, TOPK])
            got = fsb("got", [P, 2, TOPK, DIM])
            acc = fsb("acc", [P, 2, TOPK + 1, DIM])
            fence = fsb("fence", [P, 2])
            rt_ps = bank03[:, 0, 0:2 * P]
            g_ps = bank03[:, 1, 0:SPAD]
            u_ps = bank03[:, 2, 0:SPAD]
            srt_ps = bank03[:, 3, 0:P]
            sy_ps = bank4[:, 0:DIM]
            ld_x2t, ld_x1, gathered, st_out = (
                [cx.enter_context(nc.semaphore(f"{n}{k}")) for k in range(2)]
                for n in ("ld_x2t", "ld_x1", "gathered", "st_out"))
            (rt_psum, rt_done, g_psum, u_psum, sg_done, sh_done2, srt_psum, srt_done, sy_psum, sum_done,
             rows_done, wts_done, fenced, onehot_done, shifts_done, moved_done) = (cx.enter_context(nc.semaphore(n)) for n in (
                 "rt_psum", "rt_done", "g_psum", "u_psum", "sg_done", "sh_done2", "srt_psum", "srt_done", "sy_psum",
                 "sum_done", "rows_done", "wts_done", "fenced", "onehot_done", "shifts_done", "moved_done"))
            out_t = a["out"].rearrange("(t p) d -> t p d", p=P)

            def run(eng, body):
                pipeline(eng, 6, TILES, TILES + 4, 2, body)

            with nc.Block() as block:
                @block.sync
                def _(sp):
                    def body(s, ph):
                        i, b = s, ph % 2
                        if live(i, TILES):
                            if past(i, 2):
                                sp.wait_ge(rt_psum, i - 1)
                            sp.dma_start(x2t[:, b, :, :].rearrange("p c t -> p (c t)"), at(xn2t_d, i))\
                                .then_inc(ld_x2t[b], 16)
                            if past(i, 2):
                                sp.wait_ge(sum_done, (TOPK + 1) * (i - 1))
                            sp.dma_start(xr1[:, b, :], at(x1_d, i)).then_inc(ld_x1[b], 16)
                        i, b = s - 3, (ph - 3) % 2
                        if live(i, TILES):
                            sp.wait_ge(sum_done, (TOPK + 1) * (i + 1))
                            sp.dma_start(at(out_t, i), acc[:, b, TOPK, :]).then_inc(st_out[b], 16)
                    run(sp, body)
                    for k in range(2):
                        sp.wait_ge(st_out[k], 16 * TILES // 2)

                @block.tensor
                def _(pe):
                    def body(s, ph):
                        i, b = s - 3, (ph - 3) % 2
                        if live(i, TILES):
                            pe.wait_ge(sh_done2, i + 1)
                            if past(i, 1):
                                pe.wait_ge(srt_done, i)
                            for c in range(SCH):
                                k = P if c < SCH - 1 else SLAST
                                m = nc.tensor.matmul(srt_ps, srd_w[0:k, c, :], sh[0:k, b, c, :],
                                                     start=(c == 0), stop=(c == SCH - 1))
                            m.then_inc(srt_psum, 1)
                        i, b = s - 1, (ph - 1) % 2
                        if live(i, TILES):
                            pe.wait_ge(ld_x2t[b], landed(i, 2, b))
                            if past(i, 1):
                                pe.wait_ge(rt_done, i)
                            for r in range(2):
                                for c in range(CH):
                                    m = nc.tensor.matmul(rt_ps[:, r * P:(r + 1) * P], srgu_w[:, c, r, :],
                                                         x2t[:, b, c, :], start=(c == 0), stop=(c == CH - 1))
                            m.then_inc(rt_psum, 1)
                        i, b = s - 2, ph % 2
                        if live(i, TILES):
                            pe.wait_ge(rt_done, i + 1)
                            if past(i, 1):
                                pe.wait_ge(sg_done, i)
                            for c in range(SCH):
                                m = nc.tensor.matmul(g_ps[:, c * P:(c + 1) * P], sup_w[:, 0, c * P:(c + 1) * P],
                                                     rt[:, b, 0, :], start=True, stop=True)
                            m.then_inc(g_psum, 1)
                            if past(i, 1):
                                pe.wait_ge(sh_done2, i)
                            for c in range(SCH):
                                m = nc.tensor.matmul(u_ps[:, c * P:(c + 1) * P], sup_w[:, 1, c * P:(c + 1) * P],
                                                     rt[:, b, 1, :], start=True, stop=True)
                            m.then_inc(u_psum, 1)
                        i, b = s - 3, (ph - 3) % 2
                        if live(i, TILES):
                            pe.wait_ge(srt_done, i + 1)
                            if past(i, 1):
                                pe.wait_ge(sum_done, (TOPK + 1) * (i - 1) + 1)
                            nc.tensor.matmul(sy_ps, srt[:, b, :], sdown_w[:, :], start=True, stop=True)\
                                .then_inc(sy_psum, 1)
                    run(pe, body)

                @block.scalar
                def _(act):
                    def body(s, ph):
                        i, b = s - 3, (ph - 3) % 2
                        if live(i, TILES):
                            act.wait_ge(srt_psum, i + 1)
                            nc.scalar.activation(srt[:, b, :], srt_ps, ACT.Copy).then_inc(srt_done, 1)
                        i, b = s - 1, (ph - 1) % 2
                        if live(i, TILES):
                            act.wait_ge(rt_psum, i + 1)
                            nc.scalar.activation(rt[:, b, :, :].rearrange("p c t -> p (c t)"), rt_ps, ACT.Copy)\
                                .then_inc(rt_done, 1)
                        i, b = s - 2, ph % 2
                        if live(i, TILES):
                            act.wait_ge(g_psum, i + 1)
                            nc.scalar.activation(sg[:, b, :, :].rearrange("p c t -> p (c t)"), g_ps, ACT.Silu)\
                                .then_inc(sg_done, 1)
                    run(act, body)

                @block.gpsimd
                def _(pool):
                    def body(s, ph):
                        i, b = s, ph % 2
                        if live(i, TILES):
                            pool.wait_ge(rows_done, i + 1)
                            if past(i, 2):
                                pool.wait_ge(sum_done, (TOPK + 1) * (i - 1))
                                pool.wait_ge(fenced, i - 1)
                            nc.gpsimd.tensor_tensor(fence[:, b:b + 1], ones[:, 0:1], ones[:, 0:1], ALU.mult)\
                                .then_inc(fenced, 1)
                            for k in range(TOPK):
                                nc.gpsimd.indirect_dma_start(
                                    got[:, b, k, :], None, ys_d, bass.IndirectOffsetOnAxis(rows[:, b, k:k + 1], 0))\
                                    .then_inc(gathered[b], 16)
                    run(pool, body)

                @block.vector
                def _(dve):
                    def body(s, ph):
                        i, b = s, ph % 2
                        if live(i, TILES):
                            if past(i, 2):
                                dve.wait_ge(gathered[b], landed(i, 2, b, 64) - 64)
                            shape = [P, TOPK, EXPERTS]
                            nc.vector.tensor_tensor(
                                onehot[:, b, :, :], eiota[:, :].unsqueeze(1).broadcast_to(shape),
                                col(experts, i).unsqueeze(2).broadcast_to(shape), ALU.is_equal).then_inc(onehot_done, 1)
                            dve.wait_ge(onehot_done, i + 1)
                            nc.vector.tensor_tensor(shifts[:, b, :, :], onehot[:, b, :, :],
                                                    shift[:, :].unsqueeze(1).broadcast_to(shape), ALU.mult)\
                                .then_inc(shifts_done, 1)
                            dve.wait_ge(shifts_done, i + 1)
                            nc.vector.tensor_reduce(moved[:, b, :], shifts[:, b, :, :], AX.X, ALU.add)\
                                .then_inc(moved_done, 1)
                            dve.wait_ge(moved_done, i + 1)
                            nc.vector.tensor_tensor(rows[:, b, :], moved[:, b, :], col(slots, i), ALU.add)\
                                .then_inc(rows_done, 1)
                        i, b = s - 2, ph % 2
                        if live(i, TILES):
                            dve.wait_ge(sg_done, i + 1)
                            dve.wait_ge(u_psum, i + 1)
                            nc.vector.tensor_tensor(sh[:, b, :, :].rearrange("p c t -> p (c t)"), u_ps,
                                                    sg[:, b, :, :].rearrange("p c t -> p (c t)"), ALU.mult)\
                                .then_inc(sh_done2, 1)
                        i, b = s - 3, (ph - 3) % 2
                        if live(i, TILES):
                            dve.wait_ge(ld_x1[b], landed(i, 2, b))
                            dve.wait_ge(sy_psum, i + 1)
                            if past(i, 2):
                                dve.wait_ge(st_out[b], landed(i, 2, b) - 16)
                            nc.vector.tensor_scalar(wts[:, b, :], col(weights, i), 1.0, None, ALU.mult)\
                                .then_inc(wts_done, 1)
                            nc.vector.tensor_tensor(acc[:, b, 0, :], sy_ps, xr1[:, b, :], ALU.add).then_inc(sum_done, 1)
                            dve.wait_ge(gathered[b], landed(i, 2, b, 64))
                            dve.wait_ge(wts_done, i + 1)
                            for k in range(TOPK):
                                dve.wait_ge(sum_done, (TOPK + 1) * i + k + 1)
                                nc.vector.scalar_tensor_tensor(
                                    out=acc[:, b, k + 1, :], in0=got[:, b, k, :], scalar=wts[:, b, k:k + 1],
                                    in1=acc[:, b, k, :], op0=ALU.mult, op1=ALU.add).then_inc(sum_done, 1)
                    run(dve, body)


def kernel(**inputs):
    import concourse.bacc as bacc
    from concourse.bass_utils import run_bass_kernel_spmd

    get = {n.replace("L0_", ""): np.asarray(v) for n, v in inputs.items()}

    def rows(w):
        return w.T.reshape(-1, P, w.shape[0]).transpose(1, 0, 2)

    def feature(v):
        return v.reshape(CH, P).T

    x = get["x"].reshape(TOKENS, DIM)
    ctx = get["ctx_2048"].reshape(TOKENS, DIM)
    wv = get["xattn_w_v_img"].reshape(PAIRS, 2, HD, DIM).transpose(1, 0, 2, 3).reshape(DIM, DIM)
    t = lambda n: get["ffn_" + n].transpose(0, 2, 1)
    index = np.arange(P)
    arrays = {
        "x": x,
        "ctxt": ctx.T.reshape(CH, P, TOKENS).transpose(1, 0, 2),
        "ident": np.eye(P, dtype=np.float32),
        "tri": (index[:, None] < index[None, :]).astype(np.float32),
        "ones": np.ones((P, P), np.float32),
        "headmask": ((index[:, None] // HD) % GH == np.arange(GH)[None, :]).astype(np.float32),
        "eiota": np.tile(np.arange(EXPERTS, dtype=np.float32), (P, 1)),
        "ebase": np.tile(np.arange(EXPERTS, dtype=np.float32) * CAP, (P, 1)),
        "tileno": np.arange(ETILES, dtype=np.float32)[None, :],
        "wq": rows(get["xattn_w_q"]),
        "wkv": np.concatenate([rows(get["xattn_w_k_img"]), rows(wv)], axis=2),
        "wo": rows(get["xattn_w_o"]),
        "bq": get["xattn_b_q"][None], "bk": get["xattn_b_k_img"][None], "bo": get["xattn_b_o"][None],
        "bv": feature(get["xattn_b_v_img"]),
        "gq": feature(get["xattn_g_q"]), "gk": feature(get["xattn_g_k_img"]),
        "gate": rows(get["ffn_gate_w"]),
        "rgu": np.concatenate([rows(get["ffn_Rg"]), rows(get["ffn_Ru"])], axis=2),
        "rd": get["ffn_Rd"].T.reshape(2, HALF, RANK).transpose(1, 0, 2),
        "srgu": np.stack([rows(get["ffn_s_Rg"]), rows(get["ffn_s_Ru"])], axis=2),
        "srd": get["ffn_s_Rd"].T,
        "raw": np.concatenate([get["ffn_Ug"], t("Cg"), get["ffn_Uu"], t("Cu"), get["ffn_Ud"], t("Cd")], axis=2),
        "sraw": np.concatenate([get["ffn_s_Ug"], get["ffn_s_Cg"].T, get["ffn_s_Uu"], get["ffn_s_Cu"].T,
                                get["ffn_s_Ud"], get["ffn_s_Cd"].T], axis=1),
    }
    nc = bacc.Bacc("TRN2", target_bir_lowering=False, num_devices=1)
    feed, aps = {}, {}
    for name, v in arrays.items():
        feed["in_" + name] = np.ascontiguousarray(v)
        aps[name] = nc.dram_tensor("in_" + name, v.shape, F32, kind="ExternalInput").ap()
    aps["out"] = nc.dram_tensor("out", [TOKENS, DIM], F32, kind="ExternalOutput").ap()
    build(nc, aps)
    r = run_bass_kernel_spmd(nc, [feed], core_ids=[0])
    return r.results[0]["out"].reshape(BATCH, SEQ, DIM)
```

```python
from contextlib import ExitStack

import numpy as np

import concourse.bass as bass
from concourse import mybir

F32 = mybir.dt.float32
I32 = mybir.dt.int32
U32 = mybir.dt.uint32
ALU = mybir.AluOpType
ACT = mybir.ActivationFunctionType
AX = mybir.AxisListType

P = 128
BATCH, SEQ, DIM = 64, 64, 256
TOKENS = BATCH * SEQ
TILES = TOKENS // P
CH = DIM // P
HEADS, HD = 16, 16
PAIRS = HEADS // 2
GROUPS, GH = 2, 4
EXPERTS, TOPK = 32, 4
RANK = 128
INNER = 176
HALF = INNER // 2
SHARED = 2 * INNER
SCH = 3
SLAST = SHARED - 2 * P
SPAD = SCH * P
CAP = TOKENS + P
ETILES = (TOKENS * TOPK + EXPERTS * (P - 1)) // P + 1
DUMP = EXPERTS * CAP
LN_EPS, RMS_EPS = 1e-5, 1e-6
RAW = 2 * (RANK + INNER) + RANK + DIM


def live(i, n):
    return not isinstance(i, int) or 0 <= i < n


def past(i, k):
    return not isinstance(i, int) or i >= k


def landed(i, ring, slot, per=16):
    return (i - slot) * (per // ring) + per


def pipeline(eng, lead, stop, total, unroll, body):
    for s in range(lead):
        body(s, s)
    with eng.Fori(0, (stop - lead) // unroll) as g:
        for u in range(unroll):
            body(g * unroll + (lead + u), lead + u)
    for s in range(stop, total):
        body(s, s)


def at(ap, i):
    return ap[i] if isinstance(i, int) else ap[bass.ds(i, 1), :, :].rearrange("t p m -> (t p) m")


def col(tile, i):
    return tile[:, i, :] if isinstance(i, int) else tile[:, bass.ds(i, 1), :].rearrange("p t m -> p (t m)")


def build(nc, a):
    ctx = ExitStack()
    with ctx:
        def sb(name, shape, dt=F32):
            return ctx.enter_context(nc.sbuf_tensor(name, shape, dt))

        def ps(name, shape):
            return ctx.enter_context(nc.psum_tensor(name, shape, F32))

        def sem(name):
            return ctx.enter_context(nc.semaphore(name))

        def sems(name, n=2):
            return [sem(f"{name}{k}") for k in range(n)]

        x1_d = nc.dram_tensor("x1_d", [TILES, P, DIM], F32, kind="Internal").ap()
        xn2t_d = nc.dram_tensor("xn2t_d", [TILES, P, DIM], F32, kind="Internal").ap()
        xs_d = nc.dram_tensor("xs_d", [DUMP + P, DIM], F32, kind="Internal").ap()
        ys_d = nc.dram_tensor("ys_d", [ETILES * P, DIM], F32, kind="Internal").ap()

        ident = sb("ident", [P, P])
        tri = sb("tri", [P, P])
        ones = sb("ones", [P, P])
        headmask = sb("headmask", [P, GH])
        eiota = sb("eiota", [P, EXPERTS])
        ebase = sb("ebase", [P, EXPERTS])
        mhalf = sb("mhalf", [P, 2])
        wq = sb("wq", [P, CH, DIM])
        wkv = sb("wkv", [P, CH, 2 * DIM])
        wo = sb("wo", [P, CH, DIM])
        bq = sb("bq", [P, DIM])
        bk = sb("bk", [P, DIM])
        bo = sb("bo", [P, DIM])
        bv = sb("bv", [P, CH])
        gq = sb("gq", [P, CH])
        gk = sb("gk", [P, CH])
        gqk = sb("gqk", [P, CH])
        gate = sb("gate", [P, CH, EXPERTS])
        rgu_w = sb("rgu_w", [P, CH, 2 * RANK])
        rd_w = sb("rd_w", [HALF, 2, RANK])
        srgu_w = sb("srgu_w", [P, CH, 2, RANK])
        srd_w = sb("srd_w", [P, SCH, RANK])
        up_w = sb("up_w", [P, EXPERTS, 2 * INNER])
        down_w = sb("down_w", [P, EXPERTS, DIM])
        sup_w = sb("sup_w", [P, 2, SPAD])
        sdown_w = sb("sdown_w", [P, DIM])
        slots = sb("slots", [P, TILES, TOPK])
        experts = sb("experts", [P, TILES, TOPK])
        weights = sb("weights", [P, TILES, TOPK])

        bank03 = ps("bank03", [P, 4, 512])
        bank4, bank5, bank6, bank7 = (ps(f"bank{k}", [P, 512]) for k in range(4, 8))

        ld_const = sem("ld_const")
        consts = [(ident, "ident"), (tri, "tri"), (ones, "ones"), (headmask, "headmask"), (eiota, "eiota"),
                  (ebase, "ebase"), (wq, "wq"), (wkv, "wkv"), (wo, "wo"), (bv, "bv"), (gq, "gq"), (gk, "gk"),
                  (gate, "gate"), (rgu_w, "rgu"), (rd_w, "rd"), (srgu_w, "srgu")]
        bcasts = [(bq, "bq"), (bk, "bk"), (bo, "bo")]
        N_CONST = 16 * (len(consts) + len(bcasts) + 2)

        with ExitStack() as cx:
            def csb(name, shape, dt=F32):
                return cx.enter_context(nc.sbuf_tensor(name, shape, dt))
            sraw = csb("sraw", [P, 3 * RANK + 2 * SHARED + DIM])
            bv_cols = csb("bv_cols", [P, CH, P])
            s_ug, s_cg, s_uu, s_cu = 0, RANK, RANK + SHARED, 2 * RANK + SHARED
            s_ud, s_cd = 2 * (RANK + SHARED), 2 * (RANK + SHARED) + RANK
            ld_sraw = cx.enter_context(nc.semaphore("ld_sraw"))
            set_up = cx.enter_context(nc.semaphore("set_up"))
            sh_psum = cx.enter_context(nc.semaphore("sh_psum"))
            sh_done = cx.enter_context(nc.semaphore("sh_done"))

            with nc.Block() as block:
                @block.sync
                def _(sp):
                    for tile, name in consts:
                        sp.dma_start(tile[:], a[name]).then_inc(ld_const, 16)
                    for tile, name in bcasts:
                        sp.dma_start(tile[:], a[name].broadcast_to([P, DIM])).then_inc(ld_const, 16)
                    sp.dma_start(srd_w[:, 0:2, :], a["srd"][0:2 * P].rearrange("(c p) r -> p c r", p=P))\
                        .then_inc(ld_const, 16)
                    sp.dma_start(srd_w[0:SLAST, 2, :], a["srd"][2 * P:SHARED]).then_inc(ld_const, 16)
                    sp.dma_start(sraw[:, :], a["sraw"]).then_inc(ld_sraw, 16)

                @block.tensor
                def _(pe):
                    pe.wait_ge(ld_sraw, 16)
                    nc.tensor.matmul(bank4[:, 0:SHARED], sraw[:, s_ug:s_ug + RANK], sraw[:, s_cg:s_cg + SHARED],
                                     start=True, stop=True)
                    nc.tensor.matmul(bank5[:, 0:SHARED], sraw[:, s_uu:s_uu + RANK], sraw[:, s_cu:s_cu + SHARED],
                                     start=True, stop=True)
                    nc.tensor.matmul(bank6[:, 0:DIM], sraw[:, s_ud:s_ud + RANK], sraw[:, s_cd:s_cd + DIM],
                                     start=True, stop=True)
                    pe.wait_ge(ld_const, N_CONST)
                    pe.wait_ge(set_up, 4)
                    for c in range(CH):
                        m = nc.tensor.matmul(bank7[:, 0:DIM], bv_cols[:, c, :], wo[:, c, :],
                                             start=(c == 0), stop=(c == CH - 1))
                    m.then_inc(sh_psum, 1)

                @block.vector
                def _(dve):
                    nc.vector.memset(mhalf[:, :], -0.5)
                    nc.vector.memset(sup_w[:, :, SHARED:SPAD], 0.0)
                    dve.wait_ge(ld_const, N_CONST)
                    nc.vector.tensor_tensor(gqk[:, :], gq[:, :], gk[:, :], ALU.mult).then_inc(set_up, 1)
                    dve.wait_ge(set_up, 1)
                    nc.vector.tensor_scalar(gqk[:, :], gqk[:, :], float(HD) ** -0.5, None, ALU.mult)\
                        .then_inc(set_up, 1)
                    for c in range(CH):
                        nc.vector.tensor_scalar(bv_cols[:, c, :], ones[:, :], bv[:, c:c + 1], None, ALU.mult)\
                            .then_inc(set_up, 1)
                    dve.wait_ge(sh_psum, 1)
                    nc.vector.tensor_copy(sup_w[:, 0, 0:SHARED], bank4[:, 0:SHARED])
                    nc.vector.tensor_copy(sup_w[:, 1, 0:SHARED], bank5[:, 0:SHARED])
                    nc.vector.tensor_copy(sdown_w[:, :], bank6[:, 0:DIM])
                    nc.vector.tensor_tensor(bo[:, :], bank7[:, 0:DIM], bo[:, :], ALU.add).then_inc(sh_done, 1)

                    dve.wait_ge(sh_done, 1)

        with ExitStack() as cx:
            def asb(name, shape, dt=F32):
                return cx.enter_context(nc.sbuf_tensor(name, shape, dt))

            def asem(name):
                return cx.enter_context(nc.semaphore(name))
            assert EXPERTS == TILES
            raw = asb("raw", [P, 2, RAW])
            o_ug, o_cg, o_uu, o_cu = 0, RANK, RANK + INNER, 2 * RANK + INNER
            o_ud, o_cd = 2 * (RANK + INNER), 2 * (RANK + INNER) + RANK
            xin = asb("xin", [P, 2, DIM])
            ctxt = asb("ctxt", [P, 2, CH, P])
            xres = asb("xres", [P, 2, DIM])
            stats = asb("stats", [P, 2, 6])
            mean1 = asb("mean1", [P, 2, 2])
            rstd1 = asb("rstd1", [P, 2, 1])
            xn1 = asb("xn1", [P, 2, DIM])
            xn1t = asb("xn1t", [P, 2, CH, P])
            qb = asb("qb", [P, 2, DIM])
            kb = asb("kb", [P, 2, DIM])
            squares = asb("squares", [P, DIM])
            ssq = asb("ssq", [P, 2, 2])
            rqk = asb("rqk", [P, 2, 2])
            v17 = asb("v17", [P, 2, 2, PAIRS, HD + 1])
            v2 = asb("v2", [P, 2, 2, 2, PAIRS, HD + 1])
            qt = asb("qt", [P, 2, CH, P])
            ktm = asb("ktm", [P, 2, 2 * CH, GH, SEQ])
            smax = asb("smax", [P, 2, GROUPS, CH * GH])
            prob = asb("prob", [P, 2, PAIRS, P])
            probt = asb("probt", [P, 2, PAIRS, P])
            rsum = asb("rsum", [P, 2, PAIRS, 2])
            on = asb("on", [P, 2, DIM])
            ot = asb("ot", [P, 2, CH, P])
            xrb = asb("xrb", [P, 2, DIM])
            x1 = asb("x1", [P, 2, DIM])
            stats2 = asb("stats2", [P, 2, 6])
            mean2 = asb("mean2", [P, 2, 2])
            rstd2 = asb("rstd2", [P, 2, 1])
            xn2 = asb("xn2", [P, 2, DIM])
            xn2t = asb("xn2t", [P, 2, CH, P])
            rgu = asb("rgu", [P, 2, DIM])
            top8 = asb("top8", [P, 2, 8])
            logits = asb("logits", [P, 2, EXPERTS])
            ntop = asb("ntop", [P, 2, 1])
            top8i = asb("top8i", [P, 2, 8], U32)
            topif = asb("topif", [P, 2, TOPK])
            egate = asb("egate", [P, 2, EXPERTS])
            etop = asb("etop", [P, 2, TOPK])
            zsum = asb("zsum", [P, 2, 2])
            wden = asb("wden", [P, 2, 2])
            chosen = asb("chosen", [P, 2, TOPK, EXPERTS])
            member = asb("member", [P, 2, EXPERTS])
            members = asb("members", [P, EXPERTS])
            rowof = asb("rowof", [P, 2, EXPERTS])
            picked = asb("picked", [P, 2, TOPK, EXPERTS])
            slotf = asb("slotf", [P, 2, TOPK])
            sloti = asb("sloti", [P, 2, TOPK], I32)

            s_ps = bank03[:, 0:GROUPS, :]
            kv_ps = bank03[:, 2, :]
            qkt_ps = bank03[:, 3, :].rearrange("p (c t) -> p c t", c=2 * CH)
            y_ps = bank03[:, 3, 0:DIM]
            pt_ps = bank4[:, :].rearrange("p (c t) -> p c t", c=4)
            r_ps = bank5[:, 480:480 + EXPERTS]
            l_ps = bank5[:, 448:448 + EXPERTS]
            o_ps = bank5[:, 0:PAIRS * 2 * (HD + 1)].rearrange("p (g r d) -> p g r d", g=PAIRS, r=2)
            x2t_ps = bank6[:, 0:DIM]
            xnt_ps = bank7[:, 0:DIM].rearrange("p (c t) -> p c t", c=CH)
            q_ps = bank7[:, 0:DIM]
            up_ps = bank7[:, 0:2 * INNER]
            down_ps = bank6[:, 0:DIM]

            ld_x, ld_ctx, ld_xres, v2_in, st_x1, st_x2t, sc_out = (
                [asem(f"{n}{k}") for k in range(2)]
                for n in ("ld_x", "ld_ctx", "ld_xres", "v2_in", "st_x1", "st_x2t", "sc_out"))
            ld_raw = [asem(f"ld_raw{k}") for k in range(2)]
            down_psum, down_kept, up_psum, up_kept = (asem(n) for n in ("down_psum", "down_kept", "up_psum", "up_kept"))
            preset = asem("preset")
            ln1_st, ln1_mv, ln1_ve, ln1_rstd, xn1_done = (asem(n) for n in ("ln1_st", "ln1_mv", "ln1_ve", "ln1_rstd", "xn1_done"))
            xnt_psum, xnt_done, q_psum, kv_psum = (asem(n) for n in ("xnt_psum", "xnt_done", "q_psum", "kv_psum"))
            qb_done, kb_done, v_done, ssq_done, msq_done, rqk_done, kn_done = (
                asem(n) for n in ("qb_done", "kb_done", "v_done", "ssq_done", "msq_done", "rqk_done", "kn_done"))
            qkt_psum, qt_done, ktm_done, s_psum, smax_done, ssub_done, prob_done = (
                asem(n) for n in ("qkt_psum", "qt_done", "ktm_done", "s_psum", "smax_done", "ssub_done", "prob_done"))
            pt_psum, pt0_done, pt1_done, o_psum, rsum_done, on_done, ot_psum, ot_done, y_psum, xrb_done, x1_done = (
                asem(n) for n in ("pt_psum", "pt0_done", "pt1_done", "o_psum", "rsum_done", "on_done", "ot_psum", "ot_done",
                                  "y_psum", "xrb_done", "x1_done"))
            ln2_st, ln2_mv, ln2_ve, ln2_rstd, xn2_done, x2t_psum, x2t_done = (
                asem(n) for n in ("ln2_st", "ln2_mv", "ln2_ve", "ln2_rstd", "xn2_done", "x2t_psum", "x2t_done"))
            l_psum, rgu_psum, rgu_done, logits_done, top_done, ntop_done, topi_done, topif_done, gexp_done, wden_done, wt_done = (
                asem(n) for n in ("l_psum", "rgu_psum", "rgu_done", "logits_done", "top_done", "ntop_done", "topi_done",
                                  "topif_done", "gexp_done", "wden_done", "wt_done"))
            chosen_done, member_done, r_psum, rowof_done, picked_done, slotf_done, sloti_done, members_done = (
                asem(n) for n in ("chosen_done", "member_done", "r_psum", "rowof_done", "picked_done",
                                  "slotf_done", "sloti_done", "members_done"))
            STEPS = TILES + 6
            LEAD = 8

            x_t = a["x"].rearrange("(t p) d -> t p d", p=P)
            ctx_t = a["ctxt"].rearrange("p c (t k) -> t p c k", k=P)

            def run(eng, body):
                pipeline(eng, LEAD, TILES, STEPS, 2, body)

            with nc.Block() as block:
                @block.sync
                def _(sp):
                    def body(s, ph):
                        i, b = s, ph % 2
                        if live(i, TILES):
                            if past(i, 2):
                                sp.wait_ge(xn1_done, i - 1)
                            sp.dma_start(xin[:, b, :], at(x_t, i)).then_inc(ld_x[b], 16)
                            if past(i, 2):
                                sp.wait_ge(kv_psum, i - 1)
                            src = ctx_t[i] if isinstance(i, int) else \
                                ctx_t[bass.ds(i, 1), :, :, :].rearrange("t p c k -> (t p) c k")
                            sp.dma_start(ctxt[:, b, :, :], src).then_inc(ld_ctx[b], 16)
                        i, b = s - 2, ph % 2
                        if live(i, TILES):
                            if past(i, 2):
                                sp.wait_ge(xrb_done, i - 1)
                            sp.dma_start(xres[:, b, :], at(x_t, i)).then_inc(ld_xres[b], 16)
                        i, b = s - 4, ph % 2
                        if live(i, TILES):
                            sp.wait_ge(x1_done, i + 1)
                            sp.dma_start(at(x1_d, i), x1[:, b, :]).then_inc(st_x1[b], 16)
                        i, b = s - 2, ph % 2
                        if live(i, TILES):
                            sp.wait_ge(v_done, i + 1)
                            if past(i, 2):
                                sp.wait_ge(o_psum, i - 1)
                            for n in range(2):
                                for r in range(2):
                                    sp.dma_start(v2[SEQ * r:SEQ * (r + 1), b, n, r, :, :],
                                                 v17[SEQ * n:SEQ * (n + 1), b, r, :, :]).then_inc(v2_in[b], 16)
                        i, b = s - 4, ph % 2
                        if live(i, TILES):
                            sp.wait_ge(x2t_done, i + 1)
                            sp.dma_start(at(xn2t_d, i), xn2t[:, b, :, :].rearrange("p c t -> p (c t)"))\
                                .then_inc(st_x2t[b], 16)
                        e, b = s, ph % 2
                        if live(e, EXPERTS):
                            if past(e, 2):
                                sp.wait_ge(up_psum, e - 1)
                            sp.dma_start(raw[:, b, :], at(a["raw"], e)).then_inc(ld_raw[b], 16)
                    run(sp, body)
                    for k in range(2):
                        sp.wait_ge(st_x1[k], 16 * TILES // 2)
                        sp.wait_ge(st_x2t[k], 16 * TILES // 2)

                @block.tensor
                def _(pe):
                    def rank(s, ph):
                        i, b = s - 5, (ph - 5) % 2
                        if not live(i, TILES):
                            return
                        if live(s - 3, TILES):
                            pe.wait_ge(on_done, s - 2)
                        pe.wait_ge(member_done, i + 1)
                        pe.wait_ge(members_done, i + 1)
                        nc.tensor.matmul(r_ps, tri[:, :], member[:, b, :], start=True, stop=False)
                        nc.tensor.matmul(r_ps, ones[:, :], members[:, :], start=False, stop=True).then_inc(r_psum, 1)

                    def p_turn(s, ph, r):
                        i, b = s - 3, (ph - 3) % 2
                        if not live(i, TILES):
                            return
                        if r == 0:
                            pe.wait_ge(prob_done, i + 1)
                            if past(i, 1):
                                pe.wait_ge(ot_done, i)
                        else:
                            pe.wait_ge(pt0_done, i + 1)
                        for k in range(4):
                            blk = 4 * r + k
                            m = nc.tensor.transpose(pt_ps[:, k, :], prob[:, b, blk, :], ident[:, :])
                        m.then_inc(pt_psum, 1)

                    def p_times_v(s, ph):
                        i, b = s - 3, (ph - 3) % 2
                        if not live(i, TILES):
                            return
                        pe.wait_ge(pt1_done, i + 1)
                        if live(s - 5, TILES):
                            pe.wait_ge(logits_done, s - 4)
                        if live(s - 6, TILES):
                            pe.wait_ge(rowof_done, s - 5)
                        pe.wait_ge(v2_in[b], landed(i, 2, b, 64))
                        for blk in range(PAIRS):
                            group, c, hp = blk // 4, blk // 2 % 2, blk % 2
                            pair = PAIRS // CH * c + GH // 2 * group + hp
                            for n in range(2):
                                m = nc.tensor.matmul(o_ps[SEQ * n:SEQ * (n + 1), pair, :, :],
                                                     probt[:, b, blk, SEQ * n:SEQ * (n + 1)],
                                                     v2[:, b, n, :, pair, :], start=True, stop=True)
                        m.then_inc(o_psum, 1)

                    def x_turn(s, ph):
                        i, b = s - 1, (ph - 1) % 2
                        if not live(i, TILES):
                            return
                        pe.wait_ge(xn1_done, i + 1)
                        if live(s - 2, EXPERTS):
                            pe.wait_ge(up_kept, s - 1)
                        for c in range(CH):
                            m = nc.tensor.transpose(xnt_ps[:, c, :], xn1[:, b, c * P:(c + 1) * P], ident[:, :])
                        m.then_inc(xnt_psum, 1)

                    def q_in(s, ph):
                        i, b = s - 1, (ph - 1) % 2
                        if not live(i, TILES):
                            return
                        pe.wait_ge(xnt_done, i + 1)
                        for c in range(CH):
                            m = nc.tensor.matmul(q_ps, xn1t[:, b, c, :], wq[:, c, :], start=(c == 0), stop=(c == CH - 1))
                        m.then_inc(q_psum, 1)

                    def kv_in(s, ph):
                        i, b = s - 1, (ph - 1) % 2
                        if not live(i, TILES):
                            return
                        if past(i, 1):
                            pe.wait_ge(kb_done, i)
                            pe.wait_ge(v_done, i)
                        pe.wait_ge(ld_ctx[b], landed(i, 2, b))
                        for c in range(CH):
                            m = nc.tensor.matmul(kv_ps, ctxt[:, b, c, :], wkv[:, c, :], start=(c == 0), stop=(c == CH - 1))
                        m.then_inc(kv_psum, 1)

                    def qk_turn(s, ph):
                        i, b = s - 2, ph % 2
                        if not live(i, TILES):
                            return
                        pe.wait_ge(qb_done, i + 1)
                        pe.wait_ge(kn_done, i + 1)
                        if live(s - 4, TILES):
                            pe.wait_ge(x1_done, s - 3)
                        for c in range(CH):
                            nc.tensor.transpose(qkt_ps[:, c, :], qb[:, b, c * P:(c + 1) * P], ident[:, :])
                        for c in range(CH):
                            m = nc.tensor.transpose(qkt_ps[:, CH + c, :], kb[:, b, c * P:(c + 1) * P], ident[:, :])
                        m.then_inc(qkt_psum, 1)

                    def scores_ready(s, ph):
                        i = s - 2
                        if not live(i, TILES):
                            return
                        pe.wait_ge(ktm_done, i + 1)
                        if past(i, 1):
                            pe.wait_ge(ssub_done, i)

                    def scores(s, ph):
                        i, b = s - 2, ph % 2
                        if not live(i, TILES):
                            return
                        for c in range(CH):
                            for n in range(2):
                                for g in range(GROUPS):
                                    feats = slice(64 * g, 64 * (g + 1))
                                    m = nc.tensor.matmul(s_ps[SEQ * n:SEQ * (n + 1), g, c * 256:(c + 1) * 256],
                                                         qt[feats, b, c, SEQ * n:SEQ * (n + 1)],
                                                         ktm[feats, b, 2 * c + n, :, :], start=True, stop=True)
                        m.then_inc(s_psum, 1)

                    def x2_turn(s, ph):
                        i, b = s - 4, ph % 2
                        if not live(i, TILES):
                            return
                        pe.wait_ge(xn2_done, i + 1)
                        if past(i, 1):
                            pe.wait_ge(rgu_done, i)
                        if live(s - 1, EXPERTS):
                            pe.wait_ge(down_kept, s)
                        for c in range(CH):
                            m = nc.tensor.transpose(x2t_ps[:, c * P:(c + 1) * P], xn2[:, b, c * P:(c + 1) * P], ident[:, :])
                        m.then_inc(x2t_psum, 1)

                    def rgu_in(s, ph):
                        i, b = s - 4, ph % 2
                        if not live(i, TILES):
                            return
                        pe.wait_ge(x2t_done, i + 1)
                        for c in range(CH):
                            m = nc.tensor.matmul(x2t_ps, xn2t[:, b, c, :], rgu_w[:, c, :], start=(c == 0), stop=(c == CH - 1))
                        m.then_inc(rgu_psum, 1)

                    def gate_in(s, ph):
                        i, b = s - 4, ph % 2
                        if not live(i, TILES):
                            return
                        if live(s - 3, TILES):
                            pe.wait_ge(on_done, s - 2)
                        for c in range(CH):
                            m = nc.tensor.matmul(l_ps, xn2t[:, b, c, :], gate[:, c, :], start=(c == 0), stop=(c == CH - 1))
                        m.then_inc(l_psum, 1)

                    def o_turn(s, ph):
                        i, b = s - 3, (ph - 3) % 2
                        if not live(i, TILES):
                            return
                        pe.wait_ge(on_done, i + 1)
                        for c in range(CH):
                            m = nc.tensor.transpose(pt_ps[:, c, :], on[:, b, c * P:(c + 1) * P], ident[:, :])
                        m.then_inc(ot_psum, 1)

                    def project(s, ph):
                        i, b = s - 3, (ph - 3) % 2
                        if not live(i, TILES):
                            return
                        pe.wait_ge(ot_done, i + 1)
                        if live(s - 2, TILES):
                            pe.wait_ge(ktm_done, s - 1)
                        for c in range(CH):
                            m = nc.tensor.matmul(y_ps, ot[:, b, c, :], wo[:, c, :], start=(c == 0), stop=(c == CH - 1))
                        m.then_inc(y_psum, 1)

                    def down_product(s, ph):
                        e, b = s - 1, (ph - 1) % 2
                        if not live(e, EXPERTS):
                            return
                        if live(s - 5, TILES):
                            pe.wait_ge(rgu_done, s - 4)
                        pe.wait_ge(ld_raw[b], landed(e, 2, b))
                        nc.tensor.matmul(down_ps, raw[:, b, o_ud:o_ud + RANK], raw[:, b, o_cd:o_cd + DIM],
                                         start=True, stop=True).then_inc(down_psum, 1)

                    def up_products(s, ph):
                        e, b = s - 1, (ph - 1) % 2
                        if not live(e, EXPERTS):
                            return
                        if live(s - 1, TILES):
                            pe.wait_ge(qb_done, s)
                        nc.tensor.matmul(up_ps[:, 0:INNER], raw[:, b, o_ug:o_ug + RANK],
                                         raw[:, b, o_cg:o_cg + INNER], start=True, stop=True)
                        nc.tensor.matmul(up_ps[:, INNER:2 * INNER], raw[:, b, o_uu:o_uu + RANK],
                                         raw[:, b, o_cu:o_cu + INNER], start=True, stop=True).then_inc(up_psum, 1)

                    def body(s, ph):
                        x_turn(s, ph)
                        p_turn(s, ph, 0)
                        qk_turn(s, ph)
                        q_in(s, ph)
                        down_product(s, ph)
                        p_turn(s, ph, 1)
                        kv_in(s, ph)
                        scores_ready(s, ph)
                        x2_turn(s, ph)
                        scores(s, ph)
                        p_times_v(s, ph)
                        rgu_in(s, ph)
                        up_products(s, ph)
                        o_turn(s, ph)
                        rank(s, ph)
                        gate_in(s, ph)
                        project(s, ph)
                    run(pe, body)

                @block.scalar
                def _(act):
                    act.wait_ge(preset, 2)

                    def p_keep(s, ph, r, done):
                        i, b = s - 3, (ph - 3) % 2
                        if not live(i, TILES):
                            return
                        act.wait_ge(pt_psum, 2 * i + r + 1)
                        nc.scalar.activation(probt[:, b, 4 * r:4 * r + 4, :], pt_ps, ACT.Copy).then_inc(done, 1)

                    def body(s, ph):
                        i, b = s - 1, (ph - 1) % 2
                        if live(i, TILES):
                            act.wait_ge(xnt_psum, i + 1)
                            nc.scalar.activation(xn1t[:, b, :, :], xnt_ps, ACT.Copy).then_inc(xnt_done, 1)
                        p_keep(s, ph, 0, pt0_done)
                        i, b = s - 2, ph % 2
                        if live(i, TILES):
                            act.wait_ge(qkt_psum, i + 1)
                            for c in range(CH):
                                nc.scalar.activation(qt[:, b, c, :], qkt_ps[:, c, :], ACT.Copy,
                                                     scale=gqk[:, c:c + 1])
                            kt = qkt_ps[:, CH:2 * CH, :].rearrange("p c (n k) -> p (c n) k", n=2)
                            for g in range(GH):
                                m = nc.scalar.activation(ktm[:, b, :, g, :], kt, ACT.Copy, scale=headmask[:, g:g + 1])
                            m.then_inc(ktm_done, 1)
                        e = s - 1
                        if live(e, EXPERTS):
                            act.wait_ge(down_psum, e + 1)
                        p_keep(s, ph, 1, pt1_done)
                        if live(e, EXPERTS):
                            nc.scalar.activation(col(down_w, e), down_ps, ACT.Copy).then_inc(down_kept, 1)
                        i, b = s - 4, ph % 2
                        if live(i, TILES):
                            act.wait_ge(x2t_psum, i + 1)
                            if past(i, 2):
                                act.wait_ge(st_x2t[b], landed(i, 2, b) - 16)
                            nc.scalar.activation(xn2t[:, b, :, :].rearrange("p c t -> p (c t)"), x2t_ps,
                                                 ACT.Copy).then_inc(x2t_done, 1)
                        i, b = s - 1, (ph - 1) % 2
                        if live(i, TILES):
                            act.wait_ge(qb_done, i + 1)
                            if past(i, 1):
                                act.wait_ge(ssq_done, 2 * i)
                            nc.scalar.activation(squares[:, :], qb[:, b, :], ACT.Square,
                                                 accum_out=ssq[:, b, 0:1]).then_inc(ssq_done, 1)
                            act.wait_ge(kb_done, i + 1)
                            act.wait_ge(ssq_done, 2 * i + 1)
                            nc.scalar.activation(squares[:, :], kb[:, b, :], ACT.Square,
                                                 accum_out=ssq[:, b, 1:2]).then_inc(ssq_done, 1)
                            if past(i, 2):
                                act.wait_ge(v2_in[b], landed(i, 2, b, 64) - 64)
                            nc.scalar.activation(
                                v17[:, b, :, :, 0:HD],
                                kv_ps[:, DIM:2 * DIM].rearrange("p (r g d) -> p r g d", r=2, g=PAIRS),
                                ACT.Copy).then_inc(v_done, 1)
                        e = s - 1
                        if live(e, EXPERTS):
                            act.wait_ge(up_psum, e + 1)
                        i, b = s - 3, (ph - 3) % 2
                        if live(i, TILES):
                            act.wait_ge(ot_psum, i + 1)
                            nc.scalar.activation(ot[:, b, :, :], pt_ps[:, 0:CH, :], ACT.Copy).then_inc(ot_done, 1)
                        if live(e, EXPERTS):
                            nc.scalar.activation(col(up_w, e), up_ps, ACT.Copy).then_inc(up_kept, 1)
                        i, b = s - 2, ph % 2
                        if live(i, TILES):
                            act.wait_ge(ssub_done, i + 1)
                            pb = prob[:, b, :, :].rearrange("p q k -> p (q k)")
                            nc.scalar.activation(pb, pb, ACT.Exp, scale=rqk[:, b, 0:1]).then_inc(prob_done, 1)
                        i, b = s - 4, ph % 2
                        if live(i, TILES):
                            act.wait_ge(rgu_psum, i + 1)
                            if past(i, 2):
                                act.wait_ge(sc_out[b], landed(i, 2, b, 64) - 64)
                            nc.scalar.activation(rgu[:, b, :], x2t_ps, ACT.Copy).then_inc(rgu_done, 1)
                            act.wait_ge(ntop_done, i + 1)
                            nc.scalar.activation(egate[:, b, :], logits[:, b, :], ACT.Exp, bias=ntop[:, b, :],
                                                 accum_out=zsum[:, b, 0:1]).then_inc(gexp_done, 1)
                            nc.scalar.activation(etop[:, b, :], top8[:, b, 0:TOPK], ACT.Exp, bias=ntop[:, b, :],
                                                 accum_out=zsum[:, b, 1:2]).then_inc(gexp_done, 1)
                    run(act, body)

                @block.gpsimd
                def _(pool):
                    def body(s, ph):
                        i, b = s - 6, ph % 2
                        if live(i, TILES):
                            pool.wait_ge(rgu_done, i + 1)
                            pool.wait_ge(sloti_done, i + 1)
                        i, b = s - 3, (ph - 3) % 2
                        if live(i, TILES):
                            if past(i, 2):
                                pool.wait_ge(x1_done, i - 1)
                            pool.wait_ge(ld_xres[b], landed(i, 2, b))
                            nc.gpsimd.tensor_tensor(xrb[:, b, :], xres[:, b, :], bo[:, :], ALU.add).then_inc(xrb_done, 1)
                        i, b = s - 6, ph % 2
                        if live(i, TILES):
                            for k in range(TOPK):
                                nc.gpsimd.indirect_dma_start(
                                    xs_d, bass.IndirectOffsetOnAxis(sloti[:, b, k:k + 1], 0), rgu[:, b, :], None)\
                                    .then_inc(sc_out[b], 16)
                        i, b = s, ph % 2
                        if live(i, TILES):
                            pool.wait_ge(preset, 2)
                            pool.wait_ge(ln1_ve, i + 1)
                            nc.gpsimd.tensor_tensor(rstd1[:, b, :], mean1[:, b, 1:2], mhalf[:, 0:1], ALU.pow)\
                                .then_inc(ln1_rstd, 1)
                        i, b = s - 1, (ph - 1) % 2
                        if live(i, TILES):
                            pool.wait_ge(msq_done, i + 1)
                            nc.gpsimd.tensor_tensor(rqk[:, b, :], ssq[:, b, :], mhalf[:, :], ALU.pow).then_inc(rqk_done, 1)
                        i, b = s - 3, (ph - 3) % 2
                        if live(i, TILES):
                            pool.wait_ge(ln2_ve, i + 1)
                            nc.gpsimd.tensor_tensor(rstd2[:, b, :], mean2[:, b, 1:2], mhalf[:, 0:1], ALU.pow)\
                                .then_inc(ln2_rstd, 1)
                    run(pool, body)
                    for k in range(2):
                        pool.wait_ge(sc_out[k], 16 * TOPK * TILES // 2)

                @block.vector
                def _(dve):
                    nc.vector.memset(v17[:, :, :, :, :], 1.0).then_inc(preset, 1)
                    nc.vector.memset(v2[:, :, :, :, :, :], 0.0).then_inc(preset, 1)
                    nc.vector.memset(members[:, :], 0.0).then_inc(members_done, 1)

                    def rank_keep(s, ph):
                        i, b = s - 5, (ph - 5) % 2
                        if not live(i, TILES):
                            return
                        dve.wait_ge(r_psum, i + 1)
                        nc.vector.tensor_tensor(rowof[:, b, :], r_ps, ebase[:, :], ALU.add).then_inc(rowof_done, 1)
                        nc.vector.tensor_tensor(members[:, :], members[:, :], member[:, b, :], ALU.add)\
                            .then_inc(members_done, 1)

                    def slot_rows(s, ph):
                        i, b = s - 5, (ph - 5) % 2
                        if not live(i, TILES):
                            return
                        dve.wait_ge(rowof_done, i + 1)
                        nc.vector.tensor_tensor(picked[:, b, :, :], chosen[:, b, :, :],
                                                rowof[:, b, :].unsqueeze(1).broadcast_to([P, TOPK, EXPERTS]),
                                                ALU.mult).then_inc(picked_done, 1)
                        dve.wait_ge(picked_done, i + 1)
                        nc.vector.tensor_reduce(slotf[:, b, :], picked[:, b, :, :], AX.X, ALU.add).then_inc(slotf_done, 1)
                        dve.wait_ge(slotf_done, i + 1)
                        nc.vector.tensor_scalar(col(slots, i), slotf[:, b, :], 1.0, None, ALU.mult)
                        if past(i, 2):
                            dve.wait_ge(sc_out[b], landed(i, 2, b, 64) - 64)
                        nc.vector.tensor_copy(sloti[:, b, :], slotf[:, b, :]).then_inc(sloti_done, 1)

                    def norm1_stats(s, ph):
                        i, b = s, ph % 2
                        if not live(i, TILES):
                            return
                        dve.wait_ge(ld_x[b], landed(i, 2, b))
                        nc.vector.bn_stats(stats[:, b, :], xin[:, b, :]).then_inc(ln1_st, 1)

                    def norm1_mean(s, ph):
                        i, b = s, ph % 2
                        if live(i, TILES):
                            dve.wait_ge(ln1_st, i + 1)
                        q_bias(s, ph)
                        if not live(i, TILES):
                            return
                        nc.vector.bn_aggr(mean1[:, b, :], stats[:, b, :]).then_inc(ln1_mv, 1)
                        dve.wait_ge(ln1_mv, i + 1)
                        nc.vector.tensor_scalar(mean1[:, b, 1:2], mean1[:, b, 1:2], LN_EPS, None, ALU.add)\
                            .then_inc(ln1_ve, 1)

                    def norm1(s, ph):
                        i, b = s, ph % 2
                        if not live(i, TILES):
                            return
                        dve.wait_ge(ln1_rstd, i + 1)
                        nc.vector.tensor_scalar(xn1[:, b, :], xin[:, b, :], mean1[:, b, 0:1], rstd1[:, b, :],
                                                ALU.subtract, ALU.mult).then_inc(xn1_done, 1)

                    def soft_max(s, ph):
                        i, b = s - 2, ph % 2
                        if not live(i, TILES):
                            return
                        dve.wait_ge(s_psum, i + 1)
                        sv = s_ps.rearrange("p g (h k) -> p (g h) k", k=SEQ)
                        mv = smax[:, b, :, :].rearrange("p g h -> p (g h)")
                        nc.vector.tensor_reduce(mv, sv, AX.X, ALU.max).then_inc(smax_done, 1)

                    def soft(s, ph):
                        i, b = s - 2, ph % 2
                        if not live(i, TILES):
                            return
                        sv = s_ps.rearrange("p g (h k) -> p (g h) k", k=SEQ)
                        mv = smax[:, b, :, :].rearrange("p g h -> p (g h)")
                        dve.wait_ge(smax_done, i + 1)
                        nc.vector.tensor_tensor(
                            prob[:, b, :, :].rearrange("p q (r k) -> p (q r) k", r=2), sv,
                            mv.unsqueeze(2).broadcast_to([P, HEADS, SEQ]), ALU.subtract).then_inc(ssub_done, 1)

                    def q_bias(s, ph):
                        i, b = s - 1, (ph - 1) % 2
                        if not live(i, TILES):
                            return
                        dve.wait_ge(q_psum, i + 1)
                        nc.vector.tensor_tensor(qb[:, b, :], q_ps, bq[:, :], ALU.add).then_inc(qb_done, 1)

                    def k_bias(s, ph):
                        i, b = s - 1, (ph - 1) % 2
                        if not live(i, TILES):
                            return
                        dve.wait_ge(kv_psum, i + 1)
                        nc.vector.tensor_tensor(kb[:, b, :], kv_ps[:, 0:DIM], bk[:, :], ALU.add).then_inc(kb_done, 1)

                    def o_norm(s, ph):
                        i, b = s - 3, (ph - 3) % 2
                        if not live(i, TILES):
                            return
                        dve.wait_ge(o_psum, i + 1)
                        nc.vector.reciprocal(rsum[:, b, :, :], o_ps[:, :, :, HD]).then_inc(rsum_done, 1)
                        dve.wait_ge(rsum_done, i + 1)
                        ov = on[:, b, :].rearrange("p (g r d) -> p (g r) d", g=PAIRS, r=2)
                        nc.vector.tensor_tensor(
                            ov, o_ps[:, :, :, 0:HD].rearrange("p g r d -> p (g r) d"),
                            rsum[:, b, :, :].rearrange("p g r -> p (g r)").unsqueeze(2).broadcast_to([P, HEADS, HD]),
                            ALU.mult).then_inc(on_done, 1)

                    def mean_square(s, ph):
                        i, b = s - 1, (ph - 1) % 2
                        if not live(i, TILES):
                            return
                        dve.wait_ge(ssq_done, 2 * i + 2)
                        nc.vector.tensor_scalar(ssq[:, b, :], ssq[:, b, :], 1.0 / DIM, RMS_EPS, ALU.mult, ALU.add)\
                            .then_inc(msq_done, 1)

                    def k_norm(s, ph):
                        i, b = s - 1, (ph - 1) % 2
                        if not live(i, TILES):
                            return
                        dve.wait_ge(rqk_done, i + 1)
                        nc.vector.tensor_scalar(kb[:, b, :], kb[:, b, :], rqk[:, b, 1:2], None, ALU.mult)\
                            .then_inc(kn_done, 1)

                    def gate_top(s, ph):
                        i, b = s - 4, ph % 2
                        if not live(i, TILES):
                            return
                        dve.wait_ge(l_psum, i + 1)
                        nc.vector.tensor_copy(logits[:, b, :], l_ps).then_inc(logits_done, 1)
                        dve.wait_ge(logits_done, i + 1)
                        rank_keep(s, ph)
                        nc.vector.max(top8[:, b, :], logits[:, b, :]).then_inc(top_done, 1)
                        dve.wait_ge(top_done, i + 1)
                        nc.vector.tensor_scalar(ntop[:, b, :], top8[:, b, 0:1], -1.0, None, ALU.mult).then_inc(ntop_done, 1)
                        nc.vector.max_index(top8i[:, b, :], top8[:, b, :], logits[:, b, :]).then_inc(topi_done, 1)

                    def choose(s, ph):
                        i, b = s - 4, ph % 2
                        j, d = s - 3, (ph - 3) % 2
                        if live(j, TILES):
                            dve.wait_ge(ln2_st, j + 1)
                        if live(i, TILES):
                            dve.wait_ge(topi_done, i + 1)
                            nc.vector.tensor_copy(topif[:, b, :], top8i[:, b, 0:TOPK]).then_inc(topif_done, 1)
                        if live(j, TILES):
                            nc.vector.bn_aggr(mean2[:, d, :], stats2[:, d, :]).then_inc(ln2_mv, 1)
                        if live(i, TILES):
                            nc.vector.tensor_scalar(col(experts, i), top8i[:, b, 0:TOPK], 1, None, ALU.mult)
                            dve.wait_ge(topif_done, i + 1)
                            nc.vector.tensor_tensor(chosen[:, b, :, :],
                                                    eiota[:, :].unsqueeze(1).broadcast_to([P, TOPK, EXPERTS]),
                                                    topif[:, b, :].unsqueeze(2).broadcast_to([P, TOPK, EXPERTS]),
                                                    ALU.is_equal).then_inc(chosen_done, 1)
                        if live(j, TILES):
                            dve.wait_ge(ln2_mv, j + 1)
                            nc.vector.tensor_scalar(mean2[:, d, 1:2], mean2[:, d, 1:2], LN_EPS, None, ALU.add)\
                                .then_inc(ln2_ve, 1)
                        if live(i, TILES):
                            dve.wait_ge(chosen_done, i + 1)
                            nc.vector.tensor_reduce(member[:, b, :], chosen[:, b, :, :].rearrange("p k e -> p e k"),
                                                    AX.X, ALU.add).then_inc(member_done, 1)

                    def gate_weights(s, ph):
                        i, b = s - 4, ph % 2
                        if not live(i, TILES):
                            return
                        dve.wait_ge(gexp_done, 2 * i + 2)
                        nc.vector.scalar_tensor_tensor(out=wden[:, b, 0:1], in0=zsum[:, b, 0:1], scalar=1e-20,
                                                       in1=zsum[:, b, 1:2], op0=ALU.mult, op1=ALU.add)\
                            .then_inc(wden_done, 1)
                        dve.wait_ge(wden_done, 2 * i + 1)
                        nc.vector.reciprocal(wden[:, b, 1:2], wden[:, b, 0:1]).then_inc(wden_done, 1)
                        dve.wait_ge(wden_done, 2 * i + 2)
                        nc.vector.tensor_scalar(col(weights, i), etop[:, b, :], wden[:, b, 1:2], None, ALU.mult)\
                            .then_inc(wt_done, 1)

                    def residual(s, ph):
                        i, b = s - 3, (ph - 3) % 2
                        if not live(i, TILES):
                            return
                        dve.wait_ge(y_psum, i + 1)
                        dve.wait_ge(xrb_done, i + 1)
                        if past(i, 2):
                            dve.wait_ge(st_x1[b], landed(i, 2, b) - 16)
                        nc.vector.tensor_tensor(x1[:, b, :], y_ps, xrb[:, b, :], ALU.add).then_inc(x1_done, 1)
                        dve.wait_ge(x1_done, i + 1)
                        nc.vector.bn_stats(stats2[:, b, :], x1[:, b, :]).then_inc(ln2_st, 1)

                    def norm2(s, ph):
                        i, b = s - 3, (ph - 3) % 2
                        if not live(i, TILES):
                            return
                        dve.wait_ge(ln2_rstd, i + 1)
                        nc.vector.tensor_scalar(xn2[:, b, :], x1[:, b, :], mean2[:, b, 0:1], rstd2[:, b, :],
                                                ALU.subtract, ALU.mult).then_inc(xn2_done, 1)

                    def body(s, ph):
                        norm1_stats(s, ph)
                        norm1_mean(s, ph)
                        k_bias(s, ph)
                        soft_max(s, ph)
                        mean_square(s, ph)
                        o_norm(s, ph)
                        soft(s, ph)
                        norm1(s, ph)
                        k_norm(s, ph)
                        gate_top(s, ph)
                        if not live(s - 4, TILES):
                            rank_keep(s, ph)
                        residual(s, ph)
                        choose(s, ph)
                        gate_weights(s, ph)
                        norm2(s, ph)
                        slot_rows(s, ph)
                    run(dve, body)
        LOOK = 7
        GROUP = 4
        table = sb("table", [1, 2, ETILES + 2 * LOOK + 2], I32)
        shift = sb("shift", [P, EXPERTS])
        zeros = sb("zeros", [P, DIM])
        counts = sb("counts", [1, EXPERTS], I32)

        def entries(engine, part, first, count, top, why):
            src = part[0:1, first:first + count] if isinstance(first, int) else part[0:1, bass.ds(first, count)]
            return nc.values_load_multi_w_load_instructions(
                src, engines=[engine], min_val=0, max_val=top, skip_runtime_bounds_check_because=why)[1]

        with ExitStack() as cx:
            def tsb(name, shape, dt=F32):
                return cx.enter_context(nc.sbuf_tensor(name, shape, dt))
            KT = -(-ETILES // P)
            total_f = tsb("total_f", [P, EXPERTS])
            total_i = tsb("total_i", [P, EXPERTS], I32)
            tiles_i = tsb("tiles_i", [P, EXPERTS], I32)
            tiles_f = tsb("tiles_f", [P, EXPERTS])
            tail_f = tsb("tail_f", [P, EXPERTS])
            ends = tsb("ends", [P, EXPERTS])
            tile_no = tsb("tile_no", [P, KT])
            over = tsb("over", [P, KT, EXPERTS])
            skipped = tsb("skipped", [P, KT, EXPERTS])
            owner = tsb("owner", [P, KT])
            start = tsb("start", [P, KT])
            row = tsb("row", [P, KT])
            found = tsb("found", [P, 2, KT])
            ld_no, tot_psum, counts_done, found_done, found_psum = (
                cx.enter_context(nc.semaphore(n)) for n in ("ld_no", "tot_psum", "counts_done", "found_done",
                                                            "found_psum"))
            chain = cx.enter_context(nc.semaphore("chain"))
            tail_out = [cx.enter_context(nc.semaphore(f"tail_out{k}")) for k in range(2)]
            with nc.Block() as block:
                @block.tensor
                def _(pe):
                    nc.tensor.matmul(bank7[:, 0:EXPERTS], ones[:, :], members[:, :], start=True, stop=True)\
                        .then_inc(tot_psum, 1)
                    pe.wait_ge(found_done, 1)
                    for k in range(2 * KT):
                        m = nc.tensor.matmul(bank6[0:1, k * P:(k + 1) * P], found[:, k // KT, k % KT].unsqueeze(1),
                                             ident[:, :], start=True, stop=True)
                    m.then_inc(found_psum, 1)

                @block.vector
                def _(dve):
                    done = [0]

                    def step(ins):
                        ins.then_inc(chain, 1)
                        done[0] += 1
                        dve.wait_ge(chain, done[0])
                    nc.vector.memset(table[:, :, :], 0)
                    step(nc.vector.memset(zeros[:, :], 0.0))
                    dve.wait_ge(tot_psum, 1)
                    step(nc.vector.tensor_copy(total_f[:, :], bank7[:, 0:EXPERTS]))
                    step(nc.vector.tensor_tensor(tail_f[:, :], total_f[:, :], ebase[:, :], ALU.add))
                    nc.vector.tensor_copy(counts[:, :], tail_f[0:1, :]).then_inc(counts_done, 1)
                    step(nc.vector.tensor_scalar(total_f[:, :], total_f[:, :], float(P - 1), None, ALU.add))
                    step(nc.vector.tensor_copy(total_i[:, :], total_f[:, :]))
                    step(nc.vector.tensor_scalar(tiles_i[:, :], total_i[:, :], 7, None, ALU.logical_shift_right))
                    step(nc.vector.tensor_copy(tiles_f[:, :], tiles_i[:, :]))
                    step(nc.vector.tensor_tensor_scan(ends[:, :], ones[:, 0:EXPERTS], tiles_f[:, :], 0.0,
                                                      ALU.mult, ALU.add))
                    dve.wait_ge(ld_no, 16)
                    shape = [P, KT, EXPERTS]
                    step(nc.vector.tensor_tensor(over[:, :, :], ends[:, :].unsqueeze(1).broadcast_to(shape),
                                                 tile_no[:, :].unsqueeze(2).broadcast_to(shape), ALU.is_le))
                    step(nc.vector.tensor_tensor(skipped[:, :, :], over[:, :, :],
                                                 tiles_f[:, :].unsqueeze(1).broadcast_to(shape), ALU.mult))
                    step(nc.vector.tensor_reduce(owner[:, :], over[:, :, :], AX.X, ALU.add))
                    step(nc.vector.tensor_reduce(start[:, :], skipped[:, :, :], AX.X, ALU.add))
                    step(nc.vector.tensor_tensor(start[:, :], tile_no[:, :], start[:, :], ALU.subtract))
                    step(nc.vector.tensor_scalar(start[:, :], start[:, :], float(P), None, ALU.mult))
                    step(nc.vector.scalar_tensor_tensor(out=row[:, :], in0=owner[:, :], scalar=float(CAP),
                                                        in1=start[:, :], op0=ALU.mult, op1=ALU.add))
                    nc.vector.tensor_scalar(found[:, 0, :], owner[:, :], float(EXPERTS - 1), None, ALU.min)
                    nc.vector.tensor_scalar(found[:, 1, :], row[:, :], float(DUMP), None, ALU.min)\
                        .then_inc(found_done, 1)
                    step(nc.vector.tensor_tensor(shift[:, :], ends[:, :], tiles_f[:, :], ALU.subtract))
                    step(nc.vector.scalar_tensor_tensor(out=shift[:, :], in0=shift[:, :], scalar=float(P),
                                                        in1=ebase[:, :], op0=ALU.mult, op1=ALU.subtract))
                    dve.wait_ge(found_psum, 1)
                    step(nc.vector.tensor_copy(
                        table[:, :, LOOK:LOOK + ETILES],
                        bank6[0:1, :].rearrange("p (c t) -> p c t", c=2)[:, :, 0:ETILES]))

                def tails(eng, engine, first, count, out):
                    eng.wait_ge(chain, 1)
                    eng.wait_ge(counts_done, 1)

                    def tail(g, ph):
                        for free in entries(engine, counts, g * GROUP + first, GROUP, DUMP - P,
                                            "a region's base and at most TOKENS tokens"):
                            eng.dma_start(xs_d[bass.ds(free, P), :], zeros[:, :]).then_inc(out, 16)
                    pipeline(eng, 1, count // GROUP, count // GROUP, 1, tail)

                @block.sync
                def _(sp):
                    sp.dma_start(tile_no[:, :], a["tileno"]).then_inc(ld_no, 16)
                    tails(sp, mybir.EngineType.SP, 0, EXPERTS // 2, tail_out[0])
                    sp.wait_ge(tail_out[0], 16 * EXPERTS // 2)

                @block.scalar
                def _(act):
                    act.wait_ge(chain, 1)
                    act.dma_start(xs_d[DUMP:DUMP + P, :], zeros[:, :]).then_inc(tail_out[1], 16)
                    tails(act, mybir.EngineType.Activation, EXPERTS // 2, EXPERTS // 2, tail_out[1])
                    act.wait_ge(tail_out[1], 16 * (EXPERTS // 2 + 1))

        with ExitStack() as cx:
            def esb(name, shape, dt=F32):
                return cx.enter_context(nc.sbuf_tensor(name, shape, dt))
            RING = 4
            xg = esb("xg", [P, RING, DIM])
            xgt = esb("xgt", [P, 2, 2, P])
            gated = esb("gated", [P, 2, INNER])
            h = esb("h", [P, 2, INNER])
            ht = esb("ht", [HALF, 2, 2, P])
            rdt = esb("rdt", [P, 2, P])
            yo = esb("yo", [P, RING, DIM])
            xgt_ps = bank03[:, 0, 0:2 * P]
            ht_ps = bank03[0:HALF, 1, 0:2 * P]
            gu_ps = [bank03[:, 2 + k, 0:2 * INNER] for k in range(2)]
            y_ps = [bank4[:, 0:DIM], bank5[:, 0:DIM]]
            rd_ps = bank6[:, 0:P]
            ld_xg = [cx.enter_context(nc.semaphore(f"ld_xg{k}")) for k in range(RING)]
            st_y = [cx.enter_context(nc.semaphore(f"st_y{k}")) for k in range(RING)]
            (xgt_psum, xgt_done, gu_psum, gated_done, h_done, ht_psum, ht_done, rd_psum, rdt_done, ye_psum,
             yo_done) = (cx.enter_context(nc.semaphore(n)) for n in (
                 "xgt_psum", "xgt_done", "gu_psum", "gated_done", "h_done", "ht_psum", "ht_done", "rd_psum",
                 "rdt_done", "ye_psum", "yo_done"))
            N = ETILES
            ys_t = ys_d.rearrange("(t p) d -> t p d", p=P)
            UP, DOWN, LAG = 4, 7, 8

            def run(eng, body):
                pipeline(eng, 12, N, N + LAG, RING, body)

            with nc.Block() as block:
                @block.sync
                def _(sp):
                    first = [None]

                    def body(s, ph):
                        i, b = s, ph % RING
                        if live(i, N):
                            if b == 0:
                                first[0] = entries(mybir.EngineType.SP, table[:, 1, :], i + LOOK, RING, DUMP,
                                                   "clamped to DUMP when the table was made")
                            if past(i, RING):
                                sp.wait_ge(xgt_psum, i - RING + 1)
                            sp.dma_start(xg[:, b, :], xs_d[bass.ds(first[0][b], P), :]).then_inc(ld_xg[b], 16)
                        i, b = s - 8, ph % RING
                        if live(i, N):
                            sp.wait_ge(yo_done, i + 1)
                            sp.dma_start(at(ys_t, i), yo[:, b, :]).then_inc(st_y[b], 16)
                    run(sp, body)
                    for k in range(RING):
                        sp.wait_ge(st_y[k], 16 * N // RING)

                @block.tensor
                def _(pe):
                    owners = [None]

                    def body(s, ph):
                        if ph % RING == 0:
                            owners[0] = entries(mybir.EngineType.PE, table[:, 0, :], s - DOWN + LOOK,
                                                DOWN - UP + RING, EXPERTS - 1,
                                                "clamped to the last expert when the table was made")

                        def weight(w, lag):
                            e = owners[0][DOWN - lag + ph % RING]
                            return w[:, bass.ds(e, 1), :].rearrange("p e n -> p (e n)")
                        i, b = s - DOWN, (ph - DOWN) % 2
                        if live(i, N):
                            pe.wait_ge(rdt_done, i + 1)
                            nc.tensor.matmul(y_ps[b], rdt[:, b, :], weight(down_w, DOWN), start=True, stop=True)\
                                .then_inc(ye_psum, 1)
                        i, b = s - 6, ph % 2
                        if live(i, N):
                            pe.wait_ge(ht_done, i + 1)
                            for c in range(2):
                                m = nc.tensor.matmul(rd_ps, rd_w[:, c, :], ht[:, b, c, :],
                                                     start=(c == 0), stop=(c == 1))
                            m.then_inc(rd_psum, 1)
                        i, b = s - 5, (ph - 5) % 2
                        if live(i, N):
                            pe.wait_ge(h_done, i + 1)
                            for c in range(2):
                                m = nc.tensor.transpose(ht_ps[:, c * P:(c + 1) * P],
                                                        h[:, b, c * HALF:(c + 1) * HALF], ident[:, :])
                            m.then_inc(ht_psum, 1)
                        i, b = s - UP, ph % 2
                        if live(i, N):
                            w = weight(up_w, UP)
                            pe.wait_ge(xgt_done, i + 1)
                            nc.tensor.matmul(gu_ps[b][:, 0:INNER], xgt[:, b, 0, :], w[:, 0:INNER],
                                             start=True, stop=True)
                            nc.tensor.matmul(gu_ps[b][:, INNER:2 * INNER], xgt[:, b, 1, :], w[:, INNER:2 * INNER],
                                             start=True, stop=True).then_inc(gu_psum, 1)
                        i = s - 3
                        if live(i, N):
                            b = (ph - 3) % RING
                            pe.wait_ge(ld_xg[b], landed(i, RING, b))
                            for c in range(2):
                                m = nc.tensor.transpose(xgt_ps[:, c * P:(c + 1) * P],
                                                        xg[:, b, c * P:(c + 1) * P], ident[:, :])
                            m.then_inc(xgt_psum, 1)
                    run(pe, body)

                @block.scalar
                def _(act):
                    def body(s, ph):
                        i, b = s - 6, ph % 2
                        if live(i, N):
                            act.wait_ge(rd_psum, i + 1)
                            nc.scalar.activation(rdt[:, b, :], rd_ps, ACT.Copy).then_inc(rdt_done, 1)
                        i, b = s - UP, ph % 2
                        if live(i, N):
                            act.wait_ge(gu_psum, i + 1)
                            nc.scalar.activation(gated[:, b, :], gu_ps[b][:, 0:INNER], ACT.Silu).then_inc(gated_done, 1)
                        i, b = s - 3, (ph - 3) % 2
                        if live(i, N):
                            act.wait_ge(xgt_psum, i + 1)
                            nc.scalar.activation(xgt[:, b, :, :].rearrange("p c t -> p (c t)"), xgt_ps, ACT.Copy)\
                                .then_inc(xgt_done, 1)
                    run(act, body)

                @block.vector
                def _(dve):
                    def body(s, ph):
                        i, b = s - DOWN, (ph - DOWN) % 2
                        if live(i, N):
                            dve.wait_ge(ye_psum, i + 1)
                            if past(i, RING):
                                o = (ph - DOWN) % RING
                                dve.wait_ge(st_y[o], landed(i, RING, o) - 16)
                            nc.vector.tensor_copy(yo[:, (ph - DOWN) % RING, :], y_ps[b]).then_inc(yo_done, 1)
                        i, b = s - 5, (ph - 5) % 2
                        if live(i, N):
                            dve.wait_ge(ht_psum, i + 1)
                            nc.vector.tensor_copy(ht[:, b, :, :].rearrange("p c t -> p (c t)"), ht_ps)\
                                .then_inc(ht_done, 1)
                        i, b = s - UP, ph % 2
                        if live(i, N):
                            dve.wait_ge(gated_done, i + 1)
                            nc.vector.tensor_tensor(h[:, b, :], gu_ps[b][:, INNER:2 * INNER], gated[:, b, :], ALU.mult)\
                                .then_inc(h_done, 1)
                    run(dve, body)

        with ExitStack() as cx:
            def fsb(name, shape, dt=F32):
                return cx.enter_context(nc.sbuf_tensor(name, shape, dt))
            DEPTH = 4
            x2t = fsb("x2t", [P, DEPTH, CH, P])
            xr1 = fsb("xr1", [P, DEPTH, DIM])
            rt = fsb("rt", [P, 2, 2, P])
            sg = fsb("sg", [P, 2, SCH, P])
            sh = fsb("sh", [P, 2, SCH, P])
            srt = fsb("srt", [P, 2, P])
            rows = fsb("rows", [P, DEPTH, TOPK], I32)
            onehot = fsb("onehot", [P, 2, TOPK, EXPERTS])
            shifts = fsb("shifts", [P, 2, TOPK, EXPERTS])
            moved = fsb("moved", [P, 2, TOPK])
            wts = fsb("wts", [P, 2, TOPK])
            got = fsb("got", [P, DEPTH, TOPK, DIM])
            acc = fsb("acc", [P, 2, TOPK + 1, DIM])
            fence = fsb("fence", [P, DEPTH])
            rt_ps = bank03[:, 0, 0:2 * P]
            g_ps = bank03[:, 1, 0:SPAD]
            u_ps = bank03[:, 2, 0:SPAD]
            srt_ps = bank03[:, 3, 0:P]
            sy_ps = bank4[:, 0:DIM]
            ld_x2t, ld_x1, gathered, st_out = (
                [cx.enter_context(nc.semaphore(f"{n}{k}")) for k in range(DEPTH)]
                for n in ("ld_x2t", "ld_x1", "gathered", "st_out"))
            (rt_psum, rt_done, g_psum, u_psum, sg_done, sh_done2, srt_psum, srt_done, sy_psum, sum_done,
             rows_done, wts_done, fenced, onehot_done, shifts_done, moved_done) = (cx.enter_context(nc.semaphore(n)) for n in (
                 "rt_psum", "rt_done", "g_psum", "u_psum", "sg_done", "sh_done2", "srt_psum", "srt_done", "sy_psum",
                 "sum_done", "rows_done", "wts_done", "fenced", "onehot_done", "shifts_done", "moved_done"))
            out_t = a["out"].rearrange("(t p) d -> t p d", p=P)

            def run(eng, body):
                pipeline(eng, 8, TILES, TILES + 3, DEPTH, body)

            with nc.Block() as block:
                @block.sync
                def _(sp):
                    def body(s, ph):
                        i, b = s, ph % DEPTH
                        if live(i, TILES):
                            if past(i, DEPTH):
                                sp.wait_ge(rt_psum, i - DEPTH + 1)
                            sp.dma_start(x2t[:, b, :, :].rearrange("p c t -> p (c t)"), at(xn2t_d, i))\
                                .then_inc(ld_x2t[b], 16)
                            if past(i, DEPTH):
                                sp.wait_ge(sum_done, (TOPK + 1) * (i - DEPTH + 1))
                            sp.dma_start(xr1[:, b, :], at(x1_d, i)).then_inc(ld_x1[b], 16)
                        i, b = s - 3, (ph - 3) % 2
                        if live(i, TILES):
                            sp.wait_ge(sum_done, (TOPK + 1) * (i + 1))
                            sp.dma_start(at(out_t, i), acc[:, b, TOPK, :]).then_inc(st_out[(ph - 3) % DEPTH], 16)
                    run(sp, body)
                    for k in range(DEPTH):
                        sp.wait_ge(st_out[k], 16 * TILES // DEPTH)

                @block.tensor
                def _(pe):
                    def body(s, ph):
                        i, b = s - 3, (ph - 3) % 2
                        if live(i, TILES):
                            pe.wait_ge(sh_done2, i + 1)
                            if past(i, 1):
                                pe.wait_ge(srt_done, i)
                            for c in range(SCH):
                                k = P if c < SCH - 1 else SLAST
                                m = nc.tensor.matmul(srt_ps, srd_w[0:k, c, :], sh[0:k, b, c, :],
                                                     start=(c == 0), stop=(c == SCH - 1))
                            m.then_inc(srt_psum, 1)
                        i, b = s - 1, (ph - 1) % 2
                        if live(i, TILES):
                            pe.wait_ge(ld_x2t[(ph - 1) % DEPTH], landed(i, DEPTH, (ph - 1) % DEPTH))
                            if past(i, 1):
                                pe.wait_ge(rt_done, i)
                            for r in range(2):
                                for c in range(CH):
                                    m = nc.tensor.matmul(rt_ps[:, r * P:(r + 1) * P], srgu_w[:, c, r, :],
                                                         x2t[:, (ph - 1) % DEPTH, c, :], start=(c == 0), stop=(c == CH - 1))
                            m.then_inc(rt_psum, 1)
                        i, b = s - 2, ph % 2
                        if live(i, TILES):
                            pe.wait_ge(rt_done, i + 1)
                            if past(i, 1):
                                pe.wait_ge(sg_done, i)
                            for c in range(SCH):
                                m = nc.tensor.matmul(g_ps[:, c * P:(c + 1) * P], sup_w[:, 0, c * P:(c + 1) * P],
                                                     rt[:, b, 0, :], start=True, stop=True)
                            m.then_inc(g_psum, 1)
                            if past(i, 1):
                                pe.wait_ge(sh_done2, i)
                            for c in range(SCH):
                                m = nc.tensor.matmul(u_ps[:, c * P:(c + 1) * P], sup_w[:, 1, c * P:(c + 1) * P],
                                                     rt[:, b, 1, :], start=True, stop=True)
                            m.then_inc(u_psum, 1)
                        i, b = s - 3, (ph - 3) % 2
                        if live(i, TILES):
                            pe.wait_ge(srt_done, i + 1)
                            if past(i, 1):
                                pe.wait_ge(sum_done, (TOPK + 1) * (i - 1) + 1)
                            nc.tensor.matmul(sy_ps, srt[:, b, :], sdown_w[:, :], start=True, stop=True)\
                                .then_inc(sy_psum, 1)
                    run(pe, body)

                @block.scalar
                def _(act):
                    def body(s, ph):
                        i, b = s - 3, (ph - 3) % 2
                        if live(i, TILES):
                            act.wait_ge(srt_psum, i + 1)
                            nc.scalar.activation(srt[:, b, :], srt_ps, ACT.Copy).then_inc(srt_done, 1)
                        i, b = s - 1, (ph - 1) % 2
                        if live(i, TILES):
                            act.wait_ge(rt_psum, i + 1)
                            nc.scalar.activation(rt[:, b, :, :].rearrange("p c t -> p (c t)"), rt_ps, ACT.Copy)\
                                .then_inc(rt_done, 1)
                        i, b = s - 2, ph % 2
                        if live(i, TILES):
                            act.wait_ge(g_psum, i + 1)
                            nc.scalar.activation(sg[:, b, :, :].rearrange("p c t -> p (c t)"), g_ps, ACT.Silu)\
                                .then_inc(sg_done, 1)
                    run(act, body)

                @block.gpsimd
                def _(pool):
                    def body(s, ph):
                        i, b = s, ph % DEPTH
                        if live(i, TILES):
                            pool.wait_ge(rows_done, i + 1)
                            if past(i, DEPTH):
                                pool.wait_ge(sum_done, (TOPK + 1) * (i - DEPTH + 1))
                                pool.wait_ge(fenced, i - DEPTH + 1)
                            nc.gpsimd.tensor_tensor(fence[:, b:b + 1], ones[:, 0:1], ones[:, 0:1], ALU.mult)\
                                .then_inc(fenced, 1)
                            for k in range(TOPK):
                                nc.gpsimd.indirect_dma_start(
                                    got[:, b, k, :], None, ys_d, bass.IndirectOffsetOnAxis(rows[:, b, k:k + 1], 0))\
                                    .then_inc(gathered[b], 16)
                    run(pool, body)

                @block.vector
                def _(dve):
                    def body(s, ph):
                        i, b, d = s, ph % 2, ph % DEPTH
                        if live(i, TILES):
                            if past(i, DEPTH):
                                dve.wait_ge(gathered[d], landed(i, DEPTH, d, 16 * TOPK) - 16 * TOPK)
                            shape = [P, TOPK, EXPERTS]
                            nc.vector.tensor_tensor(
                                onehot[:, b, :, :], eiota[:, :].unsqueeze(1).broadcast_to(shape),
                                col(experts, i).unsqueeze(2).broadcast_to(shape), ALU.is_equal).then_inc(onehot_done, 1)
                            dve.wait_ge(onehot_done, i + 1)
                            nc.vector.tensor_tensor(shifts[:, b, :, :], onehot[:, b, :, :],
                                                    shift[:, :].unsqueeze(1).broadcast_to(shape), ALU.mult)\
                                .then_inc(shifts_done, 1)
                            dve.wait_ge(shifts_done, i + 1)
                            nc.vector.tensor_reduce(moved[:, b, :], shifts[:, b, :, :], AX.X, ALU.add)\
                                .then_inc(moved_done, 1)
                            dve.wait_ge(moved_done, i + 1)
                            nc.vector.tensor_tensor(rows[:, d, :], moved[:, b, :], col(slots, i), ALU.add)\
                                .then_inc(rows_done, 1)
                        i, b = s - 2, ph % 2
                        if live(i, TILES):
                            dve.wait_ge(sg_done, i + 1)
                            dve.wait_ge(u_psum, i + 1)
                            nc.vector.tensor_tensor(sh[:, b, :, :].rearrange("p c t -> p (c t)"), u_ps,
                                                    sg[:, b, :, :].rearrange("p c t -> p (c t)"), ALU.mult)\
                                .then_inc(sh_done2, 1)
                        i, b, d = s - 3, (ph - 3) % 2, (ph - 3) % DEPTH
                        if live(i, TILES):
                            dve.wait_ge(ld_x1[d], landed(i, DEPTH, d))
                            dve.wait_ge(sy_psum, i + 1)
                            if past(i, 2):
                                o = (ph - 5) % DEPTH
                                dve.wait_ge(st_out[o], landed(i - 2, DEPTH, o))
                            nc.vector.tensor_scalar(wts[:, b, :], col(weights, i), 1.0, None, ALU.mult)\
                                .then_inc(wts_done, 1)
                            nc.vector.tensor_tensor(acc[:, b, 0, :], sy_ps, xr1[:, d, :], ALU.add).then_inc(sum_done, 1)
                            dve.wait_ge(gathered[d], landed(i, DEPTH, d, 16 * TOPK))
                            dve.wait_ge(wts_done, i + 1)
                            for k in range(TOPK):
                                dve.wait_ge(sum_done, (TOPK + 1) * i + k + 1)
                                nc.vector.scalar_tensor_tensor(
                                    out=acc[:, b, k + 1, :], in0=got[:, d, k, :], scalar=wts[:, b, k:k + 1],
                                    in1=acc[:, b, k, :], op0=ALU.mult, op1=ALU.add).then_inc(sum_done, 1)
                    run(dve, body)


def kernel(**inputs):
    import concourse.bacc as bacc
    from concourse.bass_utils import run_bass_kernel_spmd

    get = {n.replace("L0_", ""): np.asarray(v) for n, v in inputs.items()}

    def rows(w):
        return w.T.reshape(-1, P, w.shape[0]).transpose(1, 0, 2)

    def feature(v):
        return v.reshape(CH, P).T

    x = get["x"].reshape(TOKENS, DIM)
    ctx = get["ctx_2048"].reshape(TOKENS, DIM)
    wv = get["xattn_w_v_img"].reshape(PAIRS, 2, HD, DIM).transpose(1, 0, 2, 3).reshape(DIM, DIM)
    t = lambda n: get["ffn_" + n].transpose(0, 2, 1)
    index = np.arange(P)
    arrays = {
        "x": x,
        "ctxt": ctx.T.reshape(CH, P, TOKENS).transpose(1, 0, 2),
        "ident": np.eye(P, dtype=np.float32),
        "tri": (index[:, None] < index[None, :]).astype(np.float32),
        "ones": np.ones((P, P), np.float32),
        "headmask": ((index[:, None] // HD) % GH == np.arange(GH)[None, :]).astype(np.float32),
        "eiota": np.tile(np.arange(EXPERTS, dtype=np.float32), (P, 1)),
        "ebase": np.tile(np.arange(EXPERTS, dtype=np.float32) * CAP, (P, 1)),
        "tileno": np.arange(-(-ETILES // P) * P, dtype=np.float32).reshape(-1, P).T,
        "wq": rows(get["xattn_w_q"]),
        "wkv": np.concatenate([rows(get["xattn_w_k_img"]), rows(wv)], axis=2),
        "wo": rows(get["xattn_w_o"]),
        "bq": get["xattn_b_q"][None], "bk": get["xattn_b_k_img"][None], "bo": get["xattn_b_o"][None],
        "bv": feature(get["xattn_b_v_img"]),
        "gq": feature(get["xattn_g_q"]), "gk": feature(get["xattn_g_k_img"]),
        "gate": rows(get["ffn_gate_w"]),
        "rgu": np.concatenate([rows(get["ffn_Rg"]), rows(get["ffn_Ru"])], axis=2),
        "rd": get["ffn_Rd"].T.reshape(2, HALF, RANK).transpose(1, 0, 2),
        "srgu": np.stack([rows(get["ffn_s_Rg"]), rows(get["ffn_s_Ru"])], axis=2),
        "srd": get["ffn_s_Rd"].T,
        "raw": np.concatenate([get["ffn_Ug"], t("Cg"), get["ffn_Uu"], t("Cu"), get["ffn_Ud"], t("Cd")], axis=2),
        "sraw": np.concatenate([get["ffn_s_Ug"], get["ffn_s_Cg"].T, get["ffn_s_Uu"], get["ffn_s_Cu"].T,
                                get["ffn_s_Ud"], get["ffn_s_Cd"].T], axis=1),
    }
    nc = bacc.Bacc("TRN2", target_bir_lowering=False, num_devices=1)
    feed, aps = {}, {}
    for name, v in arrays.items():
        feed["in_" + name] = np.ascontiguousarray(v)
        aps[name] = nc.dram_tensor("in_" + name, v.shape, F32, kind="ExternalInput").ap()
    aps["out"] = nc.dram_tensor("out", [TOKENS, DIM], F32, kind="ExternalOutput").ap()
    build(nc, aps)
    r = run_bass_kernel_spmd(nc, [feed], core_ids=[0])
    return r.results[0]["out"].reshape(BATCH, SEQ, DIM)
```

```python
from contextlib import ExitStack

import numpy as np

import concourse.bass as bass
from concourse import mybir

F32 = mybir.dt.float32
BF16 = mybir.dt.bfloat16
I32 = mybir.dt.int32
U32 = mybir.dt.uint32
ALU = mybir.AluOpType
ACT = mybir.ActivationFunctionType
AX = mybir.AxisListType

P = 128
BATCH, SEQ, DIM = 64, 64, 256
TOKENS = BATCH * SEQ
TILES = TOKENS // P
CH = DIM // P
HEADS, HD = 16, 16
PAIRS = HEADS // 2
GROUPS, GH = 2, 4
EXPERTS, TOPK = 32, 4
RANK = 128
INNER = 176
HALF = INNER // 2
SHARED = 2 * INNER
SCH = 3
SLAST = SHARED - 2 * P
SPAD = SCH * P
CAP = TOKENS + P
ETILES = (TOKENS * TOPK + EXPERTS * (P - 1)) // P + 1
DUMP = EXPERTS * CAP
SPARE = ETILES - TOKENS * TOPK // P
LN_EPS, RMS_EPS = 1e-5, 1e-6
ROW = DIM + 1
RAW = 2 * (RANK + INNER) + RANK + DIM


def live(i, n):
    return not isinstance(i, int) or 0 <= i < n


def past(i, k):
    return not isinstance(i, int) or i >= k


def landed(i, ring, slot, per=16):
    return (i - slot) * (per // ring) + per


def pipeline(eng, lead, stop, total, unroll, body):
    for s in range(lead):
        body(s, s)
    with eng.Fori(0, (stop - lead) // unroll) as g:
        for u in range(unroll):
            body(g * unroll + (lead + u), lead + u)
    for s in range(stop, total):
        body(s, s)


def at(ap, i):
    return ap[i] if isinstance(i, int) else ap[bass.ds(i, 1), :, :].rearrange("t p m -> (t p) m")


def col(tile, i):
    return tile[:, i, :] if isinstance(i, int) else tile[:, bass.ds(i, 1), :].rearrange("p t m -> p (t m)")


def build(nc, a):
    ctx = ExitStack()
    with ctx:
        def sb(name, shape, dt=F32):
            return ctx.enter_context(nc.sbuf_tensor(name, shape, dt))

        def ps(name, shape):
            return ctx.enter_context(nc.psum_tensor(name, shape, F32))

        def sem(name):
            return ctx.enter_context(nc.semaphore(name))

        def sems(name, n=2):
            return [sem(f"{name}{k}") for k in range(n)]

        x1_d = nc.dram_tensor("x1_d", [TILES, P, DIM], F32, kind="Internal").ap()
        xn2t_d = nc.dram_tensor("xn2t_d", [TILES, P, DIM], F32, kind="Internal").ap()
        xs_d = nc.dram_tensor("xs_d", [DUMP + SPARE * P, ROW], F32, kind="Internal").ap()
        yt_d = nc.dram_tensor("yt_d", [TOKENS * TOPK + (EXPERTS + SPARE) * P, DIM], F32, kind="Internal").ap()

        ident = sb("ident", [P, P])
        tri = sb("tri", [P, P])
        ones = sb("ones", [P, P])
        tri_h = sb("tri_h", [P, P], BF16)
        ones_h = sb("ones_h", [P, P], BF16)
        headmask = sb("headmask", [P, GH])
        eiota = sb("eiota", [P, EXPERTS])
        ebase = sb("ebase", [P, EXPERTS])
        mhalf = sb("mhalf", [P, 2])
        wq = sb("wq", [P, CH, DIM])
        wkv = sb("wkv", [P, CH, 2 * DIM])
        wo = sb("wo", [P, CH, DIM])
        bq = sb("bq", [P, DIM])
        bk = sb("bk", [P, DIM])
        bo = sb("bo", [P, DIM])
        bv = sb("bv", [P, CH])
        gq = sb("gq", [P, CH])
        gk = sb("gk", [P, CH])
        gqk = sb("gqk", [P, CH])
        rgu_w = sb("rgu_w", [P, CH, DIM + EXPERTS])
        rd_w = sb("rd_w", [HALF, 2, RANK])
        srgu_w = sb("srgu_w", [P, CH, 2, RANK])
        srd_w = sb("srd_w", [P, SCH, RANK])
        up_w = sb("up_w", [P, EXPERTS, 2 * INNER])
        down_w = sb("down_w", [P, EXPERTS, DIM])
        sup_w = sb("sup_w", [P, 2, SPAD])
        sdown_w = sb("sdown_w", [P, DIM])
        names = sb("names", [P, TILES, TOPK])
        weights = sb("weights", [P, TILES, TOPK])

        bank03 = ps("bank03", [P, 4, 512])
        bank4, bank5, bank6, bank7 = (ps(f"bank{k}", [P, 512]) for k in range(4, 8))

        loads_first = [(ident, "ident"), (wq, "wq"), (bq, "bq")]
        loads_next = [(wkv, "wkv"), (bk, "bk"), (gq, "gq"), (gk, "gk"), (headmask, "headmask"), (ones, "ones"),
                      (bv, "bv")]
        loads_then = [(wo, "wo"), (bo, "bo"), (rgu_w, "rgu"), (eiota, "eiota"), (tri, "tri"),
                      (ebase, "ebase"), (names, "names"), (rd_w, "rd")]

        LOOK = 7
        GROUP = 4
        table = sb("table", [1, 2, ETILES + 2 * LOOK + 2], I32)
        counts = sb("counts", [1, EXPERTS], I32)

        def entries(engine, part, first, count, top, why):
            src = part[0:1, first:first + count] if isinstance(first, int) else part[0:1, bass.ds(first, count)]
            return nc.values_load_multi_w_load_instructions(
                src, engines=[engine], min_val=0, max_val=top, skip_runtime_bounds_check_because=why)[1]

        with ExitStack() as cx:
            def asb(name, shape, dt=F32):
                return cx.enter_context(nc.sbuf_tensor(name, shape, dt))

            def asem(name):
                return cx.enter_context(nc.semaphore(name))
            assert EXPERTS == TILES
            raw = asb("raw", [P, 2, RAW])
            o_ug, o_cg, o_uu, o_cu = 0, RANK, RANK + INNER, 2 * RANK + INNER
            o_ud, o_cd = 2 * (RANK + INNER), 2 * (RANK + INNER) + RANK
            sraw = asb("sraw", [P, 3 * RANK + 2 * SHARED + DIM])
            s_ug, s_cg, s_uu, s_cu = 0, RANK, RANK + SHARED, 2 * RANK + SHARED
            s_ud, s_cd = 2 * (RANK + SHARED), 2 * (RANK + SHARED) + RANK
            bv_cols = asb("bv_cols", [P, CH, P])
            xin = asb("xin", [P, 2, DIM])
            ctxt = asb("ctxt", [P, 2, CH, P])
            xres = asb("xres", [P, 2, DIM])
            stats = asb("stats", [P, 2, 6])
            mean1 = asb("mean1", [P, 2, 2])
            rstd1 = asb("rstd1", [P, 2, 1])
            xn1 = asb("xn1", [P, 2, DIM])
            xn1t = asb("xn1t", [P, 2, CH, P])
            qb = asb("qb", [P, 2, DIM])
            kb = asb("kb", [P, 2, DIM])
            squares = asb("squares", [P, DIM])
            ssq = asb("ssq", [P, 2, 2])
            rqk = asb("rqk", [P, 2, 2])
            v17 = asb("v17", [P, 2, 2, PAIRS, HD + 1])
            v2 = asb("v2", [P, 2, 2, 2, PAIRS, HD + 1])
            qt = asb("qt", [P, 2, CH, P])
            ktm = asb("ktm", [P, 2, 2 * CH, GH, SEQ])
            smax = asb("smax", [P, 2, GROUPS, CH * GH])
            prob = asb("prob", [P, 2, PAIRS, P])
            probt = asb("probt", [P, 2, PAIRS, P])
            rsum = asb("rsum", [P, 2, PAIRS, 2])
            on = asb("on", [P, 2, DIM])
            ot = asb("ot", [P, 2, CH, P])
            xrb = asb("xrb", [P, 2, DIM])
            x1 = asb("x1", [P, 2, DIM])
            stats2 = asb("stats2", [P, 2, 6])
            mean2 = asb("mean2", [P, 2, 2])
            rstd2 = asb("rstd2", [P, 2, 1])
            xn2 = asb("xn2", [P, 2, DIM])
            xn2t = asb("xn2t", [P, 2, CH, P])
            rgu = asb("rgu", [P, 2, TOPK, ROW])
            top8 = asb("top8", [P, 2, 8])
            rgl = asb("rgl", [P, 2, DIM + EXPERTS])
            ntop = asb("ntop", [P, 2, 1])
            top8i = asb("top8i", [P, 2, 8], U32)
            topif = asb("topif", [P, 2, TOPK])
            egate = asb("egate", [P, 2, EXPERTS])
            etop = asb("etop", [P, 2, TOPK])
            zsum = asb("zsum", [P, 2, 2])
            wden = asb("wden", [P, 2, 2])
            chosen = asb("chosen", [P, 2, TOPK, EXPERTS])
            member = asb("member", [P, 2, EXPERTS], BF16)
            free = asb("free", [P, EXPERTS])
            rowof = asb("rowof", [P, 2, EXPERTS])
            picked = asb("picked", [P, 2, TOPK, EXPERTS])
            slotf = asb("slotf", [P, 2, TOPK])
            sloti = asb("sloti", [P, 2, TOPK], I32)

            s_ps = bank03[:, 0:GROUPS, :]
            kv_ps = bank03[:, 2, :]
            qkt_ps = bank03[:, 3, :].rearrange("p (c t) -> p c t", c=2 * CH)
            y_ps = bank4[:, DIM:2 * DIM]
            pt_ps = bank4[:, :].rearrange("p (c t) -> p c t", c=4)
            r_ps = bank5[:, 480:480 + EXPERTS]
            c_ps = bank5[:, 448:448 + EXPERTS]
            o_ps = bank5[:, 0:PAIRS * 2 * (HD + 1)].rearrange("p (g r d) -> p g r d", g=PAIRS, r=2)
            x2t_ps = bank6[:, 0:DIM]
            rgl_ps = bank6[:, 0:DIM + EXPERTS]
            xnt_ps = bank7[:, 0:DIM].rearrange("p (c t) -> p c t", c=CH)
            q_ps = bank7[:, 0:DIM]
            up_ps = bank7[:, 0:2 * INNER]
            down_ps = bank6[:, 0:DIM]

            ld_x, ld_ctx, ld_xres, v2_in, st_x1, st_x2t, sc_out = (
                [asem(f"{n}{k}") for k in range(2)]
                for n in ("ld_x", "ld_ctx", "ld_xres", "v2_in", "st_x1", "st_x2t", "sc_out"))
            ld_raw = [asem(f"ld_raw{k}") for k in range(2)]
            down_psum, down_kept, up_psum, up_kept = (asem(n) for n in ("down_psum", "down_kept", "up_psum", "up_kept"))
            st_fill = asem("st_fill")
            rows_done = asem("rows_done")
            ld_first, ld_next, ld_then, ld_shared = (
                asem(n) for n in ("ld_first", "ld_next", "ld_then", "ld_shared"))
            set_up = asem("set_up")
            bias_psum, bo_done = asem("bias_psum"), asem("bo_done")
            halves_done = asem("halves_done")
            sh_psum = asem("sh_psum")
            preset = asem("preset")
            ln1_st, ln1_mv, ln1_ve, ln1_rstd, xn1_done = (asem(n) for n in ("ln1_st", "ln1_mv", "ln1_ve", "ln1_rstd", "xn1_done"))
            xnt_psum, xnt_done, q_psum, kv_psum = (asem(n) for n in ("xnt_psum", "xnt_done", "q_psum", "kv_psum"))
            qb_done, kb_done, v_done, ssq_done, msq_done, rqk_done, kn_done = (
                asem(n) for n in ("qb_done", "kb_done", "v_done", "ssq_done", "msq_done", "rqk_done", "kn_done"))
            qkt_psum, ktm_done, s_psum, smax_done, ssub_done, prob_done = (
                asem(n) for n in ("qkt_psum", "ktm_done", "s_psum", "smax_done", "ssub_done", "prob_done"))
            pt_psum, pt0_done, pt1_done, o_psum, rsum_done, on_done, ot_psum, ot_done, y_psum, xrb_done, x1_done = (
                asem(n) for n in ("pt_psum", "pt0_done", "pt1_done", "o_psum", "rsum_done", "on_done", "ot_psum", "ot_done",
                                  "y_psum", "xrb_done", "x1_done"))
            ln2_st, ln2_mv, ln2_ve, ln2_rstd, xn2_done, x2t_psum, x2t_done = (
                asem(n) for n in ("ln2_st", "ln2_mv", "ln2_ve", "ln2_rstd", "xn2_done", "x2t_psum", "x2t_done"))
            rgu_psum, rgu_done, top_done, ntop_done, topi_done, topif_done, gexp_done, wden_done = (
                asem(n) for n in ("rgu_psum", "rgu_done", "top_done", "ntop_done", "topi_done",
                                  "topif_done", "gexp_done", "wden_done"))
            chosen_done, member_done, r_psum, rowof_done, picked_done, slotf_done, sloti_done, free_done = (
                asem(n) for n in ("chosen_done", "member_done", "r_psum", "rowof_done", "picked_done",
                                  "slotf_done", "sloti_done", "free_done"))
            STEPS = TILES + 6
            LEAD = 8

            x_t = a["x"].rearrange("(t p) d -> t p d", p=P)
            ctx_t = a["ctxt"].rearrange("p c (t k) -> t p c k", k=P)

            def run(eng, body):
                pipeline(eng, LEAD, TILES, STEPS, 2, body)

            KT = -(-ETILES // P)
            total_f = asb("total_f", [P, EXPERTS])
            total_i = asb("total_i", [P, EXPERTS], I32)
            tiles_i = asb("tiles_i", [P, EXPERTS], I32)
            tiles_f = asb("tiles_f", [P, EXPERTS])
            ends = asb("ends", [P, EXPERTS])
            tile_no = asb("tile_no", [P, KT])
            over = asb("over", [P, KT, EXPERTS])
            skipped = asb("skipped", [P, KT, EXPERTS])
            owner = asb("owner", [P, KT])
            start = asb("start", [P, KT])
            row = asb("row", [P, KT])
            found = asb("found", [P, 2, KT])
            ld_no, counts_done, found_done, found_psum = (
                asem(n) for n in ("ld_no", "counts_done", "found_done", "found_psum"))
            chain = asem("chain")
            tail_out = [asem(f"tail_out{k}") for k in range(3)]

            def at_step(s, n):
                return isinstance(s, int) and s == n

            with nc.Block() as block:
                def tails(eng, engine, first, count, out):
                    eng.wait_ge(counts_done, 1)

                    def tail(g, ph):
                        free = entries(engine, counts, g * GROUP + first, GROUP, DUMP - P,
                                       "a region's base and at most TOKENS tokens")
                        for k in range(GROUP):
                            dst = xs_d[bass.ds(free[k], P), :].rearrange("(a b) d -> a (b d)", a=16)
                            eng.dma_start(dst, at(a["tails"], g * GROUP + (first + k))).then_inc(out, 16)
                    pipeline(eng, 1, count // GROUP, count // GROUP, 1, tail)

                @block.sync
                def _(sp):
                    def constants(loads, done):
                        for tile, name in loads:
                            src = a[name].broadcast_to([P, DIM]) if name in ("bq", "bk", "bo") else a[name]
                            sp.dma_start(tile[:], src).then_inc(done, 16)

                    def body(s, ph):
                        i, b = s, ph % 2
                        if live(i, TILES):
                            if past(i, 2):
                                sp.wait_ge(xn1_done, i - 1)
                            sp.dma_start(xin[:, b, :], at(x_t, i)).then_inc(ld_x[b], 16)
                        if at_step(s, 0):
                            constants(loads_first, ld_first)
                        if live(i, TILES):
                            if past(i, 2):
                                sp.wait_ge(kv_psum, i - 1)
                            src = ctx_t[i] if isinstance(i, int) else \
                                ctx_t[bass.ds(i, 1), :, :, :].rearrange("t p c k -> (t p) c k")
                            sp.dma_start(ctxt[:, b, :, :], src).then_inc(ld_ctx[b], 16)
                        if at_step(s, 0):
                            constants(loads_next, ld_next)
                        i, b = s - 2, ph % 2
                        if live(i, TILES):
                            if past(i, 2):
                                sp.wait_ge(xrb_done, i - 1)
                            sp.dma_start(xres[:, b, :], at(x_t, i)).then_inc(ld_xres[b], 16)
                        i, b = s - 4, ph % 2
                        if live(i, TILES):
                            sp.wait_ge(x1_done, i + 1)
                            sp.dma_start(at(x1_d, i), x1[:, b, :]).then_inc(st_x1[b], 16)
                        i, b = s - 2, ph % 2
                        if live(i, TILES):
                            sp.wait_ge(v_done, i + 1)
                            if past(i, 2):
                                sp.wait_ge(o_psum, i - 1)
                            for n in range(2):
                                for r in range(2):
                                    sp.dma_start(v2[SEQ * r:SEQ * (r + 1), b, n, r, :, :],
                                                 v17[SEQ * n:SEQ * (n + 1), b, r, :, :]).then_inc(v2_in[b], 16)
                        i, b = s - 4, ph % 2
                        if live(i, TILES):
                            sp.wait_ge(x2t_done, i + 1)
                            sp.dma_start(at(xn2t_d, i), xn2t[:, b, :, :].rearrange("p c t -> p (c t)"))\
                                .then_inc(st_x2t[b], 16)
                        e, b = s, ph % 2
                        if live(e, EXPERTS):
                            if past(e, 2):
                                sp.wait_ge(up_psum, e - 1)
                            sp.dma_start(raw[:, b, :], at(a["raw"], e)).then_inc(ld_raw[b], 16)
                        if at_step(s, 0):
                            constants(loads_then, ld_then)
                        if at_step(s, TILES):
                            sp.dma_start(sraw[:, :], a["sraw"]).then_inc(ld_shared, 16)
                            sp.dma_start(srgu_w[:], a["srgu"]).then_inc(ld_shared, 16)
                            sp.dma_start(srd_w[:, 0:2, :], a["srd"][0:2 * P].rearrange("(c p) r -> p c r", p=P))\
                                .then_inc(ld_shared, 16)
                            sp.dma_start(srd_w[0:SLAST, 2, :], a["srd"][2 * P:SHARED]).then_inc(ld_shared, 16)
                        if isinstance(s, int) and TILES <= s < TILES + 4:
                            n = SPARE * P // 4
                            k = s - TILES
                            sp.dma_start(xs_d[DUMP + k * n:DUMP + (k + 1) * n, :], a["spare"][k * n:(k + 1) * n])\
                                .then_inc(st_fill, 16)
                    sp.dma_start(tile_no[:, :], a["tileno"]).then_inc(ld_no, 16)
                    run(sp, body)
                    tails(sp, mybir.EngineType.SP, 0, 3 * GROUP, tail_out[0])
                    sp.wait_ge(tail_out[0], 16 * 3 * GROUP)
                    sp.wait_ge(st_fill, 16 * 4)
                    sp.wait_ge(ld_shared, 4 * 16)
                    for k in range(2):
                        sp.wait_ge(st_x1[k], 16 * TILES // 2)
                        sp.wait_ge(st_x2t[k], 16 * TILES // 2)

                @block.tensor
                def _(pe):
                    def rank(s, ph):
                        i, b = s - 5, (ph - 5) % 2
                        if not live(i, TILES):
                            return
                        if live(s - 3, TILES):
                            pe.wait_ge(on_done, s - 2)
                        pe.wait_ge(member_done, i + 1)
                        nc.tensor.matmul(r_ps, tri_h[:, :], member[:, b, :], start=True, stop=True)
                        nc.tensor.matmul(c_ps, ones_h[:, :], member[:, b, :], start=True, stop=True).then_inc(r_psum, 1)

                    def p_turn(s, ph, r):
                        i, b = s - 3, (ph - 3) % 2
                        if not live(i, TILES):
                            return
                        if r == 0:
                            pe.wait_ge(prob_done, i + 1)
                            if past(i, 1):
                                pe.wait_ge(x1_done, i)
                        else:
                            pe.wait_ge(pt0_done, i + 1)
                        for k in range(4):
                            blk = 4 * r + k
                            m = nc.tensor.transpose(pt_ps[:, k, :], prob[:, b, blk, :], ident[:, :])
                        m.then_inc(pt_psum, 1)

                    def p_times_v(s, ph):
                        i, b = s - 3, (ph - 3) % 2
                        if not live(i, TILES):
                            return
                        pe.wait_ge(pt1_done, i + 1)
                        if live(s - 6, TILES):
                            pe.wait_ge(free_done, s - 4)
                        pe.wait_ge(v2_in[b], landed(i, 2, b, 64))
                        for blk in range(PAIRS):
                            group, c, hp = blk // 4, blk // 2 % 2, blk % 2
                            pair = PAIRS // CH * c + GH // 2 * group + hp
                            for n in range(2):
                                m = nc.tensor.matmul(o_ps[SEQ * n:SEQ * (n + 1), pair, :, :],
                                                     probt[:, b, blk, SEQ * n:SEQ * (n + 1)],
                                                     v2[:, b, n, :, pair, :], start=True, stop=True)
                        m.then_inc(o_psum, 1)

                    def x_turn(s, ph):
                        i, b = s - 1, (ph - 1) % 2
                        if not live(i, TILES):
                            return
                        pe.wait_ge(xn1_done, i + 1)
                        if live(s - 2, EXPERTS):
                            pe.wait_ge(up_kept, s - 1)
                        for c in range(CH):
                            m = nc.tensor.transpose(xnt_ps[:, c, :], xn1[:, b, c * P:(c + 1) * P], ident[:, :])
                        m.then_inc(xnt_psum, 1)

                    def q_in(s, ph):
                        i, b = s - 1, (ph - 1) % 2
                        if not live(i, TILES):
                            return
                        pe.wait_ge(xnt_done, i + 1)
                        for c in range(CH):
                            m = nc.tensor.matmul(q_ps, xn1t[:, b, c, :], wq[:, c, :], start=(c == 0), stop=(c == CH - 1))
                        m.then_inc(q_psum, 1)

                    def kv_in(s, ph):
                        i, b = s - 1, (ph - 1) % 2
                        if not live(i, TILES):
                            return
                        if at_step(s, 1):
                            pe.wait_ge(ld_next, 16 * len(loads_next))
                        if past(i, 1):
                            pe.wait_ge(kb_done, i)
                            pe.wait_ge(v_done, i)
                        pe.wait_ge(ld_ctx[b], landed(i, 2, b))
                        for c in range(CH):
                            m = nc.tensor.matmul(kv_ps, ctxt[:, b, c, :], wkv[:, c, :], start=(c == 0), stop=(c == CH - 1))
                        m.then_inc(kv_psum, 1)

                    def qk_turn(s, ph):
                        i, b = s - 2, ph % 2
                        if not live(i, TILES):
                            return
                        pe.wait_ge(qb_done, i + 1)
                        pe.wait_ge(kn_done, i + 1)
                        for c in range(CH):
                            nc.tensor.transpose(qkt_ps[:, c, :], qb[:, b, c * P:(c + 1) * P], ident[:, :])
                        for c in range(CH):
                            m = nc.tensor.transpose(qkt_ps[:, CH + c, :], kb[:, b, c * P:(c + 1) * P], ident[:, :])
                        m.then_inc(qkt_psum, 1)

                    def scores_ready(s, ph):
                        i = s - 2
                        if not live(i, TILES):
                            return
                        pe.wait_ge(ktm_done, i + 1)
                        if past(i, 1):
                            pe.wait_ge(ssub_done, i)

                    def scores(s, ph):
                        i, b = s - 2, ph % 2
                        if not live(i, TILES):
                            return
                        for c in range(CH):
                            for n in range(2):
                                for g in range(GROUPS):
                                    feats = slice(64 * g, 64 * (g + 1))
                                    m = nc.tensor.matmul(s_ps[SEQ * n:SEQ * (n + 1), g, c * 256:(c + 1) * 256],
                                                         qt[feats, b, c, SEQ * n:SEQ * (n + 1)],
                                                         ktm[feats, b, 2 * c + n, :, :], start=True, stop=True)
                        m.then_inc(s_psum, 1)

                    def x2_turn(s, ph):
                        i, b = s - 4, ph % 2
                        if not live(i, TILES):
                            return
                        pe.wait_ge(xn2_done, i + 1)
                        if past(i, 1):
                            pe.wait_ge(rgu_done, i)
                        if live(s - 1, EXPERTS):
                            pe.wait_ge(down_kept, s)
                        for c in range(CH):
                            m = nc.tensor.transpose(x2t_ps[:, c * P:(c + 1) * P], xn2[:, b, c * P:(c + 1) * P], ident[:, :])
                        m.then_inc(x2t_psum, 1)

                    def rgu_in(s, ph):
                        i, b = s - 4, ph % 2
                        if not live(i, TILES):
                            return
                        pe.wait_ge(x2t_done, i + 1)
                        for c in range(CH):
                            m = nc.tensor.matmul(rgl_ps, xn2t[:, b, c, :], rgu_w[:, c, :], start=(c == 0), stop=(c == CH - 1))
                        m.then_inc(rgu_psum, 1)

                    def o_turn(s, ph):
                        i, b = s - 3, (ph - 3) % 2
                        if not live(i, TILES):
                            return
                        pe.wait_ge(on_done, i + 1)
                        for c in range(CH):
                            m = nc.tensor.transpose(pt_ps[:, c, :], on[:, b, c * P:(c + 1) * P], ident[:, :])
                        m.then_inc(ot_psum, 1)

                    def project(s, ph):
                        i, b = s - 3, (ph - 3) % 2
                        if not live(i, TILES):
                            return
                        pe.wait_ge(ot_done, i + 1)
                        for c in range(CH):
                            m = nc.tensor.matmul(y_ps, ot[:, b, c, :], wo[:, c, :], start=(c == 0), stop=(c == CH - 1))
                        m.then_inc(y_psum, 1)

                    def down_product(s, ph):
                        e, b = s - 1, (ph - 1) % 2
                        if not live(e, EXPERTS):
                            return
                        if live(s - 5, TILES):
                            pe.wait_ge(rgu_done, s - 4)
                        pe.wait_ge(ld_raw[b], landed(e, 2, b))
                        nc.tensor.matmul(down_ps, raw[:, b, o_ud:o_ud + RANK], raw[:, b, o_cd:o_cd + DIM],
                                         start=True, stop=True).then_inc(down_psum, 1)

                    def up_products(s, ph):
                        e, b = s - 1, (ph - 1) % 2
                        if not live(e, EXPERTS):
                            return
                        if live(s - 1, TILES):
                            pe.wait_ge(qb_done, s)
                        nc.tensor.matmul(up_ps[:, 0:INNER], raw[:, b, o_ug:o_ug + RANK],
                                         raw[:, b, o_cg:o_cg + INNER], start=True, stop=True)
                        nc.tensor.matmul(up_ps[:, INNER:2 * INNER], raw[:, b, o_uu:o_uu + RANK],
                                         raw[:, b, o_cu:o_cu + INNER], start=True, stop=True).then_inc(up_psum, 1)

                    def bias_product():
                        pe.wait_ge(set_up, 2 + CH)
                        pe.wait_ge(ld_then, 16 * len(loads_then))
                        for c in range(CH):
                            m = nc.tensor.matmul(bank4[:, 0:DIM], bv_cols[:, c, :], wo[:, c, :],
                                                 start=(c == 0), stop=(c == CH - 1))
                        m.then_inc(bias_psum, 1)

                    def body(s, ph):
                        if at_step(s, 1):
                            pe.wait_ge(ld_first, 16 * len(loads_first))
                        if at_step(s, 3):
                            pe.wait_ge(bo_done, 1)
                            pe.wait_ge(halves_done, 2)
                        x_turn(s, ph)
                        down_product(s, ph)
                        qk_turn(s, ph)
                        p_turn(s, ph, 0)
                        q_in(s, ph)
                        p_turn(s, ph, 1)
                        kv_in(s, ph)
                        scores_ready(s, ph)
                        x2_turn(s, ph)
                        scores(s, ph)
                        p_times_v(s, ph)
                        rgu_in(s, ph)
                        o_turn(s, ph)
                        up_products(s, ph)
                        rank(s, ph)
                        project(s, ph)
                        if at_step(s, 2):
                            bias_product()
                    run(pe, body)

                    pe.wait_ge(rgu_done, TILES)
                    pe.wait_ge(found_done, 1)
                    for k in range(2 * KT):
                        m = nc.tensor.matmul(bank6[0:1, k * P:(k + 1) * P], found[:, k // KT, k % KT].unsqueeze(1),
                                             ident[:, :], start=True, stop=True)
                    m.then_inc(found_psum, 1)
                    pe.wait_ge(ld_shared, 4 * 16)
                    nc.tensor.matmul(bank03[:, 0, 0:SHARED], sraw[:, s_ug:s_ug + RANK], sraw[:, s_cg:s_cg + SHARED],
                                     start=True, stop=True)
                    nc.tensor.matmul(bank03[:, 1, 0:SHARED], sraw[:, s_uu:s_uu + RANK], sraw[:, s_cu:s_cu + SHARED],
                                     start=True, stop=True)
                    nc.tensor.matmul(bank03[:, 2, 0:DIM], sraw[:, s_ud:s_ud + RANK], sraw[:, s_cd:s_cd + DIM],
                                     start=True, stop=True).then_inc(sh_psum, 1)

                @block.scalar
                def _(act):
                    act.wait_ge(preset, 3)

                    def p_keep(s, ph, r, done):
                        i, b = s - 3, (ph - 3) % 2
                        if not live(i, TILES):
                            return
                        act.wait_ge(pt_psum, 2 * i + r + 1)
                        nc.scalar.activation(probt[:, b, 4 * r:4 * r + 4, :], pt_ps, ACT.Copy).then_inc(done, 1)

                    def body(s, ph):
                        if at_step(s, 2):
                            act.wait_ge(set_up, 2 + CH)
                        i, b = s - 1, (ph - 1) % 2
                        if live(i, TILES):
                            act.wait_ge(xnt_psum, i + 1)
                            nc.scalar.activation(xn1t[:, b, :, :], xnt_ps, ACT.Copy).then_inc(xnt_done, 1)
                        e = s - 1
                        if live(e, EXPERTS):
                            act.wait_ge(down_psum, e + 1)
                        i, b = s - 2, ph % 2
                        if live(i, TILES):
                            act.wait_ge(qkt_psum, i + 1)
                            for c in range(CH):
                                nc.scalar.activation(qt[:, b, c, :], qkt_ps[:, c, :], ACT.Copy,
                                                     scale=gqk[:, c:c + 1])
                        p_keep(s, ph, 0, pt0_done)
                        i, b = s - 2, ph % 2
                        if live(i, TILES):
                            kt = qkt_ps[:, CH:2 * CH, :].rearrange("p c (n k) -> p (c n) k", n=2)
                            for g in range(GH):
                                m = nc.scalar.activation(ktm[:, b, :, g, :], kt, ACT.Copy, scale=headmask[:, g:g + 1])
                            m.then_inc(ktm_done, 1)
                        p_keep(s, ph, 1, pt1_done)
                        if live(e, EXPERTS):
                            nc.scalar.activation(col(down_w, e), down_ps, ACT.Copy).then_inc(down_kept, 1)
                        i, b = s - 4, ph % 2
                        if live(i, TILES):
                            act.wait_ge(x2t_psum, i + 1)
                            if past(i, 2):
                                act.wait_ge(st_x2t[b], landed(i, 2, b) - 16)
                            nc.scalar.activation(xn2t[:, b, :, :].rearrange("p c t -> p (c t)"), x2t_ps,
                                                 ACT.Copy).then_inc(x2t_done, 1)
                        i, b = s - 1, (ph - 1) % 2
                        if live(i, TILES):
                            act.wait_ge(qb_done, i + 1)
                            if past(i, 1):
                                act.wait_ge(ssq_done, 2 * i)
                            nc.scalar.activation(squares[:, :], qb[:, b, :], ACT.Square,
                                                 accum_out=ssq[:, b, 0:1]).then_inc(ssq_done, 1)
                            act.wait_ge(kb_done, i + 1)
                            act.wait_ge(ssq_done, 2 * i + 1)
                            nc.scalar.activation(squares[:, :], kb[:, b, :], ACT.Square,
                                                 accum_out=ssq[:, b, 1:2]).then_inc(ssq_done, 1)
                            if past(i, 2):
                                act.wait_ge(v2_in[b], landed(i, 2, b, 64) - 64)
                            nc.scalar.activation(
                                v17[:, b, :, :, 0:HD],
                                kv_ps[:, DIM:2 * DIM].rearrange("p (r g d) -> p r g d", r=2, g=PAIRS),
                                ACT.Copy).then_inc(v_done, 1)
                        i, b = s - 5, (ph - 5) % 2
                        if live(i, TILES):
                            act.wait_ge(ntop_done, i + 1)
                            nc.scalar.activation(egate[:, b, :], rgl[:, b, DIM:DIM + EXPERTS], ACT.Exp, bias=ntop[:, b, :],
                                                 accum_out=zsum[:, b, 0:1]).then_inc(gexp_done, 1)
                            nc.scalar.activation(etop[:, b, :], top8[:, b, 0:TOPK], ACT.Exp, bias=ntop[:, b, :],
                                                 accum_out=zsum[:, b, 1:2]).then_inc(gexp_done, 1)
                            act.wait_ge(rgu_done, i + 1)
                            if past(i, 2):
                                act.wait_ge(sc_out[b], landed(i, 2, b, 64) - 64)
                            nc.scalar.activation(rgu[:, b, :, 0:DIM],
                                                 rgl[:, b, 0:DIM].unsqueeze(1).broadcast_to([P, TOPK, DIM]), ACT.Copy)
                            nc.scalar.activation(rgu[:, b, :, DIM:ROW].rearrange("p k o -> p (k o)"), col(names, i),
                                                 ACT.Copy).then_inc(rows_done, 1)
                        i, b = s - 3, (ph - 3) % 2
                        if live(i, TILES):
                            act.wait_ge(ot_psum, i + 1)
                            nc.scalar.activation(ot[:, b, :, :], pt_ps[:, 0:CH, :], ACT.Copy).then_inc(ot_done, 1)
                        e = s - 1
                        if live(e, EXPERTS):
                            act.wait_ge(up_psum, e + 1)
                        i, b = s - 4, ph % 2
                        if live(i, TILES):
                            act.wait_ge(rgu_psum, i + 1)
                            if past(i, 2):
                                act.wait_ge(topi_done, i - 1)
                            nc.scalar.activation(rgl[:, b, :], rgl_ps, ACT.Copy).then_inc(rgu_done, 1)
                        if live(e, EXPERTS):
                            nc.scalar.activation(col(up_w, e), up_ps, ACT.Copy).then_inc(up_kept, 1)
                        i, b = s - 2, ph % 2
                        if live(i, TILES):
                            act.wait_ge(ssub_done, i + 1)
                            pb = prob[:, b, :, :].rearrange("p q k -> p (q k)")
                            nc.scalar.activation(pb, pb, ACT.Exp, scale=rqk[:, b, 0:1]).then_inc(prob_done, 1)
                    run(act, body)
                    tails(act, mybir.EngineType.Activation, 3 * GROUP, 3 * GROUP, tail_out[1])
                    act.wait_ge(tail_out[1], 16 * 3 * GROUP)

                @block.gpsimd
                def _(pool):
                    def body(s, ph):
                        i, b = s - 6, ph % 2
                        if live(i, TILES):
                            pool.wait_ge(rows_done, i + 1)
                            pool.wait_ge(sloti_done, i + 1)
                        i, b = s - 3, (ph - 3) % 2
                        if live(i, TILES):
                            if past(i, 2):
                                pool.wait_ge(x1_done, i - 1)
                            if at_step(s, 3):
                                pool.wait_ge(bo_done, 1)
                            pool.wait_ge(ld_xres[b], landed(i, 2, b))
                            nc.gpsimd.tensor_tensor(xrb[:, b, :], xres[:, b, :], bo[:, :], ALU.add).then_inc(xrb_done, 1)
                        i, b = s - 6, ph % 2
                        if live(i, TILES):
                            for k in range(TOPK):
                                nc.gpsimd.indirect_dma_start(
                                    xs_d, bass.IndirectOffsetOnAxis(sloti[:, b, k:k + 1], 0), rgu[:, b, k, :], None)\
                                    .then_inc(sc_out[b], 16)
                        i, b = s, ph % 2
                        if live(i, TILES):
                            pool.wait_ge(preset, 3)
                            pool.wait_ge(ln1_ve, i + 1)
                            nc.gpsimd.tensor_tensor(rstd1[:, b, :], mean1[:, b, 1:2], mhalf[:, 0:1], ALU.pow)\
                                .then_inc(ln1_rstd, 1)
                        i, b = s - 1, (ph - 1) % 2
                        if live(i, TILES):
                            pool.wait_ge(msq_done, i + 1)
                            nc.gpsimd.tensor_tensor(rqk[:, b, :], ssq[:, b, :], mhalf[:, :], ALU.pow).then_inc(rqk_done, 1)
                        i, b = s - 3, (ph - 3) % 2
                        if live(i, TILES):
                            pool.wait_ge(ln2_ve, i + 1)
                            nc.gpsimd.tensor_tensor(rstd2[:, b, :], mean2[:, b, 1:2], mhalf[:, 0:1], ALU.pow)\
                                .then_inc(ln2_rstd, 1)
                    run(pool, body)
                    tails(pool, mybir.EngineType.Pool, 6 * GROUP, EXPERTS - 6 * GROUP, tail_out[2])
                    pool.wait_ge(tail_out[2], 16 * (EXPERTS - 6 * GROUP))
                    for k in range(2):
                        pool.wait_ge(sc_out[k], 16 * TOPK * TILES // 2)

                @block.vector
                def _(dve):
                    nc.vector.memset(mhalf[:, :], -0.5).then_inc(preset, 1)
                    nc.vector.memset(v17[:, :, :, :, :], 1.0).then_inc(preset, 1)
                    nc.vector.memset(v2[:, :, :, :, :, :], 0.0).then_inc(preset, 1)

                    def rank_keep(s, ph):
                        i, b = s - 5, (ph - 5) % 2
                        if not live(i, TILES):
                            return
                        dve.wait_ge(r_psum, i + 1)
                        dve.wait_ge(free_done, i + 1)
                        nc.vector.tensor_tensor(rowof[:, b, :], r_ps, free[:, :], ALU.add).then_inc(rowof_done, 1)
                        nc.vector.tensor_tensor(free[:, :], c_ps, free[:, :], ALU.add).then_inc(free_done, 1)

                    def slot_rows(s, ph):
                        i, b = s - 5, (ph - 5) % 2
                        if not live(i, TILES):
                            return
                        dve.wait_ge(rowof_done, i + 1)
                        nc.vector.tensor_tensor(picked[:, b, :, :], chosen[:, b, :, :],
                                                rowof[:, b, :].unsqueeze(1).broadcast_to([P, TOPK, EXPERTS]),
                                                ALU.mult).then_inc(picked_done, 1)
                        dve.wait_ge(picked_done, i + 1)
                        nc.vector.tensor_reduce(slotf[:, b, :], picked[:, b, :, :], AX.X, ALU.add).then_inc(slotf_done, 1)
                        dve.wait_ge(slotf_done, i + 1)
                        if past(i, 2):
                            dve.wait_ge(sc_out[b], landed(i, 2, b, 64) - 64)
                        nc.vector.tensor_copy(sloti[:, b, :], slotf[:, b, :]).then_inc(sloti_done, 1)

                    def norm1_stats(s, ph):
                        i, b = s, ph % 2
                        if not live(i, TILES):
                            return
                        dve.wait_ge(ld_x[b], landed(i, 2, b))
                        nc.vector.bn_stats(stats[:, b, :], xin[:, b, :]).then_inc(ln1_st, 1)

                    def norm1_mean(s, ph):
                        i, b = s, ph % 2
                        if live(i, TILES):
                            dve.wait_ge(ln1_st, i + 1)
                        q_bias(s, ph)
                        if not live(i, TILES):
                            return
                        nc.vector.bn_aggr(mean1[:, b, :], stats[:, b, :]).then_inc(ln1_mv, 1)
                        dve.wait_ge(ln1_mv, i + 1)
                        nc.vector.tensor_scalar(mean1[:, b, 1:2], mean1[:, b, 1:2], LN_EPS, None, ALU.add)\
                            .then_inc(ln1_ve, 1)

                    def norm1(s, ph):
                        i, b = s, ph % 2
                        if not live(i, TILES):
                            return
                        dve.wait_ge(ln1_rstd, i + 1)
                        nc.vector.tensor_scalar(xn1[:, b, :], xin[:, b, :], mean1[:, b, 0:1], rstd1[:, b, :],
                                                ALU.subtract, ALU.mult).then_inc(xn1_done, 1)

                    def soft_max(s, ph):
                        i, b = s - 2, ph % 2
                        if not live(i, TILES):
                            return
                        dve.wait_ge(s_psum, i + 1)
                        sv = s_ps.rearrange("p g (h k) -> p (g h) k", k=SEQ)
                        mv = smax[:, b, :, :].rearrange("p g h -> p (g h)")
                        nc.vector.tensor_reduce(mv, sv, AX.X, ALU.max).then_inc(smax_done, 1)

                    def soft(s, ph):
                        i, b = s - 2, ph % 2
                        if not live(i, TILES):
                            return
                        sv = s_ps.rearrange("p g (h k) -> p (g h) k", k=SEQ)
                        mv = smax[:, b, :, :].rearrange("p g h -> p (g h)")
                        dve.wait_ge(smax_done, i + 1)
                        nc.vector.tensor_tensor(
                            prob[:, b, :, :].rearrange("p q (r k) -> p (q r) k", r=2), sv,
                            mv.unsqueeze(2).broadcast_to([P, HEADS, SEQ]), ALU.subtract).then_inc(ssub_done, 1)

                    def q_bias(s, ph):
                        i, b = s - 1, (ph - 1) % 2
                        if not live(i, TILES):
                            return
                        dve.wait_ge(q_psum, i + 1)
                        nc.vector.tensor_tensor(qb[:, b, :], q_ps, bq[:, :], ALU.add).then_inc(qb_done, 1)

                    def k_bias(s, ph):
                        i, b = s - 1, (ph - 1) % 2
                        if not live(i, TILES):
                            return
                        if at_step(s, 1):
                            dve.wait_ge(ld_next, 16 * len(loads_next))
                        dve.wait_ge(kv_psum, i + 1)
                        nc.vector.tensor_tensor(kb[:, b, :], kv_ps[:, 0:DIM], bk[:, :], ALU.add).then_inc(kb_done, 1)

                    def o_norm(s, ph):
                        i, b = s - 3, (ph - 3) % 2
                        if not live(i, TILES):
                            return
                        dve.wait_ge(o_psum, i + 1)
                        nc.vector.reciprocal(rsum[:, b, :, :], o_ps[:, :, :, HD]).then_inc(rsum_done, 1)
                        dve.wait_ge(rsum_done, i + 1)
                        ov = on[:, b, :].rearrange("p (g r d) -> p (g r) d", g=PAIRS, r=2)
                        nc.vector.tensor_tensor(
                            ov, o_ps[:, :, :, 0:HD].rearrange("p g r d -> p (g r) d"),
                            rsum[:, b, :, :].rearrange("p g r -> p (g r)").unsqueeze(2).broadcast_to([P, HEADS, HD]),
                            ALU.mult).then_inc(on_done, 1)

                    def mean_square(s, ph):
                        i, b = s - 1, (ph - 1) % 2
                        if not live(i, TILES):
                            return
                        dve.wait_ge(ssq_done, 2 * i + 2)
                        nc.vector.tensor_scalar(ssq[:, b, :], ssq[:, b, :], 1.0 / DIM, RMS_EPS, ALU.mult, ALU.add)\
                            .then_inc(msq_done, 1)

                    def k_norm(s, ph):
                        i, b = s - 1, (ph - 1) % 2
                        if not live(i, TILES):
                            return
                        dve.wait_ge(rqk_done, i + 1)
                        nc.vector.tensor_scalar(kb[:, b, :], kb[:, b, :], rqk[:, b, 1:2], None, ALU.mult)\
                            .then_inc(kn_done, 1)

                    def gate_top(s, ph):
                        i, b = s - 4, ph % 2
                        if not live(i, TILES):
                            return
                        dve.wait_ge(rgu_done, i + 1)
                        rank_keep(s, ph)
                        logits = rgl[:, b, DIM:DIM + EXPERTS]
                        nc.vector.max(top8[:, b, :], logits).then_inc(top_done, 1)
                        dve.wait_ge(top_done, i + 1)
                        nc.vector.tensor_scalar(ntop[:, b, :], top8[:, b, 0:1], -1.0, None, ALU.mult).then_inc(ntop_done, 1)
                        nc.vector.max_index(top8i[:, b, :], top8[:, b, :], logits).then_inc(topi_done, 1)

                    def choose(s, ph):
                        i, b = s - 4, ph % 2
                        j, d = s - 3, (ph - 3) % 2
                        if live(j, TILES):
                            dve.wait_ge(ln2_st, j + 1)
                        if live(i, TILES):
                            dve.wait_ge(topi_done, i + 1)
                            nc.vector.tensor_copy(topif[:, b, :], top8i[:, b, 0:TOPK]).then_inc(topif_done, 1)
                        if live(j, TILES):
                            nc.vector.bn_aggr(mean2[:, d, :], stats2[:, d, :]).then_inc(ln2_mv, 1)
                        if live(i, TILES):
                            dve.wait_ge(topif_done, i + 1)
                            nc.vector.tensor_tensor(chosen[:, b, :, :],
                                                    eiota[:, :].unsqueeze(1).broadcast_to([P, TOPK, EXPERTS]),
                                                    topif[:, b, :].unsqueeze(2).broadcast_to([P, TOPK, EXPERTS]),
                                                    ALU.is_equal).then_inc(chosen_done, 1)
                        if live(j, TILES):
                            dve.wait_ge(ln2_mv, j + 1)
                            nc.vector.tensor_scalar(mean2[:, d, 1:2], mean2[:, d, 1:2], LN_EPS, None, ALU.add)\
                                .then_inc(ln2_ve, 1)
                        if live(i, TILES):
                            dve.wait_ge(chosen_done, i + 1)
                            nc.vector.tensor_reduce(member[:, b, :], chosen[:, b, :, :].rearrange("p k e -> p e k"),
                                                    AX.X, ALU.max).then_inc(member_done, 1)

                    def gate_weights(s, ph):
                        i, b = s - 5, (ph - 5) % 2
                        if not live(i, TILES):
                            return
                        dve.wait_ge(gexp_done, 2 * i + 2)
                        nc.vector.scalar_tensor_tensor(out=wden[:, b, 0:1], in0=zsum[:, b, 0:1], scalar=1e-20,
                                                       in1=zsum[:, b, 1:2], op0=ALU.mult, op1=ALU.add)\
                            .then_inc(wden_done, 1)
                        dve.wait_ge(wden_done, 2 * i + 1)
                        nc.vector.reciprocal(wden[:, b, 1:2], wden[:, b, 0:1]).then_inc(wden_done, 1)
                        dve.wait_ge(wden_done, 2 * i + 2)
                        nc.vector.tensor_scalar(col(weights, i), etop[:, b, :], wden[:, b, 1:2], None, ALU.mult)

                    def residual(s, ph):
                        i, b = s - 3, (ph - 3) % 2
                        if not live(i, TILES):
                            return
                        dve.wait_ge(y_psum, i + 1)
                        dve.wait_ge(xrb_done, i + 1)
                        if past(i, 2):
                            dve.wait_ge(st_x1[b], landed(i, 2, b) - 16)
                        nc.vector.tensor_tensor(x1[:, b, :], y_ps, xrb[:, b, :], ALU.add).then_inc(x1_done, 1)
                        dve.wait_ge(x1_done, i + 1)
                        nc.vector.bn_stats(stats2[:, b, :], x1[:, b, :]).then_inc(ln2_st, 1)

                    def norm2(s, ph):
                        i, b = s - 3, (ph - 3) % 2
                        if not live(i, TILES):
                            return
                        dve.wait_ge(ln2_rstd, i + 1)
                        nc.vector.tensor_scalar(xn2[:, b, :], x1[:, b, :], mean2[:, b, 0:1], rstd2[:, b, :],
                                                ALU.subtract, ALU.mult).then_inc(xn2_done, 1)

                    def set_up_biases():
                        dve.wait_ge(ld_next, 16 * len(loads_next))
                        nc.vector.tensor_tensor(gqk[:, :], gq[:, :], gk[:, :], ALU.mult).then_inc(set_up, 1)
                        dve.wait_ge(set_up, 1)
                        nc.vector.tensor_scalar(gqk[:, :], gqk[:, :], float(HD) ** -0.5, None, ALU.mult)\
                            .then_inc(set_up, 1)
                        for c in range(CH):
                            nc.vector.tensor_scalar(bv_cols[:, c, :], ones[:, :], bv[:, c:c + 1], None, ALU.mult)\
                                .then_inc(set_up, 1)

                    def body(s, ph):
                        if at_step(s, 1):
                            dve.wait_ge(ld_first, 16 * len(loads_first))
                        if at_step(s, 2):
                            set_up_biases()
                        if at_step(s, 3):
                            dve.wait_ge(ld_then, 16 * len(loads_then))
                            nc.vector.tensor_copy(tri_h[:, :], tri[:, :]).then_inc(halves_done, 1)
                            nc.vector.tensor_copy(ones_h[:, :], ones[:, :]).then_inc(halves_done, 1)
                            nc.vector.tensor_copy(free[:, :], ebase[:, :]).then_inc(free_done, 1)
                            dve.wait_ge(bias_psum, 1)
                            nc.vector.tensor_tensor(bo[:, :], bank4[:, 0:DIM], bo[:, :], ALU.add).then_inc(bo_done, 1)
                        norm1_stats(s, ph)
                        norm1_mean(s, ph)
                        k_bias(s, ph)
                        soft_max(s, ph)
                        mean_square(s, ph)
                        o_norm(s, ph)
                        soft(s, ph)
                        norm1(s, ph)
                        k_norm(s, ph)
                        gate_top(s, ph)
                        if not live(s - 4, TILES):
                            rank_keep(s, ph)
                        residual(s, ph)
                        choose(s, ph)
                        gate_weights(s, ph)
                        norm2(s, ph)
                        slot_rows(s, ph)
                    run(dve, body)

                    done = [0]

                    def step(ins):
                        ins.then_inc(chain, 1)
                        done[0] += 1
                        dve.wait_ge(chain, done[0])
                    step(nc.vector.memset(table[:, :, :], 0))
                    dve.wait_ge(ld_no, 16)
                    dve.wait_ge(free_done, TILES + 1)
                    nc.vector.tensor_copy(counts[:, :], free[0:1, :]).then_inc(counts_done, 1)
                    step(nc.vector.tensor_tensor(total_f[:, :], free[:, :], ebase[:, :], ALU.subtract))
                    step(nc.vector.tensor_scalar(total_f[:, :], total_f[:, :], float(P - 1), None, ALU.add))
                    step(nc.vector.tensor_copy(total_i[:, :], total_f[:, :]))
                    step(nc.vector.tensor_scalar(tiles_i[:, :], total_i[:, :], 7, None, ALU.logical_shift_right))
                    step(nc.vector.tensor_copy(tiles_f[:, :], tiles_i[:, :]))
                    step(nc.vector.tensor_tensor_scan(ends[:, :], ones[:, 0:EXPERTS], tiles_f[:, :], 0.0,
                                                      ALU.mult, ALU.add))
                    shape = [P, KT, EXPERTS]
                    step(nc.vector.tensor_tensor(over[:, :, :], ends[:, :].unsqueeze(1).broadcast_to(shape),
                                                 tile_no[:, :].unsqueeze(2).broadcast_to(shape), ALU.is_le))
                    step(nc.vector.tensor_tensor(skipped[:, :, :], over[:, :, :],
                                                 tiles_f[:, :].unsqueeze(1).broadcast_to(shape), ALU.mult))
                    step(nc.vector.tensor_reduce(owner[:, :], over[:, :, :], AX.X, ALU.add))
                    step(nc.vector.tensor_reduce(start[:, :], skipped[:, :, :], AX.X, ALU.add))
                    step(nc.vector.tensor_tensor(start[:, :], tile_no[:, :], start[:, :], ALU.subtract))
                    step(nc.vector.tensor_scalar(start[:, :], start[:, :], float(P), None, ALU.mult))
                    step(nc.vector.scalar_tensor_tensor(out=row[:, :], in0=owner[:, :], scalar=float(CAP),
                                                        in1=start[:, :], op0=ALU.mult, op1=ALU.add))
                    nc.vector.tensor_scalar(found[:, 0, :], owner[:, :], float(EXPERTS - 1), None, ALU.min)
                    nc.vector.tensor_scalar(found[:, 1, :], row[:, :], float(DUMP + (SPARE - 1) * P), None,
                                            ALU.min)\
                        .then_inc(found_done, 1)
                    dve.wait_ge(found_psum, 1)
                    step(nc.vector.tensor_copy(
                        table[:, :, LOOK:LOOK + ETILES],
                        bank6[0:1, :].rearrange("p (c t) -> p c t", c=2)[:, :, 0:ETILES]))
                    nc.vector.memset(sup_w[:, :, SHARED:SPAD], 0.0)
                    dve.wait_ge(sh_psum, 1)
                    nc.vector.tensor_copy(sup_w[:, 0, 0:SHARED], bank03[:, 0, 0:SHARED])
                    nc.vector.tensor_copy(sup_w[:, 1, 0:SHARED], bank03[:, 1, 0:SHARED])
                    step(nc.vector.tensor_copy(sdown_w[:, :], bank03[:, 2, 0:DIM]))
        with ExitStack() as cx:
            def esb(name, shape, dt=F32):
                return cx.enter_context(nc.sbuf_tensor(name, shape, dt))

            def esem(name):
                return cx.enter_context(nc.semaphore(name))
            RING, AHEAD = 4, 8
            xg = esb("xg", [P, AHEAD, ROW])
            xgt = esb("xgt", [P, 2, 2, P])
            gated = esb("gated", [P, 2, INNER])
            h = esb("h", [P, 2, INNER])
            ht = esb("ht", [HALF, 2, 2, P])
            rdt = esb("rdt", [P, 2, P])
            yo = esb("yo", [P, RING, DIM])
            name_f = esb("name_f", [P, RING, 1])
            name_i = esb("name_i", [P, RING, 1], I32)
            fence = esb("fence", [P, RING])
            xgt_ps = bank03[:, 0, 0:2 * P]
            ht_ps = bank03[0:HALF, 1, 0:2 * P]
            gu_ps = [bank03[:, 2 + k, 0:2 * INNER] for k in range(2)]
            y_ps = [bank4[:, 0:DIM], bank5[:, 0:DIM]]
            rd_ps = bank6[:, 0:P]
            ld_xg = [esem(f"ld_xg{k}") for k in range(AHEAD)]
            st_y = [esem(f"st_y{k}") for k in range(RING)]
            (xgt_psum, xgt_done, gu_psum, gated_done, h_done, ht_psum, ht_done, rd_psum, rdt_done, ye_psum,
             yo_done, name_done, fenced) = (esem(n) for n in (
                 "xgt_psum", "xgt_done", "gu_psum", "gated_done", "h_done", "ht_psum", "ht_done", "rd_psum",
                 "rdt_done", "ye_psum", "yo_done", "name_done", "fenced"))
            N = ETILES
            UP, DOWN, LAG = 4, 7, 8

            def run_experts(eng, body):
                pipeline(eng, 2 * AHEAD, N, N + LAG, AHEAD, body)

            DEPTH = 4
            x2t = esb("x2t", [P, DEPTH, CH, P])
            xr1 = esb("xr1", [P, DEPTH, DIM])
            rt = esb("rt", [P, 2, 2, P])
            sg = esb("sg", [P, 2, SCH, P])
            sh = esb("sh", [P, 2, SCH, P])
            srt = esb("srt", [P, 2, P])
            wts = esb("wts", [P, DEPTH, TOPK])
            got = esb("got", [P, DEPTH, TOPK, DIM])
            scaled = esb("scaled", [P, 2, 2, DIM])
            part = esb("part", [P, 2, 2, DIM])
            acc = esb("acc", [P, 2, 3, DIM])
            rt_ps = bank03[:, 0, 0:2 * P]
            g_ps = bank03[:, 1, 0:SPAD]
            u_ps = bank03[:, 2, 0:SPAD]
            srt_ps = bank03[:, 3, 0:P]
            sy_ps = [bank7[:, 0:DIM], bank6[:, 0:DIM]]
            ld_x2t, ld_x1, ld_got, st_out = (
                [esem(f"{n}{k}") for k in range(DEPTH)] for n in ("ld_x2t", "ld_x1", "ld_got", "st_out"))
            (rt_psum, rt_done, g_psum, u_psum, sg_done, sh_done2, srt_psum, srt_done, sy_psum, sum_done,
             wts_done, scaled_done, part_done) = (esem(n) for n in (
                 "rt_psum", "rt_done", "g_psum", "u_psum", "sg_done", "sh_done2", "srt_psum", "srt_done", "sy_psum",
                 "sum_done", "wts_done", "scaled_done", "part_done"))
            out_t = a["out"].rearrange("(t p) d -> t p d", p=P)
            yt_t = yt_d.rearrange("(t p k) d -> t p (k d)", p=P, k=TOPK)

            def run_combine(eng, body):
                pipeline(eng, 2 * DEPTH, TILES, TILES + 5, 2 * DEPTH, body)

            with nc.Block() as block:
                @block.sync
                def _(sp):
                    first = [None]

                    def expert(s, ph):
                        i, b = s, ph % AHEAD
                        if live(i, N):
                            if b % RING == 0:
                                first[0] = entries(mybir.EngineType.SP, table[:, 1, :], i + LOOK, RING,
                                                   DUMP + (SPARE - 1) * P,
                                                   "clamped when the table was made")
                            if past(i, AHEAD):
                                sp.wait_ge(name_done, i - AHEAD + 1)
                            sp.dma_start(xg[:, b, :], xs_d[bass.ds(first[0][b % RING], P), :]).then_inc(ld_xg[b], 16)
                    run_experts(sp, expert)

                    def combine(s, ph):
                        i, b = s, ph % DEPTH
                        if live(i, TILES):
                            if past(i, DEPTH):
                                sp.wait_ge(rt_psum, i - DEPTH + 1)
                            sp.dma_start(x2t[:, b, :, :].rearrange("p c t -> p (c t)"), at(xn2t_d, i))\
                                .then_inc(ld_x2t[b], 16)
                        i, b = s - 2, (ph - 2) % DEPTH
                        if live(i, TILES):
                            if past(i, DEPTH):
                                sp.wait_ge(sum_done, 3 * (i - DEPTH + 1))
                            sp.dma_start(xr1[:, b, :], at(x1_d, i)).then_inc(ld_x1[b], 16)
                            if isinstance(i, int) and i == 0:
                                for k in range(RING):
                                    sp.wait_ge(st_y[k], 16 * N // RING)
                            sp.dma_start(got[:, b, :, :].rearrange("p k d -> p (k d)"), at(yt_t, i))\
                                .then_inc(ld_got[b], 16)
                        i, b = s - 4, ph % 2
                        if live(i, TILES):
                            sp.wait_ge(sum_done, 3 * (i + 1))
                            sp.dma_start(at(out_t, i), acc[:, b, 2, :]).then_inc(st_out[ph % DEPTH], 16)
                    run_combine(sp, combine)
                    for k in range(DEPTH):
                        sp.wait_ge(st_out[k], 16 * TILES // DEPTH)

                @block.tensor
                def _(pe):
                    owners = [None]

                    def expert(s, ph):
                        if ph % RING == 0:
                            owners[0] = entries(mybir.EngineType.PE, table[:, 0, :], s - DOWN + LOOK,
                                                DOWN - UP + RING, EXPERTS - 1,
                                                "clamped to the last expert when the table was made")

                        def weight(w, lag):
                            e = owners[0][DOWN - lag + ph % RING]
                            return w[:, bass.ds(e, 1), :].rearrange("p e n -> p (e n)")
                        i, b = s - DOWN, (ph - DOWN) % 2
                        if live(i, N):
                            pe.wait_ge(rdt_done, i + 1)
                            nc.tensor.matmul(y_ps[b], rdt[:, b, :], weight(down_w, DOWN), start=True, stop=True)\
                                .then_inc(ye_psum, 1)
                        i, b = s - 6, ph % 2
                        if live(i, N):
                            pe.wait_ge(ht_done, i + 1)
                            for c in range(2):
                                m = nc.tensor.matmul(rd_ps, rd_w[:, c, :], ht[:, b, c, :],
                                                     start=(c == 0), stop=(c == 1))
                            m.then_inc(rd_psum, 1)
                        i, b = s - 5, (ph - 5) % 2
                        if live(i, N):
                            pe.wait_ge(h_done, i + 1)
                            for c in range(2):
                                m = nc.tensor.transpose(ht_ps[:, c * P:(c + 1) * P],
                                                        h[:, b, c * HALF:(c + 1) * HALF], ident[:, :])
                            m.then_inc(ht_psum, 1)
                        i, b = s - UP, ph % 2
                        if live(i, N):
                            w = weight(up_w, UP)
                            pe.wait_ge(xgt_done, i + 1)
                            nc.tensor.matmul(gu_ps[b][:, 0:INNER], xgt[:, b, 0, :], w[:, 0:INNER],
                                             start=True, stop=True)
                            nc.tensor.matmul(gu_ps[b][:, INNER:2 * INNER], xgt[:, b, 1, :], w[:, INNER:2 * INNER],
                                             start=True, stop=True).then_inc(gu_psum, 1)
                        i = s - 3
                        if live(i, N):
                            b = (ph - 3) % AHEAD
                            pe.wait_ge(ld_xg[b], landed(i, AHEAD, b))
                            for c in range(2):
                                m = nc.tensor.transpose(xgt_ps[:, c * P:(c + 1) * P],
                                                        xg[:, b, c * P:(c + 1) * P], ident[:, :])
                            m.then_inc(xgt_psum, 1)
                    run_experts(pe, expert)

                    def combine(s, ph):
                        i, b = s - 4, ph % 2
                        if live(i, TILES):
                            if past(i, 2):
                                pe.wait_ge(sum_done, 3 * (i - 2) + 1)
                            pe.wait_ge(srt_done, i + 1)
                            nc.tensor.matmul(sy_ps[b], srt[:, b, :], sdown_w[:, :], start=True, stop=True)\
                                .then_inc(sy_psum, 1)
                        i, b = s - 3, (ph - 3) % 2
                        if live(i, TILES):
                            pe.wait_ge(sh_done2, i + 1)
                            for c in range(SCH):
                                k = P if c < SCH - 1 else SLAST
                                m = nc.tensor.matmul(srt_ps, srd_w[0:k, c, :], sh[0:k, b, c, :],
                                                     start=(c == 0), stop=(c == SCH - 1))
                            m.then_inc(srt_psum, 1)
                        i, b = s - 2, ph % 2
                        if live(i, TILES):
                            pe.wait_ge(rt_done, i + 1)
                            for c in range(SCH):
                                m = nc.tensor.matmul(g_ps[:, c * P:(c + 1) * P], sup_w[:, 0, c * P:(c + 1) * P],
                                                     rt[:, b, 0, :], start=True, stop=True)
                            m.then_inc(g_psum, 1)
                            for c in range(SCH):
                                m = nc.tensor.matmul(u_ps[:, c * P:(c + 1) * P], sup_w[:, 1, c * P:(c + 1) * P],
                                                     rt[:, b, 1, :], start=True, stop=True)
                            m.then_inc(u_psum, 1)
                        i, b = s - 1, (ph - 1) % 2
                        if live(i, TILES):
                            d = (ph - 1) % DEPTH
                            pe.wait_ge(ld_x2t[d], landed(i, DEPTH, d))
                            for r in range(2):
                                for c in range(CH):
                                    m = nc.tensor.matmul(rt_ps[:, r * P:(r + 1) * P], srgu_w[:, c, r, :],
                                                         x2t[:, d, c, :], start=(c == 0), stop=(c == CH - 1))
                            m.then_inc(rt_psum, 1)
                    run_combine(pe, combine)

                @block.scalar
                def _(act):
                    def expert(s, ph):
                        i, b = s - 6, ph % 2
                        if live(i, N):
                            act.wait_ge(rd_psum, i + 1)
                            nc.scalar.activation(rdt[:, b, :], rd_ps, ACT.Copy).then_inc(rdt_done, 1)
                        i, b = s - UP, ph % 2
                        if live(i, N):
                            act.wait_ge(gu_psum, i + 1)
                            nc.scalar.activation(gated[:, b, :], gu_ps[b][:, 0:INNER], ACT.Silu).then_inc(gated_done, 1)
                        i, b = s - 3, (ph - 3) % 2
                        if live(i, N):
                            act.wait_ge(xgt_psum, i + 1)
                            nc.scalar.activation(xgt[:, b, :, :].rearrange("p c t -> p (c t)"), xgt_ps, ACT.Copy)\
                                .then_inc(xgt_done, 1)
                    run_experts(act, expert)

                    def combine(s, ph):
                        i, b = s - 3, (ph - 3) % 2
                        if live(i, TILES):
                            act.wait_ge(srt_psum, i + 1)
                            nc.scalar.activation(srt[:, b, :], srt_ps, ACT.Copy).then_inc(srt_done, 1)
                        i, b = s - 2, ph % 2
                        if live(i, TILES):
                            act.wait_ge(g_psum, i + 1)
                            nc.scalar.activation(sg[:, b, :, :].rearrange("p c t -> p (c t)"), g_ps, ACT.Silu)\
                                .then_inc(sg_done, 1)
                        i, b = s - 1, (ph - 1) % 2
                        if live(i, TILES):
                            act.wait_ge(rt_psum, i + 1)
                            nc.scalar.activation(rt[:, b, :, :].rearrange("p c t -> p (c t)"), rt_ps, ACT.Copy)\
                                .then_inc(rt_done, 1)
                    run_combine(act, combine)

                @block.gpsimd
                def _(pool):
                    def expert(s, ph):
                        i, b = s - 8, ph % RING
                        if live(i, N):
                            if past(i, RING):
                                pool.wait_ge(fenced, i - RING + 1)
                            pool.wait_ge(yo_done, 2 * i + 2)
                            nc.gpsimd.tensor_tensor(fence[:, b:b + 1], ones[:, 0:1], ones[:, 0:1], ALU.mult)\
                                .then_inc(fenced, 1)
                            nc.gpsimd.indirect_dma_start(
                                yt_d, bass.IndirectOffsetOnAxis(name_i[:, b, :], 0), yo[:, b, :], None)\
                                .then_inc(st_y[b], 16)
                    run_experts(pool, expert)

                    def combine(s, ph):
                        i, b, d = s - 4, ph % 2, ph % DEPTH
                        if live(i, TILES):
                            pool.wait_ge(wts_done, i + 1)
                            pool.wait_ge(ld_got[d], landed(i, DEPTH, d))
                            nc.gpsimd.tensor_tensor(scaled[:, b, :, :], got[:, d, 0:2, :],
                                                    wts[:, d, 0:2].unsqueeze(2).broadcast_to([P, 2, DIM]), ALU.mult)\
                                .then_inc(scaled_done, 1)
                            if past(i, 2):
                                pool.wait_ge(sum_done, 3 * (i - 1))
                            pool.wait_ge(scaled_done, i + 1)
                            nc.gpsimd.tensor_tensor(part[:, b, 0, :], scaled[:, b, 0, :], scaled[:, b, 1, :], ALU.add)\
                                .then_inc(part_done, 1)
                            pool.wait_ge(ld_x1[d], landed(i, DEPTH, d))
                            pool.wait_ge(part_done, 2 * i + 1)
                            nc.gpsimd.tensor_tensor(part[:, b, 1, :], part[:, b, 0, :], xr1[:, d, :], ALU.add)\
                                .then_inc(part_done, 1)
                    run_combine(pool, combine)

                @block.vector
                def _(dve):
                    def expert(s, ph):
                        i, b = s - DOWN, (ph - DOWN) % 2
                        if live(i, N):
                            o = (ph - DOWN) % RING
                            dve.wait_ge(ye_psum, i + 1)
                            if past(i, RING):
                                dve.wait_ge(st_y[o], landed(i, RING, o) - 16)
                            nc.vector.tensor_copy(yo[:, o, :], y_ps[b]).then_inc(yo_done, 1)
                            nc.vector.tensor_copy(name_i[:, o, :], name_f[:, o, :]).then_inc(yo_done, 1)
                        i, b = s - 5, (ph - 5) % 2
                        if live(i, N):
                            dve.wait_ge(ht_psum, i + 1)
                            nc.vector.tensor_copy(ht[:, b, :, :].rearrange("p c t -> p (c t)"), ht_ps)\
                                .then_inc(ht_done, 1)
                        i, b = s - UP, ph % 2
                        if live(i, N):
                            dve.wait_ge(gated_done, i + 1)
                            nc.vector.tensor_tensor(h[:, b, :], gu_ps[b][:, INNER:2 * INNER], gated[:, b, :], ALU.mult)\
                                .then_inc(h_done, 1)
                        i, b = s - 4, ph % RING
                        if live(i, N):
                            dve.wait_ge(xgt_psum, i + 1)
                            nc.vector.tensor_copy(name_f[:, b, :], xg[:, (ph - 4) % AHEAD, DIM:ROW]).then_inc(name_done, 1)
                    run_experts(dve, expert)

                    def combine(s, ph):
                        i, b = s - 2, ph % 2
                        if live(i, TILES):
                            dve.wait_ge(sg_done, i + 1)
                            dve.wait_ge(u_psum, i + 1)
                            nc.vector.tensor_tensor(sh[:, b, :, :].rearrange("p c t -> p (c t)"), u_ps,
                                                    sg[:, b, :, :].rearrange("p c t -> p (c t)"), ALU.mult)\
                                .then_inc(sh_done2, 1)
                        i, b, d = s - 4, ph % 2, ph % DEPTH
                        if live(i, TILES):
                            if past(i, 2):
                                o = (ph - 6) % DEPTH
                                dve.wait_ge(st_out[o], landed(i - 2, DEPTH, o))
                            dve.wait_ge(part_done, 2 * i + 2)
                            dve.wait_ge(sy_psum, i + 1)
                            nc.vector.tensor_tensor(acc[:, b, 0, :], sy_ps[b], part[:, b, 1, :], ALU.add)\
                                .then_inc(sum_done, 1)
                            for k in range(2):
                                dve.wait_ge(sum_done, 3 * i + k + 1)
                                nc.vector.scalar_tensor_tensor(
                                    out=acc[:, b, k + 1, :], in0=got[:, d, 2 + k, :], scalar=wts[:, d, 2 + k:3 + k],
                                    in1=acc[:, b, k, :], op0=ALU.mult, op1=ALU.add).then_inc(sum_done, 1)
                        i, b = s - 1, (ph - 1) % DEPTH
                        if live(i, TILES):
                            nc.vector.tensor_scalar(wts[:, b, :], col(weights, i), 1.0, None, ALU.mult)\
                                .then_inc(wts_done, 1)
                    run_combine(dve, combine)



def kernel(**inputs):
    import concourse.bacc as bacc
    from concourse.bass_utils import run_bass_kernel_spmd

    get = {n.replace("L0_", ""): np.asarray(v) for n, v in inputs.items()}

    def rows(w):
        return w.T.reshape(-1, P, w.shape[0]).transpose(1, 0, 2)

    def feature(v):
        return v.reshape(CH, P).T

    def filler(first, tiles):
        f = np.zeros((tiles, P, ROW), np.float32)
        f[:, :, DIM] = TOKENS * TOPK + first * P + np.arange(tiles * P).reshape(tiles, P)
        return f

    x = get["x"].reshape(TOKENS, DIM)
    ctx = get["ctx_2048"].reshape(TOKENS, DIM)
    wv = get["xattn_w_v_img"].reshape(PAIRS, 2, HD, DIM).transpose(1, 0, 2, 3).reshape(DIM, DIM)
    t = lambda n: get["ffn_" + n].transpose(0, 2, 1)
    index = np.arange(P)
    arrays = {
        "x": x,
        "ctxt": ctx.T.reshape(CH, P, TOKENS).transpose(1, 0, 2),
        "ident": np.eye(P, dtype=np.float32),
        "tri": (index[:, None] < index[None, :]).astype(np.float32),
        "ones": np.ones((P, P), np.float32),
        "headmask": ((index[:, None] // HD) % GH == np.arange(GH)[None, :]).astype(np.float32),
        "eiota": np.tile(np.arange(EXPERTS, dtype=np.float32), (P, 1)),
        "ebase": np.tile(np.arange(EXPERTS, dtype=np.float32) * CAP, (P, 1)),
        "names": np.arange(TOKENS * TOPK, dtype=np.float32).reshape(TILES, P, TOPK).transpose(1, 0, 2),
        "tails": filler(0, EXPERTS).reshape(EXPERTS, 16, P // 16 * ROW),
        "spare": filler(EXPERTS, SPARE).reshape(SPARE * P, ROW),
        "tileno": np.arange(-(-ETILES // P) * P, dtype=np.float32).reshape(-1, P).T,
        "wq": rows(get["xattn_w_q"]),
        "wkv": np.concatenate([rows(get["xattn_w_k_img"]), rows(wv)], axis=2),
        "wo": rows(get["xattn_w_o"]),
        "bq": get["xattn_b_q"][None], "bk": get["xattn_b_k_img"][None], "bo": get["xattn_b_o"][None],
        "bv": feature(get["xattn_b_v_img"]),
        "gq": feature(get["xattn_g_q"]), "gk": feature(get["xattn_g_k_img"]),
        "rgu": np.concatenate([rows(get["ffn_Rg"]), rows(get["ffn_Ru"]), rows(get["ffn_gate_w"])], axis=2),
        "rd": get["ffn_Rd"].T.reshape(2, HALF, RANK).transpose(1, 0, 2),
        "srgu": np.stack([rows(get["ffn_s_Rg"]), rows(get["ffn_s_Ru"])], axis=2),
        "srd": get["ffn_s_Rd"].T,
        "raw": np.concatenate([get["ffn_Ug"], t("Cg"), get["ffn_Uu"], t("Cu"), get["ffn_Ud"], t("Cd")], axis=2),
        "sraw": np.concatenate([get["ffn_s_Ug"], get["ffn_s_Cg"].T, get["ffn_s_Uu"], get["ffn_s_Cu"].T,
                                get["ffn_s_Ud"], get["ffn_s_Cd"].T], axis=1),
    }
    nc = bacc.Bacc("TRN2", target_bir_lowering=False, num_devices=1)
    feed, aps = {}, {}
    for name, v in arrays.items():
        feed["in_" + name] = np.ascontiguousarray(v)
        aps[name] = nc.dram_tensor("in_" + name, v.shape, F32, kind="ExternalInput").ap()
    aps["out"] = nc.dram_tensor("out", [TOKENS, DIM], F32, kind="ExternalOutput").ap()
    build(nc, aps)
    r = run_bass_kernel_spmd(nc, [feed], core_ids=[0])
    return r.results[0]["out"].reshape(BATCH, SEQ, DIM)
```
